# Optimizing a Trainium2 kernel written in Bass

```python
import numpy as np
import jax
import jax.numpy as jnp

def _softmax(x, axis=-1):
    return jax.nn.softmax(x, axis=axis)

def _gelu(x):
    return jax.nn.gelu(x, approximate=True)

def _silu(x):
    return jax.nn.silu(x)

def _sigmoid(x):
    return jax.nn.sigmoid(x)

def _layernorm(x, axis=-1, eps=1e-05):
    m = jnp.mean(x, axis=axis, keepdims=True)
    v = jnp.var(x, axis=axis, keepdims=True)
    return (x - m) / jnp.sqrt(v + eps)

def _scatter_add(tgt, idx, src, axis=0):
    return tgt.at[idx].add(src)

def _segment_sum(src, seg, n):
    return jax.ops.segment_sum(src, seg, n)
kernel_name = 'mk_xattn_ffn_d2_seqx_r8_f45824'

def setup_inputs(seed: int=0):
    np.random.seed(seed)
    _w = jnp.asarray

    def _rec_inputs():
        import jax
        import jax.numpy as jnp
        _rk = jax.random.key(seed)
        x = 7.22e-05 + 1 * jax.random.normal(jax.random.fold_in(_rk, 1), (8, 128, 512), jnp.float32)
        _lenS = 128 - jax.random.randint(jax.random.fold_in(_rk, 7), (8,), 0, max(1, 128 // 4) + 1, jnp.int32)
        _lenS2 = 128 - jax.random.randint(jax.random.fold_in(_rk, 8), (8,), 0, max(1, 128 // 4) + 1, jnp.int32)
        _ctx_4096P = jax.random.normal(jax.random.fold_in(_rk, 11), (8, 16, 512), jnp.float32)
        _ctx_4096c = jax.random.dirichlet(jax.random.fold_in(_rk, 511), 0.3 * jnp.ones((16,), jnp.float32), (8, 128))
        _ctx_4096t = jnp.einsum('bsk,bkd->bsd', _ctx_4096c, _ctx_4096P)
        _ctx_4096t = _ctx_4096t * jax.lax.rsqrt(jnp.mean(jnp.square(_ctx_4096t)) + 1e-12) * 0.953939
        ctx_4096 = 4.13588e-05 + 0.999923 * (_ctx_4096t + 0.3 * jax.random.normal(jax.random.fold_in(_rk, 611), (8, 128, 512), jnp.float32))
        _validS = jnp.arange(128)[None, :] < _lenS[:, None]
        _validS2 = jnp.arange(128)[None, :] < _lenS2[:, None]
        _causal = jnp.tril(jnp.ones((128, 128), dtype=bool))
        mask_BxSxS2_ff1 = jnp.where(jnp.ones((8, 128, 128), dtype=bool), 1.0, 0.0).astype(jnp.float32)
        mask_BxSxS2_bk0 = jnp.logical_not(jnp.broadcast_to(_validS2[:, None, :], (8, 128, 128)))
        return (x, ctx_4096, mask_BxSxS2_ff1, mask_BxSxS2_bk0)
    x, ctx_4096, mask_BxSxS2_ff1, mask_BxSxS2_bk0 = _rec_inputs()

    def _L0_xattn_setup():
        import jax, jax.numpy as jnp
        import numpy as np
        N_Q_HEADS = 32
        N_KV_HEADS = 8
        D_MODEL = 512
        D_K = 128
        D_V = 128
        ROPE_BASE = 10000.0

        def _rope(x):
            d = x.shape[-1]
            s = x.shape[2]
            inv_freq = 1.0 / ROPE_BASE ** (jnp.arange(0, d, 2, dtype=jnp.float32) / d)
            ang = jnp.arange(s, dtype=jnp.float32)[:, None] * inv_freq[None, :]
            cos = jnp.concatenate([jnp.cos(ang), jnp.cos(ang)], axis=-1)[None, None]
            sin = jnp.concatenate([jnp.sin(ang), jnp.sin(ang)], axis=-1)[None, None]
            x1, x2 = (x[..., :d // 2], x[..., d // 2:])
            rot = jnp.concatenate([-x2, x1], axis=-1)
            return x * cos + rot * sin
        key = jax.random.key(seed)
        ks = jax.random.split(key, 8)
        bs, s = (2, 128)
        inp = {'query': jax.random.normal(ks[0], (bs, s, D_MODEL), dtype=jnp.float32), 'key': jax.random.normal(ks[1], (bs, s, D_MODEL), dtype=jnp.float32), 'value': jax.random.normal(ks[2], (bs, s, D_MODEL), dtype=jnp.float32), 'mask': jnp.ones((bs, s, s), dtype=jnp.float32), 'wq': jax.random.normal(ks[3], (D_MODEL, N_Q_HEADS * D_K), dtype=jnp.float32) * 0.02, 'wk': jax.random.normal(ks[4], (D_MODEL, N_KV_HEADS * D_K), dtype=jnp.float32) * 0.02, 'wv': jax.random.normal(ks[5], (D_MODEL, N_KV_HEADS * D_V), dtype=jnp.float32) * 0.02, 'wo': jax.random.normal(ks[6], (N_Q_HEADS * D_V, D_MODEL), dtype=jnp.float32) * 0.02}
        return inp
    _L0_xattn_all = _L0_xattn_setup()
    _L0_xattn_in = {k: v for k, v in _L0_xattn_all.items() if k in ('wq', 'wk', 'wv', 'wo')}
    del _L0_xattn_all

    def _L0_ffn_setup():
        import jax, jax.numpy as jnp
        import numpy as np
        M = 512
        K = 512

        def _make_2to4_mask(key, shape):
            scores = jax.random.normal(key, shape)
            g = scores.reshape(shape[0], shape[1] // 4, 4)
            rank = jnp.argsort(jnp.argsort(-jnp.abs(g), axis=-1), axis=-1)
            return (rank < 2).reshape(shape).astype(jnp.float32)
        key = jax.random.key(seed)
        k_x, k_w12, k_b12, k_w3, k_b3, k_m = jax.random.split(key, 6)
        x = jax.random.normal(k_x, (4, 256, K), dtype=jnp.float32)
        w12_dense = jax.random.normal(k_w12, (2 * M, K), dtype=jnp.float32) * (1.0 / np.sqrt(K))
        mask12 = _make_2to4_mask(k_m, (2 * M, K))
        w12 = w12_dense * mask12
        b12 = jax.random.normal(k_b12, (2 * M,), dtype=jnp.float32) * 0.01
        w3 = jax.random.normal(k_w3, (M, M), dtype=jnp.float32) * (1.0 / np.sqrt(M))
        b3 = jax.random.normal(k_b3, (M,), dtype=jnp.float32) * 0.01
        return {'x': x, 'w12': w12, 'b12': b12, 'w3': w3, 'b3': b3}
    _L0_ffn_all = _L0_ffn_setup()
    _L0_ffn_in = {k: v for k, v in _L0_ffn_all.items() if k in ('w12', 'b12', 'w3', 'b3')}
    del _L0_ffn_all

    def _L1_xattn_setup():
        import jax, jax.numpy as jnp
        import numpy as np
        B, LQ, LK, D, H, DH = (2, 128, 128, 512, 32, 128)
        EPS = 1e-05

        def _rmsnorm(x, weight):
            var = jnp.mean(jnp.square(x), axis=-1, keepdims=True)
            return x * jax.lax.rsqrt(var + EPS) * weight
        key = jax.random.key(seed)
        ks = jax.random.split(key, 8)
        scale = 0.02
        return {'hidden_states': jax.random.normal(ks[0], (B, LQ, D), jnp.float32), 'key_value_states': jax.random.normal(ks[1], (B, LK, D), jnp.float32), 'attention_mask': jax.random.randint(ks[2], (B, LQ, LK), 0, 2) > 0, 'position_bias': jax.random.normal(ks[3], (H, LQ, LK), jnp.float32), 'ln_weight': jnp.ones((D,), jnp.float32), 'w_q': jax.random.normal(ks[4], (H * DH, D), jnp.float32) * scale, 'w_k': jax.random.normal(ks[5], (H * DH, D), jnp.float32) * scale, 'w_v': jax.random.normal(ks[6], (H * DH, D), jnp.float32) * scale, 'w_out': jax.random.normal(ks[7], (D, H * DH), jnp.float32) * scale}
    _L1_xattn_all = _L1_xattn_setup()
    _L1_xattn_in = {k: v for k, v in _L1_xattn_all.items() if k in ('position_bias', 'ln_weight', 'w_q', 'w_k', 'w_v', 'w_out')}
    del _L1_xattn_all

    def _L1_ffn_setup():
        import jax, jax.numpy as jnp
        import numpy as np
        HID, BOT, RDIM, NSLOT, K, VB = (512, 64, 48, 128, 8, 32)
        TAU_LOW, TAU_HIGH, EARLY_EXIT = (0.5, 2.0, 0.05)

        def _uncertainty(h, Wu1, bu1, Wu2, bu2):
            var = jnp.var(h, axis=-1)
            log_var = jnp.log1p(var)
            norm_var = log_var / (jnp.mean(log_var) + 1e-06)
            learned = (jax.nn.gelu(h @ Wu1.T + bu1) @ Wu2.T + bu2)[..., 0]
            return jnp.clip(norm_var * 0.5 + jax.nn.sigmoid(learned) * 2.5, 0.0, 5.0)
        key = jax.random.key(seed)
        ks = jax.random.split(key, 12)
        B, S = (2, 256)
        return {'hidden_states': jax.random.normal(ks[0], (B, S, HID), dtype=jnp.float32), 'Wq': jax.random.normal(ks[1], (BOT, HID), dtype=jnp.float32) / np.sqrt(HID), 'Wr': jax.random.normal(ks[2], (RDIM, BOT), dtype=jnp.float32) / np.sqrt(BOT), 'aux_keys': jax.random.normal(ks[3], (NSLOT, BOT), dtype=jnp.float32) * 0.01, 'aux_values': jax.random.normal(ks[4], (NSLOT, HID), dtype=jnp.float32) * 0.02, 'Wvd': jax.random.normal(ks[5], (VB, HID), dtype=jnp.float32) * 0.1 / np.sqrt(HID), 'Wvu': jax.random.normal(ks[6], (HID, VB), dtype=jnp.float32) * 0.1 / np.sqrt(VB), 'Wu1': jax.random.normal(ks[7], (HID // 4, HID), dtype=jnp.float32) / np.sqrt(HID), 'bu1': jnp.zeros((HID // 4,), dtype=jnp.float32), 'Wu2': jax.random.normal(ks[8], (1, HID // 4), dtype=jnp.float32) * 0.01, 'bu2': jnp.zeros((1,), dtype=jnp.float32), 'gate_w1': jnp.float32(0.5), 'gate_bias': jnp.float32(-1.0), 'log_rel': jnp.zeros((NSLOT,), dtype=jnp.float32)}
    _L1_ffn_all = _L1_ffn_setup()
    _L1_ffn_in = {k: v for k, v in _L1_ffn_all.items() if k in ('Wq', 'Wr', 'aux_keys', 'aux_values', 'Wvd', 'Wvu', 'Wu1', 'bu1', 'Wu2', 'bu2', 'gate_w1', 'gate_bias', 'log_rel')}
    del _L1_ffn_all
    return {'x': x, 'ctx_4096': ctx_4096, 'mask_BxSxS2_ff1': mask_BxSxS2_ff1, 'mask_BxSxS2_bk0': mask_BxSxS2_bk0, 'L0_xattn_wq': _L0_xattn_in['wq'], 'L0_xattn_wk': _L0_xattn_in['wk'], 'L0_xattn_wv': _L0_xattn_in['wv'], 'L0_xattn_wo': _L0_xattn_in['wo'], 'L0_ffn_w12': _L0_ffn_in['w12'], 'L0_ffn_b12': _L0_ffn_in['b12'], 'L0_ffn_w3': _L0_ffn_in['w3'], 'L0_ffn_b3': _L0_ffn_in['b3'], 'L1_xattn_position_bias': _L1_xattn_in['position_bias'], 'L1_xattn_ln_weight': _L1_xattn_in['ln_weight'], 'L1_xattn_w_q': _L1_xattn_in['w_q'], 'L1_xattn_w_k': _L1_xattn_in['w_k'], 'L1_xattn_w_v': _L1_xattn_in['w_v'], 'L1_xattn_w_out': _L1_xattn_in['w_out'], 'L1_ffn_Wq': _L1_ffn_in['Wq'], 'L1_ffn_Wr': _L1_ffn_in['Wr'], 'L1_ffn_aux_keys': _L1_ffn_in['aux_keys'], 'L1_ffn_aux_values': _L1_ffn_in['aux_values'], 'L1_ffn_Wvd': _L1_ffn_in['Wvd'], 'L1_ffn_Wvu': _L1_ffn_in['Wvu'], 'L1_ffn_Wu1': _L1_ffn_in['Wu1'], 'L1_ffn_bu1': _L1_ffn_in['bu1'], 'L1_ffn_Wu2': _L1_ffn_in['Wu2'], 'L1_ffn_bu2': _L1_ffn_in['bu2'], 'L1_ffn_gate_w1': _L1_ffn_in['gate_w1'], 'L1_ffn_gate_bias': _L1_ffn_in['gate_bias'], 'L1_ffn_log_rel': _L1_ffn_in['log_rel']}

def reference(x, ctx_4096, mask_BxSxS2_ff1, mask_BxSxS2_bk0, L0_xattn_wq, L0_xattn_wk, L0_xattn_wv, L0_xattn_wo, L0_ffn_w12, L0_ffn_b12, L0_ffn_w3, L0_ffn_b3, L1_xattn_position_bias, L1_xattn_ln_weight, L1_xattn_w_q, L1_xattn_w_k, L1_xattn_w_v, L1_xattn_w_out, L1_ffn_Wq, L1_ffn_Wr, L1_ffn_aux_keys, L1_ffn_aux_values, L1_ffn_Wvd, L1_ffn_Wvu, L1_ffn_Wu1, L1_ffn_bu1, L1_ffn_Wu2, L1_ffn_bu2, L1_ffn_gate_w1, L1_ffn_gate_bias, L1_ffn_log_rel):
    import jax
    import jax.numpy as jnp

    def _L0_xattn_ref(query, key, value, mask, wq, wk, wv, wo):
        import jax, jax.numpy as jnp
        import numpy as np
        N_Q_HEADS = 32
        N_KV_HEADS = 8
        D_MODEL = 512
        D_K = 128
        D_V = 128
        ROPE_BASE = 10000.0

        def _rope(x):
            d = x.shape[-1]
            s = x.shape[2]
            inv_freq = 1.0 / ROPE_BASE ** (jnp.arange(0, d, 2, dtype=jnp.float32) / d)
            ang = jnp.arange(s, dtype=jnp.float32)[:, None] * inv_freq[None, :]
            cos = jnp.concatenate([jnp.cos(ang), jnp.cos(ang)], axis=-1)[None, None]
            sin = jnp.concatenate([jnp.sin(ang), jnp.sin(ang)], axis=-1)[None, None]
            x1, x2 = (x[..., :d // 2], x[..., d // 2:])
            rot = jnp.concatenate([-x2, x1], axis=-1)
            return x * cos + rot * sin
        bs, s, _ = query.shape
        g = N_Q_HEADS // N_KV_HEADS
        q = (query @ wq).reshape(bs, s, N_Q_HEADS, D_K).transpose(0, 2, 1, 3)
        k = (key @ wk).reshape(bs, s, N_KV_HEADS, D_K).transpose(0, 2, 1, 3)
        v = (value @ wv).reshape(bs, s, N_KV_HEADS, D_V).transpose(0, 2, 1, 3)
        q = _rope(q)
        k = _rope(k)
        scale = jnp.sqrt(jnp.float32(D_K))
        qg = q.reshape(bs, N_KV_HEADS, g, s, D_K)
        scores = jnp.einsum('bhgqd,bhkd->bhgqk', qg, k) / scale
        masked = jnp.where(mask[:, None, None].astype(bool), scores, -1000000000.0)
        w = jax.nn.softmax(masked, axis=-1)
        out = jnp.einsum('bhgqk,bhkd->bhgqd', w, v)
        out = out.reshape(bs, N_Q_HEADS, s, D_V).transpose(0, 2, 1, 3).reshape(bs, s, N_Q_HEADS * D_V)
        return out @ wo

    def _L0_ffn_ref(x, w12, b12, w3, b3):
        import jax, jax.numpy as jnp
        import numpy as np
        M = 512
        K = 512

        def _make_2to4_mask(key, shape):
            scores = jax.random.normal(key, shape)
            g = scores.reshape(shape[0], shape[1] // 4, 4)
            rank = jnp.argsort(jnp.argsort(-jnp.abs(g), axis=-1), axis=-1)
            return (rank < 2).reshape(shape).astype(jnp.float32)
        x12 = jnp.einsum('bsk,mk->bsm', x, w12) + b12
        x1, x2 = jnp.split(x12, 2, axis=-1)
        x4 = jax.nn.silu(x1) * x2
        return jnp.einsum('bsm,nm->bsn', x4, w3) + b3

    def _L1_xattn_ref(hidden_states, key_value_states, attention_mask, position_bias, ln_weight, w_q, w_k, w_v, w_out):
        import jax, jax.numpy as jnp
        import numpy as np
        B, LQ, LK, D, H, DH = (2, 128, 128, 512, 32, 128)
        EPS = 1e-05

        def _rmsnorm(x, weight):
            var = jnp.mean(jnp.square(x), axis=-1, keepdims=True)
            return x * jax.lax.rsqrt(var + EPS) * weight
        x = _rmsnorm(hidden_states, ln_weight)
        b, lq, _ = x.shape
        lk = key_value_states.shape[1]
        h_q = (x @ w_q.T).reshape(b, lq, H, DH)
        h_k = (key_value_states @ w_k.T).reshape(b, lk, H, DH)
        h_v = (key_value_states @ w_v.T).reshape(b, lk, H, DH)
        score = jnp.einsum('bqhd,bkhd->bhqk', h_q, h_k)
        score = score + position_bias[None]
        m = attention_mask[:, None]
        score = jnp.where(m, score, -jnp.inf)
        score = jax.nn.softmax(score, axis=-1)
        score = jnp.where(m, score, 0.0)
        attn = jnp.einsum('bhqk,bkhd->bqhd', score, h_v).reshape(b, lq, H * DH)
        out = attn @ w_out.T
        return hidden_states + out

    def _L1_ffn_ref(hidden_states, Wq, Wr, aux_keys, aux_values, Wvd, Wvu, Wu1, bu1, Wu2, bu2, gate_w1, gate_bias, log_rel):
        import jax, jax.numpy as jnp
        import numpy as np
        HID, BOT, RDIM, NSLOT, K, VB = (512, 64, 48, 128, 8, 32)
        TAU_LOW, TAU_HIGH, EARLY_EXIT = (0.5, 2.0, 0.05)

        def _uncertainty(h, Wu1, bu1, Wu2, bu2):
            var = jnp.var(h, axis=-1)
            log_var = jnp.log1p(var)
            norm_var = log_var / (jnp.mean(log_var) + 1e-06)
            learned = (jax.nn.gelu(h @ Wu1.T + bu1) @ Wu2.T + bu2)[..., 0]
            return jnp.clip(norm_var * 0.5 + jax.nn.sigmoid(learned) * 2.5, 0.0, 5.0)
        query = hidden_states @ Wq.T
        rq = query @ Wr.T
        rk = aux_keys @ Wr.T
        router_scores = jnp.einsum('bsr,nr->bsn', rq, rk) / np.sqrt(RDIM) + log_rel
        top_scores, top_idx = jax.lax.top_k(router_scores, K)
        sel_keys = aux_keys[top_idx]
        attn = jnp.einsum('bsd,bskd->bsk', query, sel_keys) / np.sqrt(BOT) + log_rel[top_idx]
        w = jax.nn.softmax(attn, axis=-1)
        sel_vals = aux_values[top_idx]
        aux_out = jnp.einsum('bsk,bskh->bsh', w, sel_vals)
        aux_out = aux_out @ Wvd.T @ Wvu.T
        u = _uncertainty(hidden_states, Wu1, bu1, Wu2, bu2)
        u_norm = jnp.clip((u - TAU_LOW) / (TAU_HIGH - TAU_LOW), 0.0, 1.0)
        gate = jax.nn.sigmoid(gate_w1 * u_norm + gate_bias)
        gate = jnp.where(gate < EARLY_EXIT, 0.0, gate)
        return hidden_states + gate[..., None] * aux_out
    x = x + _L0_xattn_ref(_layernorm(x, axis=-1), ctx_4096, ctx_4096, mask_BxSxS2_ff1, L0_xattn_wq, L0_xattn_wk, L0_xattn_wv, L0_xattn_wo)
    x = x + _L0_ffn_ref(_layernorm(x, axis=-1), L0_ffn_w12, L0_ffn_b12, L0_ffn_w3, L0_ffn_b3)
    x = x + _L1_xattn_ref(_layernorm(x, axis=-1), ctx_4096, mask_BxSxS2_bk0, L1_xattn_position_bias, L1_xattn_ln_weight, L1_xattn_w_q, L1_xattn_w_k, L1_xattn_w_v, L1_xattn_w_out)
    x = x + _L1_ffn_ref(_layernorm(x, axis=-1), L1_ffn_Wq, L1_ffn_Wr, L1_ffn_aux_keys, L1_ffn_aux_values, L1_ffn_Wvd, L1_ffn_Wvu, L1_ffn_Wu1, L1_ffn_bu1, L1_ffn_Wu2, L1_ffn_bu2, L1_ffn_gate_w1, L1_ffn_gate_bias, L1_ffn_log_rel)
    return x

_drawn_inputs = setup_inputs


def setup_inputs(seed=0):
    import zlib

    import numpy as np

    out = dict(_drawn_inputs(seed))
    spreads = {'L1_xattn_ln_weight': (1.0, 0.2), 'L1_ffn_bu1': (0.0, 2.0), 'L1_ffn_log_rel': (0.0, 2.0)}
    factors = {'L0_xattn_wq': 3.196,
     'L0_xattn_wk': 3.199,
     'L0_ffn_b12': 8.0,
     'L0_ffn_b3': 6.449,
     'L1_ffn_Wq': 64.0,
     'L1_ffn_Wr': 64.0,
     'L1_ffn_aux_keys': 64.0,
     'L1_ffn_aux_values': 64.0,
     'L1_ffn_Wvd': 64.0,
     'L1_ffn_Wvu': 64.0,
     'L1_ffn_Wu1': 64.0,
     'L1_ffn_Wu2': 64.0}
    for name, (base, spread) in spreads.items():
        noise = np.random.default_rng([zlib.crc32(name.encode()), seed]).standard_normal(out[name].shape)
        drawn = base * np.exp(spread * noise) if base else spread * noise
        out[name] = jnp.asarray(drawn.astype(out[name].dtype))
    for name, factor in factors.items():
        out[name] = (out[name] * factor).astype(out[name].dtype)
    return out
```

```python
import concourse.bass as bass
from concourse import mybir
from contextlib import ExitStack

F32 = mybir.dt.float32
F32R = mybir.dt.float32r
ALU = mybir.AluOpType
ACT = mybir.ActivationFunctionType
AX = mybir.AxisListType

B = 8
S = 128
D = 512
C = D // 128
T = B * S
HALF = 512
HD = 128
EPS = 1e-5
EXP_MAX = 80.0
MASKED = -1e30
SLOTS = 128
BOT = 64
RDIM = 48
VB = 32
ITEM = 1024


class Layer:

    def __init__(self, name, iters, heads, shared_kv, ring_base, soft_base, item_base, slots):
        self.name, self.iters, self.heads, self.shared_kv = name, iters, heads, shared_kv
        self.rope = shared_kv
        self.v_cols = HD if shared_kv else heads * HD
        self.v_units = B * self.v_cols // HALF
        self.first = [("K", 0, 0), ("K", 0, 1), ("Q", 0, 0), ("Q", 0, 1)]
        self.units = [e for j in range(heads) for e in self.steps(j, False) if e[0] in "KQVO" or e[0] == "PV"]
        self.ring_base = ring_base
        self.loop_ring = ring_base + len(self.first)
        self.ring_end = self.loop_ring + len(self.units) * iters - len(self.first)
        self.soft_base = soft_base
        self.soft_end = soft_base + 2 * heads * iters
        self.items = ["O0", "KV", "QA", "O1", "QB"] if shared_kv else ["QA", "O0", "KV", "QB"]
        self.early = ["KV", "QA", "QB"]
        self.slots = slots
        self.splits = [("O0", "KV"), ("QA",), (), ("O1", "QB")] if shared_kv else [("QA", "O0"), ("KV", "QB")]
        self.item_base = item_base
        self.loop_item = item_base + len(self.early)
        self.item_end = self.loop_item + len(self.items) * iters - len(self.early)

    def steps(self, j, last):
        k, q = [("K", j + 1, u) for u in range(2)], [("Q", j + 1, u) for u in range(2)]
        v = [("V", 0, n) for n in range(self.v_units)]
        s = [("S", j, 0), ("S", j, 1), ("N", j, 0), ("N", j, 1)]
        t = [("T", j, u) for u in range(2)]
        pv = [("PV", j, u) for u in range(2)]
        o = [("O", (j - 1) // 2 if j % 2 else j // 2 - 1, b) for b in range(B)]
        if j + 1 == self.heads:
            if last:
                return s + t + pv + o
            return s + self.first[:2] + t + self.first[2:3] + pv + self.first[3:] + o
        if self.shared_kv:
            if j == 0:
                return s + q + v[:1] + t + v[1:] + pv
            if j == 1:
                return s + q[:1] + t[:1] + q[1:] + t[1:] + pv
            return s + q + t + o + pv
        return s + v[:2] + t + v[2:] + k + q + pv

    def ring(self, i, unit, back=0):
        k = self.units.index(unit)
        if isinstance(i, int) and i == self.iters - 1:
            k -= len([n for n in self.units[:k] if n in self.first])
        return (i - back) * len(self.units) + (self.loop_ring + k + 1)

    def bank(self, unit, i=0):
        k = self.units.index(unit)
        return (self.loop_ring + k) % 4

    def soft(self, i, j, u):
        return i * (2 * self.heads) + (self.soft_base + 2 * j + u + 1)

    def item(self, i, name, back=0):
        at = self.items.index(name)
        if isinstance(i, int) and i == self.iters - 1:
            at = [n for n in self.items if n[0] == "O"].index(name)
        return (i - back) * len(self.items) + (self.loop_item + at + 1)


CTX_ITEMS = C
L0 = Layer("L0", 8, 4, True, 0, 0, CTX_ITEMS, [0, 1, 2, 0, 1])
FFN_ITEMS = ["F0", "F1", "W3a", "W3b", "F2", "F3"]
FFN_ITEM = L0.item_end
FFN_RING = L0.ring_end
FFN_J = 4
X_UNITS = [(f"X{n}", j, u) for j in range(FFN_J) for u in range(2) for n in (1, 2)]
Y_RING = FFN_RING + len(X_UNITS)
L1 = Layer("L1", 16, 2, False, Y_RING + B, L0.soft_end, FFN_ITEM + len(FFN_ITEMS), [1, 0, 1, 0])
TAIL_ITEM = L1.item_end
TAIL_RING = L1.ring_end
ITEMS = TAIL_ITEM + 1
assert FFN_RING % 4 == 0 and L1.ring_base % 4 == 0 and len(L0.units) % 4 == 0 and len(L1.units) % 4 == 0


def slot_plan():
    slot = [0, 1, 2, 0]
    slot += [1, 2, 1] + L0.slots * (L0.iters - 1) + [0, 1]
    slot += [0, 1] * (len(FFN_ITEMS) // 2)
    slot += [0, 1, 0] + L1.slots * (L1.iters - 1) + [1]
    return slot + [0]


SLOT = slot_plan()


def loads(n):
    return sum(1 for s in SLOT[:n + 1] if s == SLOT[n])


assert len(SLOT) == ITEMS and all(SLOT[n] != SLOT[n - 1] for n in range(1, ITEMS))
ROPE_ITER = len([n for n in L0.units if n[0] in "KQ"])
ROPE_ALL = len([n for n in L0.units if n[0] in "KQ"]) * L0.iters
LN_VE = [2 * B + 1, 2 * (2 * B + 2) - 1, 3 * (2 * B + 2) - 1, 4 * (2 * B + 2) - 1 + 4 + B]
LN_MS = LN_VE[2] + 4
TAIL_STEPS = (["vd", "gmat", "rk", "var1"] + [f"{n}{u}" for u in range(2) for n in ("v", "sq", "poly", "cubic", "inner")]
              + ["query0", "query1"] + [f"{n}{u}" for u in range(2) for n in ("e1", "sig", "gelu")]
              + ["rq0", "rq1", "router0", "router1", "attn0", "attn1", "logsum"]
              + [f"max{b}" for b in range(B)] + [f"replace{b}" for b in range(B)]
              + ["unselected", "selected", "amax", "learned", "mean", "imean", "half_norm", "l1", "l2", "l3", "l4", "l5", "l6", "l7",
                 "gate_in", "g1", "g2", "gate", "isum", "scale", "weights0", "weights", "wT0", "wT"])
TD = {name: n + 1 for n, name in enumerate(TAIL_STEPS)}
OUT_READY = len(TAIL_STEPS)


def xattn_ffn_kernel(nc, x, stream, mask0, mask1, cos_sin, ident_in, position_bias, ln_weight, b12, b3,
                     tail_wvd, tail_auxv, tail_wvu, tail_keys, tail_wr, tail_logrel, tail_cols, tail_scalars, out):
    es = ExitStack()
    with es:
        def sb(name, shape, dt=F32):
            return es.enter_context(nc.sbuf_tensor(name, shape, dt))

        def sem(name):
            return es.enter_context(nc.semaphore(name))

        cT = [sb(f"cT_{p}", [128, C, T], F32R) for p in ("hi", "lo")]
        xT = [sb(f"xT_{p}", [128, C, T], F32R) for p in ("hi", "lo")]
        VO = [sb(f"VO_{p}", [128, 4 * T], F32R) for p in ("hi", "lo")]
        OT = [v[:, 2 * T:4 * T].rearrange("p (h t) -> p h t", h=2) for v in VO]
        GT = [v[:, :].rearrange("p (j t) -> p j t", j=4) for v in VO]
        W = {n: [sb(f"w{n}_{p}", [128, ITEM], F32R) for p in ("hi", "lo")] for n in ("QA", "QB", "KV", "O")}
        QT = [sb(f"QT_{p}", [128, T], F32R) for p in ("hi", "lo")]
        KT = [sb(f"KT_{p}", [128, T], F32R) for p in ("hi", "lo")]
        PT = [sb(f"PT_{p}", [128, 2, HALF], F32R) for p in ("hi", "lo")]
        raw = [sb(f"raw{n}", [128, ITEM]) for n in range(3)]
        xs = sb("xs", [128, B, D])
        neg = sb("neg", [128, B, S])
        probs = sb("probs", [128, 2, HALF])
        rot = sb("rot", [128, 2, HALF])
        prod = sb("prod", [128, 2, HALF])
        table = sb("table", [128, 2, HD])
        comb = rot
        lnw = sb("lnw", [128, D])
        ident = sb("ident", [128, 128])
        nmax = sb("nmax", [128, 2, 4])
        ssum = sb("ssum", [128, 2, 4])
        sinv = sb("sinv", [128, 2, 4])
        rsum = sb("rsum", [128, 2, 4])
        stats = sb("stats", [128, B, 6])
        mv = sb("mv", [128, B, 2])
        ve = sb("ve", [128, B])
        sd = sb("sd", [128, B])
        rstd = sb("rstd", [128, B])
        msq = sb("msq", [128, B])
        rrms = sb("rrms", [128, B])
        bcol = sb("bcol", [128, 2 * FFN_J])
        logrel = sb("logrel", [128, SLOTS])
        tcols = sb("tcols", [128, 2])
        tsc = sb("tsc", [128, 3])
        keys = sb("keys", [BOT, SLOTS])
        wr = sb("wr", [BOT, RDIM])
        rk = sb("rk", [RDIM, SLOTS])
        top = sb("top", [128, B, 8])
        col = sb("col", [128, 12, B])
        auxv = raw[2][:, 0:HALF].rearrange("p (c n) -> p c n", c=C)
        wvd = sb("wvd", [128, C, VB])
        wvu = raw[2][0:VB, HALF:2 * HALF]
        vd = sb("vd", [VB, SLOTS])[:]
        gmat = lnw[:]
        query = neg[:].rearrange("p b s -> p (b s)")
        rq = prod[:].rearrange("p a s -> p (a s)")
        allones = sb("allones", [128, 128])

        ring = [es.enter_context(nc.psum_tensor(f"ring{n}", [128, HALF], F32)) for n in range(4)]
        score = [es.enter_context(nc.psum_tensor(f"score{n}", [128, HALF], F32)) for n in range(2)]
        turned = [es.enter_context(nc.psum_tensor(f"turned{n}", [128, HALF], F32)) for n in range(2)]

        x_in = sem("x_in")
        small_in = sem("small_in")
        raw_in = [sem(f"raw_in{n}") for n in range(3)]
        w_hi = sem("w_hi")
        w_ready = sem("w_ready")
        ring_filled = sem("ring_filled")
        hi_done = sem("hi_done")
        ring_freed = sem("ring_freed")
        rope_sin = sem("rope_sin")
        rope_sum = sem("rope_sum")
        rope_hi = sem("rope_hi")
        rope_ready = sem("rope_ready")
        s_filled = sem("s_filled")
        masked_ready = sem("masked_ready")
        max_ready = sem("max_ready")
        exp_done = sem("exp_done")
        inv_ready = sem("inv_ready")
        rsum_ready = sem("rsum_ready")
        p_ready = sem("p_ready")
        t_filled = sem("t_filled")
        pt_hi = sem("pt_hi")
        pt_ready = sem("pt_ready")
        bias_in = [sem("bias_in_a"), sem("bias_in_b")]
        comb_ready = sem("comb_ready")
        neg_ready = sem("neg_ready")
        mask_in = sem("mask_in")
        ln_step = sem("ln_step")
        ln_sqrt = sem("ln_sqrt")
        y_ready = sem("y_ready")
        y_turned = sem("y_turned")
        y_hi = sem("y_hi")
        y_lo = sem("y_lo")
        x_plus = sem("x_plus")
        row_in = sem("row_in")
        g_step = sem("g_step")
        g_pre = sem("g_pre")
        gate_exp = sem("gate_exp")
        g_hi = sem("g_hi")
        g_lo = sem("g_lo")
        tail_in = sem("tail_in")
        tail_pe = sem("tail_pe")
        tail_act = sem("tail_act")
        tail_dve = sem("tail_dve")
        out_done = sem("out_done")

        def both(pair, fn):
            return [fn(t) for t in pair]

        PARTS = ((0, 0), (0, 1), (1, 0))

        def weights_of(layer, kind, j):
            if layer.shared_kv:
                name, half = ("KV", 0) if kind == "K" else (("QA", "QB")[j // 2], j % 2)
            else:
                name, half = ("QA", "QB")[j], 0 if kind == "Q" else 1
            return [w[:, half * HALF:(half + 1) * HALF].rearrange("p (c d) -> p c d", c=C) for w in W[name]]

        def item_of(layer, kind, j):
            if layer.shared_kv:
                return "KV" if kind == "K" else ("QA", "QB")[j // 2]
            return ("QA", "QB")[j]

        def values(layer, part):
            return VO[part][:, 0:B * layer.v_cols].rearrange("p (b n) -> p b n", b=B)

        def destination(layer, unit):
            kind, j, u = unit
            if kind == "Q":
                return both(QT, lambda t: t[:, u * HALF:(u + 1) * HALF])
            if kind == "K":
                return both(KT, lambda t: t[:, u * HALF:(u + 1) * HALF])
            if kind == "V":
                return both(VO, lambda t: t[:, u * HALF:(u + 1) * HALF])
            return both(OT, lambda t: t[:, j % 2, u * HALF:(u + 1) * HALF])

        def rope_count(layer, i, unit):
            order = [n for n in layer.units if n[0] in "KQ"]
            if i is None:
                return layer.first.index(unit) + 1
            return i * len(order) + (len(layer.first) + order.index(unit) + 1)

        def hi_count(layer, i, unit):
            order = [n for n in layer.units if n[0] != "O"]
            base = 0 if layer is L0 else HI_L1
            if i is None:
                return base + layer.first.index(unit) + 1
            k = order.index(unit)
            if isinstance(i, int) and i == layer.iters - 1:
                k -= len([n for n in order[:k] if n in layer.first])
            return i * len(order) + (base + len(layer.first) + k + 1)

        HI_L1 = len([n for n in L0.units if n[0] != "O"]) * L0.iters

        def ring_count(layer, i, unit):
            return layer.ring_base + layer.first.index(unit) + 1 if i is None else layer.ring(i, unit)

        def ring_bank(layer, i, unit):
            if i is None:
                return (layer.ring_base + layer.first.index(unit)) % 4
            if isinstance(i, int):
                return (layer.ring(i, unit) - 1) % 4
            return layer.bank(unit)

        def is_rope(layer, unit):
            return layer.rope and unit[0] in "KQ"

        DEST = {"KV": "KV", "QA": "QA", "QB": "QB", "O0": "O", "O1": "O"}

        def freed_by(layer, i, name):
            if name == "KV":
                return layer.ring(i, ("V", 0, layer.v_units - 1))
            if layer.shared_kv:
                if name == "QA":
                    return layer.ring(i, ("Q", 1, 1))
                if name == "QB":
                    return layer.ring(i, ("Q", 3, 1))
                if name == "O1":
                    return layer.ring(i, ("O", 0, B - 1))
                return layer.ring(i, ("O", 1, B - 1), back=1) if not isinstance(i, int) else layer.ring(i - 1, ("O", 1, B - 1))
            if name == "QA":
                return i * len(layer.units) + layer.loop_ring
            if name == "QB":
                return layer.ring(i, ("Q", 1, 1))
            return layer.ring(i, ("O", 0, B - 1), back=1) if not isinstance(i, int) else layer.ring(i - 1, ("O", 0, B - 1))

        def item_plan(layer, i, last, name):
            n = layer.item(i, name)
            if isinstance(n, int):
                return n, SLOT[n - 1], 16 * loads(n - 1)
            k = layer.items.index(name)
            slot = layer.slots[k]
            each = layer.slots.count(slot)
            return n, slot, i * (16 * each) + 16 * loads(layer.loop_item + k)

        def loop(eng, layer, body):
            with eng.Fori(0, layer.iters - 1) as i:
                body(i, False)
            body(layer.iters - 1, True)

        block = es.enter_context(nc.Block())

        @block.sync
        def _(sp):
            def load(n):
                if n >= 2:
                    sp.wait_ge(w_ready, n - 1)
                sp.dma_start(raw[SLOT[n]][:], stream[n * 128:(n + 1) * 128, :]).then_inc(raw_in[SLOT[n]], 16)

            def layer_loads(layer):
                for n in range(layer.item_base, layer.loop_item):
                    load(n)

                def body(i, last):
                    for name in layer.items:
                        if last and name[0] != "O":
                            continue
                        if not layer.shared_kv and name == "QA":
                            sp.wait_ge(comb_ready, i * 4 + 2)
                            sp.dma_start(table[:, 0, :], position_bias[bass.ds(i * (2 * S) + 2 * S, S), :]).then_inc(bias_in[0], 16)
                        if not layer.shared_kv and name == "KV":
                            sp.wait_ge(comb_ready, i * 4 + 4)
                            sp.dma_start(table[:, 1, :], position_bias[bass.ds(i * (2 * S) + 3 * S, S), :]).then_inc(bias_in[1], 16)
                        n, slot, _ = item_plan(layer, i, last, name)
                        sp.wait_ge(w_ready, n - 2)
                        sp.dma_start(raw[slot][:], stream[bass.ds(n * 128 - 128, 128), :]).then_inc(raw_in[slot], 16)

                loop(sp, layer, body)

            sp.dma_start(xs[:], x.rearrange("b t d -> t b d")).then_inc(x_in, 16)
            for n in range(CTX_ITEMS):
                load(n)
            layer_loads(L0)
            for n in range(FFN_ITEM, FFN_ITEM + len(FFN_ITEMS)):
                load(n)
            layer_loads(L1)
            load(TAIL_ITEM)
            for b in range(B):
                sp.wait_ge(tail_dve, OUT_READY + b + 1)
                sp.dma_start(out[b], xs[:, b, :]).then_inc(out_done, 16)
            sp.wait_ge(out_done, 16 * B)

        @block.scalar
        def _(act):
            act.dma_start(ident[:], ident_in).then_inc(small_in, 16)
            act.dma_start(table[:], cos_sin).then_inc(small_in, 16)
            act.dma_start(bcol[:], b12).then_inc(small_in, 16)
            act.dma_start(lnw[:], b3.partition_broadcast(128)).then_inc(row_in, 16)
            act.dma_start(neg[:], mask0.rearrange("b q k -> q b k")).then_inc(mask_in, 16)
            act.dma_start(logrel[:], tail_logrel.partition_broadcast(128)).then_inc(tail_in, 16)
            act.dma_start(tcols[:], tail_cols).then_inc(tail_in, 16)
            act.dma_start(tsc[:], tail_scalars.partition_broadcast(128)).then_inc(tail_in, 16)
            act.dma_start(keys[:], tail_keys).then_inc(tail_in, 16)
            act.dma_start(wr[:], tail_wr).then_inc(tail_in, 16)
            act.dma_start(wvd[:], tail_wvd).then_inc(tail_in, 16)

            def high(dest, n, slot, count):
                act.wait_ge(raw_in[slot], count)
                act.activation(dest, raw[slot][:], ACT.Copy).then_inc(w_hi, 1)

            def normed(stage):
                act.wait_ge(ln_step, LN_VE[stage])
                act.activation(sd[:], ve[:], ACT.Sqrt).then_inc(ln_sqrt, 1)
                if stage == 2:
                    act.wait_ge(ln_step, LN_MS)
                    act.activation(msq[:], msq[:], ACT.Sqrt).then_inc(ln_sqrt, 1)
                for b in range(B):
                    act.wait_ge(y_turned, stage * B + b + 1)
                    act.activation(xT[0][:, :, b * S:(b + 1) * S],
                                   turned[b % 2][:].rearrange("p (c t) -> p c t", c=C), ACT.Copy).then_inc(y_hi, 1)

            def evacuate(layer, i, unit):
                act.wait_ge(ring_filled, ring_count(layer, i, unit))
                bank = ring[ring_bank(layer, i, unit)]
                if is_rope(layer, unit):
                    n = rope_count(layer, i, unit)
                    if not isinstance(n, int) or n > 2:
                        act.wait_ge(rope_sum, n - 2)
                    buf = rot[:, unit[2], :]
                    act.activation(buf[0:64, :], bank[64:128, :], ACT.Copy)
                    act.activation(buf[64:128, :], bank[0:64, :], ACT.Copy).then_inc(hi_done, 1)
                else:
                    act.activation(destination(layer, unit)[0], bank[:], ACT.Copy).then_inc(hi_done, 1)

            def exponentials(layer, i, j, u):
                act.wait_ge(max_ready, layer.soft(i, j, u))
                for t in range(4):
                    p = probs[:, u, t * S:(t + 1) * S]
                    ins = act.activation(p, p, ACT.Exp, bias=nmax[:, u, t:t + 1], accum_out=ssum[:, u, t:t + 1])
                ins.then_inc(exp_done, 1)

            def turned_high(layer, i, j, u):
                act.wait_ge(t_filled, layer.soft(i, j, u))
                act.activation(PT[0][:, u, :], turned[u][:], ACT.Copy).then_inc(pt_hi, 1)

            def attention(layer):
                prologue_free = {"KV": 0, "QA": 0, "QB": 0}
                if layer is L1:
                    prologue_free = {"KV": Y_RING + B, "QA": FFN_RING + 12, "QB": FFN_RING + 16}
                for k, name in enumerate(layer.early):
                    n = layer.item_base + k
                    if prologue_free[name]:
                        act.wait_ge(ring_filled, prologue_free[name])
                    high(W[name][0][:], n + 1, SLOT[n], 16 * loads(n))
                for unit in layer.first[:2]:
                    evacuate(layer, None, unit)
                normed(0 if layer is L0 else 2)
                for unit in layer.first[2:]:
                    evacuate(layer, None, unit)

                def item(i, last, name):
                    if last and name[0] != "O":
                        return
                    n, slot, count = item_plan(layer, i, last, name)
                    act.wait_ge(ring_filled, freed_by(layer, i, name))
                    high(W[DEST[name]][0][:], n, slot, count)

                def body(i, last):
                    for j in range(layer.heads):
                        for unit in layer.steps(j, last):
                            if unit[0] == "S":
                                exponentials(layer, i, *unit[1:])
                            elif unit[0] == "T":
                                turned_high(layer, i, *unit[1:])
                            elif unit[0] not in "NO":
                                evacuate(layer, i, unit)
                        for name in layer.splits[j]:
                            item(i, last, name)

                loop(act, layer, body)

            for c in range(CTX_ITEMS):
                high(cT[0][:, c, :], c + 1, SLOT[c], 16 * loads(c))
            attention(L0)

            free = {"F0": L0.ring(7, ("Q", 1, 1)), "F1": L0.ring(7, ("Q", 3, 1)), "W3a": L0.ring(7, ("V", 0, 1)),
                    "W3b": L0.ring(7, ("O", 1, B - 1)), "F2": FFN_RING + 4, "F3": FFN_RING + 8}
            dest = {"F0": "QA", "F1": "QB", "W3a": "KV", "W3b": "O", "F2": "QA", "F3": "QB"}

            def ffn_item(name):
                n = FFN_ITEM + FFN_ITEMS.index(name)
                act.wait_ge(ring_filled, free[name])
                high(W[dest[name]][0][:], n + 1, SLOT[n], 16 * loads(n))

            for name in FFN_ITEMS[:4]:
                ffn_item(name)
            normed(1)
            for j in range(FFN_J):
                for u in range(2):
                    k = 2 * j + u
                    act.wait_ge(g_pre, k + 1)
                    act.activation(rot[:, u, :], rot[:, u, :], ACT.Exp, scale=-1.0).then_inc(gate_exp, 1)
                    act.wait_ge(ring_freed, FFN_RING + 2 * k + 2)
                    act.activation(GT[0][:, j, u * HALF:(u + 1) * HALF], prod[:, u, :], ACT.Copy).then_inc(g_hi, 1)
                if j < 2:
                    ffn_item(("F2", "F3")[j])

            act.wait_ge(x_plus, B)
            act.dma_start(lnw[:], ln_weight.partition_broadcast(128)).then_inc(row_in, 16)
            act.dma_start(raw[2][:, 0:B * S // 4].bitcast(mybir.dt.uint8).rearrange("p (b k) -> p b k", b=B),
                          mask1.rearrange("b q k -> q b k")).then_inc(mask_in, 16)
            act.wait_ge(rope_ready, ROPE_ALL)
            act.dma_start(table[:, 0, :], position_bias[0:S, :]).then_inc(bias_in[0], 16)
            act.dma_start(table[:, 1, :], position_bias[S:2 * S, :]).then_inc(bias_in[1], 16)
            act.wait_ge(neg_ready, 3)
            act.dma_start(auxv, tail_auxv).then_inc(tail_in, 16)
            act.dma_start(wvu, tail_wvu).then_inc(tail_in, 16)
            attention(L1)

            act.wait_ge(ring_filled, TAIL_RING)
            high(W["QA"][0][:], ITEMS, SLOT[TAIL_ITEM], 16 * loads(TAIL_ITEM))
            normed(3)
            act.wait_ge(tail_dve, TD["var1"])
            act.activation(col[:, 1, :], col[:, 0, :], ACT.Ln).then_inc(tail_act, 1)
            for u in range(2):
                act.wait_ge(tail_dve, TD[f"inner{u}"])
                act.activation(rot[:, u, :], rot[:, u, :], ACT.Exp, scale=-2.0 * (2.0 / 3.141592653589793) ** 0.5).then_inc(tail_act, 1)
            act.wait_ge(tail_dve, TD["learned"])
            act.activation(col[:, 4, :], col[:, 3, :], ACT.Exp, scale=-1.0).then_inc(tail_act, 1)
            act.wait_ge(tail_dve, TD["gate_in"])
            act.activation(col[:, 8, :], col[:, 7, :], ACT.Exp, scale=-1.0).then_inc(tail_act, 1)
            act.wait_ge(tail_dve, TD["amax"])
            for b in range(B):
                p = raw[1][:, b * S:(b + 1) * S]
                act.activation(p, p, ACT.Exp, bias=col[:, 10, b:b + 1], accum_out=col[:, 11, b:b + 1]).then_inc(tail_act, 1)

        @block.tensor
        def _(pe):
            def ring_wait(n):
                if isinstance(n, int) and n <= 4:
                    return
                pe.wait_ge(ring_freed, n - 4)

            def project(layer, i, unit):
                kind, j, u = unit
                ring_wait(ring_count(layer, i, unit))
                bank = ring[ring_bank(layer, i, unit)]
                w = weights_of(layer, kind, j)
                src = xT if kind == "Q" else cT
                for c in range(C):
                    for k, (a, b) in enumerate(PARTS):
                        mm = pe.matmul(bank[:], w[a][:, c, :], src[b][:, c, u * HALF:(u + 1) * HALF],
                                       start=(c == 0 and k == 0), stop=(c == C - 1 and k == 2))
                mm.then_inc(ring_filled, 1)

            def project_values(layer, i, unit):
                ring_wait(ring_count(layer, i, unit))
                bank = ring[ring_bank(layer, i, unit)]
                n = layer.v_cols
                per = HALF // n
                if layer.shared_kv:
                    w = both(W["KV"], lambda t: t[:, HALF:2 * HALF].rearrange("p (c d) -> p c d", c=C))
                else:
                    w = both(W["KV"], lambda t: t[:].rearrange("p (c d) -> p c d", c=C))
                for r in range(per):
                    b = unit[2] * per + r
                    for c in range(C):
                        for k, (a, e) in enumerate(PARTS):
                            mm = pe.matmul(bank[:, r * n:(r + 1) * n], cT[a][:, c, b * S:(b + 1) * S], w[e][:, c, :],
                                           start=(c == 0 and k == 0), stop=(c == C - 1 and k == 2))
                mm.then_inc(ring_filled, 1)

            def output(layer, i, unit):
                _, pair, b = unit
                n = ring_count(layer, i, unit)
                ring_wait(n)
                bank = ring[ring_bank(layer, i, unit)]
                for h in range(2):
                    for k, (a, e) in enumerate(PARTS):
                        mm = pe.matmul(bank[:], OT[a][:, h, b * S:(b + 1) * S], W["O"][e][:, h * D:(h + 1) * D],
                                       start=(h == 0 and k == 0), stop=(h == 1 and k == 2))
                mm.then_inc(ring_filled, 1)

            def scores(layer, i, j, u):
                unit = ("Q", j, u)
                if layer.rope and j > 0:
                    pe.wait_ge(rope_ready, rope_count(layer, i, unit))
                elif layer.rope:
                    pe.wait_ge(rope_ready, i * ROPE_ITER + (len(layer.first) - 1 + u))
                elif j > 0:
                    pe.wait_ge(ring_freed, ring_count(layer, i, unit))
                else:
                    pe.wait_ge(ring_freed, i * len(layer.units) + (layer.loop_ring + layer.units.index(unit) + 1 - len(layer.units)))
                for t in range(4):
                    at = (4 * u + t) * S
                    for k, (a, b) in enumerate(PARTS):
                        mm = pe.matmul(score[u][:, t * S:(t + 1) * S], QT[a][:, at:at + S], KT[b][:, at:at + S],
                                       start=(k == 0), stop=(k == 2))
                mm.then_inc(s_filled, 1)

            def turn_probs(layer, i, j, u):
                pe.wait_ge(p_ready, layer.soft(i, j, u))
                for t in range(4):
                    mm = pe.transpose(turned[u][:, t * S:(t + 1) * S], probs[:, u, t * S:(t + 1) * S], ident[:])
                mm.then_inc(t_filled, 1)

            def attend(layer, i, j, u):
                head = 0 if layer.shared_kv else j
                v = [values(layer, p) for p in range(2)]
                unit = ("PV", j, u)
                ring_wait(ring_count(layer, i, unit))
                pe.wait_ge(pt_ready, layer.soft(i, j, u))
                if j == 0:
                    pe.wait_ge(ring_freed, layer.ring(i, ("V", 0, (u + 1) * layer.v_units // 2 - 1)))
                bank = ring[ring_bank(layer, i, unit)]
                for t in range(4):
                    b = 4 * u + t
                    for k, (a, e) in enumerate(PARTS):
                        mm = pe.matmul(bank[:, t * S:(t + 1) * S], v[a][:, b, head * HD:(head + 1) * HD],
                                       PT[e][:, u, t * S:(t + 1) * S], start=(k == 0), stop=(k == 2))
                mm.then_inc(ring_filled, 1)

            def outputs(layer, i, pair, b):
                if b == 0:
                    pe.wait_ge(w_ready, layer.item(i, f"O{pair}"))
                if b % 4 == 0:
                    pe.wait_ge(ring_freed, ring_count(layer, i, ("PV", 2 * pair + 1, b // 4)))
                output(layer, i, ("O", pair, b))

            def turn_rows(stage):
                for b in range(B):
                    pe.wait_ge(y_ready, stage * B + b + 1)
                    if stage * B + b >= 2:
                        pe.wait_ge(y_lo, stage * B + b - 1)
                    src = probs[:, b % 2, :]
                    for c in range(C):
                        mm = pe.transpose(turned[b % 2][:, c * 128:(c + 1) * 128], src[:, c * 128:(c + 1) * 128], ident[:])
                    mm.then_inc(y_turned, 1)

            def attention(layer):
                stage = 0 if layer is L0 else 2
                pe.wait_ge(w_ready, layer.item_base + layer.early.index(item_of(layer, "K", 0)) + 1)
                for unit in layer.first[:2]:
                    project(layer, None, unit)
                turn_rows(stage)
                pe.wait_ge(w_ready, layer.item_base + layer.early.index("QA") + 1)
                pe.wait_ge(y_lo, (stage + 1) * B)
                for unit in layer.first[2:]:
                    project(layer, None, unit)
                if layer is L1:
                    pe.wait_ge(ring_freed, layer.loop_ring)

                def weights_wait(i, unit):
                    kind, j, _ = unit
                    if kind != "V" and j == 0:
                        pe.wait_ge(w_ready, layer.item(i, item_of(layer, kind, 0)))
                    else:
                        name = "KV" if kind == "V" else item_of(layer, kind, j)
                        pe.wait_ge(w_ready, i * len(layer.items) + (layer.loop_item - len(layer.items) + layer.items.index(name) + 1))

                def body(i, last):
                    for j in range(layer.heads):
                        for unit in layer.steps(j, last):
                            if unit[0] in ("K", "Q", "V") and unit[2] == 0:
                                weights_wait(i, unit)
                            if unit[0] == "S":
                                scores(layer, i, *unit[1:])
                            elif unit[0] == "T":
                                turn_probs(layer, i, *unit[1:])
                            elif unit[0] == "PV":
                                attend(layer, i, *unit[1:])
                            elif unit[0] == "O":
                                outputs(layer, i, *unit[1:])
                            elif unit[0] == "V":
                                project_values(layer, i, unit)
                            elif unit[0] in "KQ":
                                project(layer, i, unit)

                loop(pe, layer, body)

            pe.wait_ge(small_in, 48)
            attention(L0)

            turn_rows(1)
            pe.wait_ge(y_lo, 2 * B)
            for j in range(FFN_J):
                pe.wait_ge(w_ready, FFN_ITEM + FFN_ITEMS.index(f"F{j}") + 1)
                for u in range(2):
                    for half in range(2):
                        k = 4 * j + 2 * u + half
                        ring_wait(FFN_RING + k + 1)
                        w = both(W[("QA", "QB")[j % 2]], lambda t: t[:, half * HALF:(half + 1) * HALF].rearrange("p (c d) -> p c d", c=C))
                        for c in range(C):
                            for p, (a, b) in enumerate(PARTS):
                                mm = pe.matmul(ring[(FFN_RING + k) % 4][:], w[a][:, c, :], xT[b][:, c, u * HALF:(u + 1) * HALF],
                                               start=(c == 0 and p == 0), stop=(c == C - 1 and p == 2))
                        mm.then_inc(ring_filled, 1)
            for b in range(B):
                ring_wait(Y_RING + b + 1)
                pe.wait_ge(g_lo, 2 * FFN_J - 1 + b // 4)
                for j in range(FFN_J):
                    w = W[("KV", "O")[j // 2]]
                    for p, (a, e) in enumerate(PARTS):
                        mm = pe.matmul(ring[(Y_RING + b) % 4][:], GT[a][:, j, b * S:(b + 1) * S],
                                       w[e][:, (j % 2) * D:(j % 2 + 1) * D], start=(j == 0 and p == 0), stop=(j == FFN_J - 1 and p == 2))
                mm.then_inc(ring_filled, 1)

            attention(L1)

            pe.wait_ge(tail_in, 16 * 8)
            for c in range(C):
                mm = pe.matmul(score[0][0:VB, 0:SLOTS], wvd[:, c, :], auxv[:, c, :], start=(c == 0), stop=(c == C - 1))
            mm.then_inc(tail_pe, 1)
            pe.wait_ge(tail_dve, TD["vd"])
            pe.matmul(score[1][:], vd, wvu, start=True, stop=True).then_inc(tail_pe, 1)
            pe.matmul(ring[0][0:RDIM, 0:SLOTS], wr[:], keys[:], start=True, stop=True).then_inc(tail_pe, 1)
            turn_rows(3)
            pe.wait_ge(w_ready, ITEMS)
            pe.wait_ge(y_lo, 4 * B)
            wq = both(W["QA"], lambda t: t[:, 0:C * BOT].rearrange("p (c d) -> p c d", c=C))
            wu = both(W["QA"], lambda t: t[:, C * BOT:C * (BOT + 128)].rearrange("p (c d) -> p c d", c=C))
            for w, m, banks in ((wu, 128, (1, 2)), (wq, BOT, (3, 0))):
                for u in range(2):
                    if banks[u] == 0:
                        pe.wait_ge(tail_dve, TD["rk"])
                    for c in range(C):
                        for p, (a, b) in enumerate(PARTS):
                            mm = pe.matmul(ring[banks[u]][0:m, :], w[a][:, c, :], xT[b][:, c, u * HALF:(u + 1) * HALF],
                                           start=(c == 0 and p == 0), stop=(c == C - 1 and p == 2))
                    mm.then_inc(tail_pe, 1)
            for u in range(2):
                pe.wait_ge(tail_dve, TD[f"query{u}"])
                pe.matmul(turned[u][0:RDIM, :], wr[:], query[0:BOT, u * HALF:(u + 1) * HALF], start=True, stop=True).then_inc(tail_pe, 1)
            for u in range(2):
                pe.wait_ge(tail_dve, TD[f"rq{u}"])
                for t in range(4):
                    at = (4 * u + t) * S
                    mm = pe.matmul(score[u][:, t * S:(t + 1) * S], rq[0:RDIM, at:at + S], rk[:], start=True, stop=True)
                mm.then_inc(tail_pe, 1)
            for u in range(2):
                for t in range(4):
                    at = (4 * u + t) * S
                    mm = pe.matmul(ring[(3, 0)[u]][:, t * S:(t + 1) * S], query[0:BOT, at:at + S], keys[:], start=True, stop=True)
                mm.then_inc(tail_pe, 1)
            pe.wait_ge(tail_dve, TD["logsum"])
            pe.matmul(turned[0][:, 0:1], allones[:], col[:, 2, 0:1], start=True, stop=True).then_inc(tail_pe, 1)
            for u in range(2):
                pe.wait_ge(tail_dve, TD[f"gelu{u}"])
                for t in range(4):
                    mm = pe.matmul(turned[1][:, 4 * u + t:4 * u + t + 1], rot[:, u, t * S:(t + 1) * S], tcols[:, 1:2], start=True, stop=True)
            mm.then_inc(tail_pe, 1)
            for u in range(2):
                pe.wait_ge(tail_dve, TD["weights"] - 1 + u)
                for t in range(4):
                    at = (4 * u + t) * S
                    mm = pe.transpose(score[u][:, t * S:(t + 1) * S], raw[1][:, at:at + S], ident[:])
                mm.then_inc(tail_pe, 1)
            for b in range(B):
                pe.wait_ge(tail_dve, TD["wT"] - 1 + b // 4)
                if b >= 4:
                    pe.wait_ge(tail_dve, OUT_READY + b - 3)
                pe.matmul(ring[b % 4][:], rot[:, b // 4, (b % 4) * S:(b % 4 + 1) * S], gmat, start=True, stop=True).then_inc(tail_pe, 1)

        @block.vector
        def _(dve):
            dve.wait_ge(mask_in, 16)
            dve.tensor_scalar(neg[:], neg[:], 0.0, MASKED, ALU.is_equal, ALU.mult).then_inc(neg_ready, 1)
            dve.wait_ge(small_in, 48)
            dve.memset(allones[:], 1.0).then_inc(neg_ready, 1)

            class Steps:
                n = 0

            def step():
                Steps.n += 1
                return Steps.n

            def row_stats():
                for b in range(B):
                    dve.bn_stats(stats[:, b, :], xs[:, b, :]).then_inc(ln_step, 1)
                    step()
                for b in range(B):
                    if b == 0:
                        dve.wait_ge(ln_step, Steps.n)
                    dve.bn_aggr(mv[:, b, :], stats[:, b, :]).then_inc(ln_step, 1)
                    step()

            def lower(stage, b):
                dve.wait_ge(y_hi, stage * B + b + 1)
                dst = slice(b * S, (b + 1) * S)
                dve.tensor_tensor(xT[1][:, :, dst], turned[b % 2][:].rearrange("p (c t) -> p c t", c=C),
                                  xT[0][:, :, dst].bitcast(F32), ALU.subtract).then_inc(y_lo, 1)

            def normed(stage):
                row_stats()
                dve.wait_ge(ln_step, Steps.n)
                dve.tensor_scalar(ve[:], mv[:, :, 1], EPS, None, ALU.add).then_inc(ln_step, 1)
                assert step() == LN_VE[stage], (stage, Steps.n)
                dve.wait_ge(ln_sqrt, stage + 1 + (stage == 3))
                dve.reciprocal(rstd[:], sd[:]).then_inc(ln_step, 1)
                dve.wait_ge(ln_step, step())
                if stage >= 2:
                    dve.tensor_tensor(msq[:], mv[:, :, 1], rstd[:], ALU.mult).then_inc(ln_step, 1)
                    dve.wait_ge(ln_step, step())
                    dve.tensor_tensor(msq[:], msq[:], rstd[:], ALU.mult).then_inc(ln_step, 1)
                    dve.wait_ge(ln_step, step())
                if stage == 2:
                    dve.tensor_scalar(msq[:], msq[:], EPS, None, ALU.add).then_inc(ln_step, 1)
                    assert step() == LN_MS, Steps.n
                    dve.wait_ge(ln_sqrt, stage + 2)
                    dve.reciprocal(rrms[:], msq[:]).then_inc(ln_step, 1)
                    dve.wait_ge(ln_step, step())
                    dve.wait_ge(row_in, 32)
                for b in range(B):
                    if b >= 2:
                        dve.wait_ge(y_turned, stage * B + b - 1)
                    y = probs[:, b % 2, :]
                    if stage == 3 and b >= 2:
                        dve.wait_ge(x_plus, 2 * B + b - 1)
                    if stage != 2:
                        dve.tensor_scalar(y, xs[:, b, :], mv[:, b, 0:1], rstd[:, b:b + 1], ALU.subtract, ALU.mult).then_inc(y_ready, 1)
                    else:
                        if b >= 2:
                            dve.wait_ge(x_plus, B + b - 1)
                        y2 = prod[:, b % 2, :]
                        dve.tensor_scalar(y2, xs[:, b, :], mv[:, b, 0:1], rstd[:, b:b + 1], ALU.subtract, ALU.mult).then_inc(ln_step, 1)
                        dve.wait_ge(ln_step, step())
                        dve.scalar_tensor_tensor(y, y2, rrms[:, b:b + 1], lnw[:], ALU.mult, ALU.mult).then_inc(y_ready, 1)
                    if b >= 1:
                        lower(stage, b - 1)
                lower(stage, B - 1)

            def lows(layer, i, unit):
                hi, lo = destination(layer, unit)
                dve.wait_ge(hi_done, hi_count(layer, i, unit))
                dve.tensor_tensor(lo, ring[ring_bank(layer, i, unit)][:], hi.bitcast(F32), ALU.subtract).then_inc(ring_freed, 1)

            def rope_cos(layer, i, unit):
                n = rope_count(layer, i, unit)
                dve.wait_ge(hi_done, hi_count(layer, i, unit))
                if not isinstance(n, int) or n > 2:
                    dve.wait_ge(rope_ready, n - 2)
                dve.tensor_tensor(prod[:, unit[2], :].rearrange("p (b t) -> p b t", b=4),
                                  ring[ring_bank(layer, i, unit)][:].rearrange("p (b t) -> p b t", b=4),
                                  table[:, 0:1, :].to_broadcast([128, 4, HD]), ALU.mult).then_inc(ring_freed, 1)

            def rope_add(layer, i, unit):
                n = rope_count(layer, i, unit)
                dve.wait_ge(rope_sin, n)
                dve.wait_ge(ring_freed, ring_count(layer, i, unit))
                p = prod[:, unit[2], :]
                dve.tensor_tensor(p, p, rot[:, unit[2], :], ALU.add).then_inc(rope_sum, 1)
                dve.wait_ge(rope_sum, n)
                dve.tensor_copy(destination(layer, unit)[0], p).then_inc(rope_hi, 1)

            def evacuate(layer, i, units):
                for k, unit in enumerate(units):
                    if not is_rope(layer, unit):
                        lows(layer, i, unit)
                        continue
                    rope_cos(layer, i, unit)
                    if k >= 1:
                        rope_add(layer, i, units[k - 1])
                if is_rope(layer, units[-1]):
                    rope_add(layer, i, units[-1])

            def mask_and_max(layer, i, j, u):
                dve.wait_ge(s_filled, layer.soft(i, j, u))
                if layer is L1:
                    dve.wait_ge(comb_ready, i * 4 + 2 * j + u + 1)
                p4 = probs[:, u, :].rearrange("p (b k) -> p b k", b=4)
                s4 = score[u][:].rearrange("p (b k) -> p b k", b=4)
                add = neg[:, 4 * u:4 * u + 4, :] if layer is L0 else comb[:, u, :].rearrange("p (b k) -> p b k", b=4)
                dve.tensor_tensor(p4, s4, add, ALU.add).then_inc(masked_ready, 1)
                dve.wait_ge(masked_ready, layer.soft(i, j, u))
                dve.tensor_reduce(nmax[:, u, :], p4, AX.X, ALU.max, negate=True).then_inc(max_ready, 1)

            def inverse_sum(layer, i, j, u):
                dve.wait_ge(exp_done, layer.soft(i, j, u))
                if layer is L0:
                    dve.reciprocal(rsum[:, u, :], ssum[:, u, :]).then_inc(rsum_ready, 1)
                else:
                    dve.reciprocal(sinv[:, u, :], ssum[:, u, :]).then_inc(inv_ready, 1)
                    dve.wait_ge(inv_ready, i * 4 + 2 * j + u + 1)
                    dve.scalar_tensor_tensor(rsum[:, u, :], nmax[:, u, :], -0.5 * MASKED, sinv[:, u, :],
                                             ALU.is_lt, ALU.mult).then_inc(rsum_ready, 1)

            def add_output(layer, i, unit):
                b = unit[2]
                dve.wait_ge(ring_filled, ring_count(layer, i, unit))
                dve.tensor_tensor(xs[:, b, :], ring[ring_bank(layer, i, unit)][:], xs[:, b, :], ALU.add).then_inc(ring_freed, 1)

            def turned_low(layer, i, j, u):
                dve.wait_ge(pt_hi, layer.soft(i, j, u))
                dve.tensor_tensor(PT[1][:, u, :], turned[u][:], PT[0][:, u, :].bitcast(F32), ALU.subtract).then_inc(pt_ready, 1)

            def attention(layer):
                evacuate(layer, None, layer.first[:2])
                if layer is L0:
                    normed(0)
                else:
                    normed(2)
                evacuate(layer, None, layer.first[2:])
                if layer is L1:
                    dve.wait_ge(x_plus, 2 * B)

                def body(i, last):
                    for j in range(layer.heads):
                        steps = layer.steps(j, last)
                        for k, unit in enumerate(steps):
                            if unit[0] == "S":
                                mask_and_max(layer, i, *unit[1:])
                            elif unit[0] == "N":
                                inverse_sum(layer, i, *unit[1:])
                            elif unit[0] == "T":
                                turned_low(layer, i, *unit[1:])
                            elif unit[0] == "O":
                                add_output(layer, i, unit)
                            elif not is_rope(layer, unit):
                                lows(layer, i, unit)
                            elif not is_rope(layer, steps[k - 1]):
                                run = [unit]
                                while is_rope(layer, steps[k + len(run)]):
                                    run.append(steps[k + len(run)])
                                evacuate(layer, i, run)

                loop(dve, layer, body)

            dve.wait_ge(neg_ready, 2)
            dve.wait_ge(x_in, 16)
            attention(L0)

            dve.wait_ge(ring_freed, L0.ring_end)
            normed(1)

            def bounded(k):
                dve.wait_ge(ring_filled, FFN_RING + 2 * k + 1)
                dve.tensor_scalar(rot[:, k % 2, :], ring[(FFN_RING + 2 * k) % 4][:], bcol[:, k // 2:k // 2 + 1], -EXP_MAX,
                                  ALU.add, ALU.max).then_inc(g_pre, 1)

            bounded(0)
            for j in range(FFN_J):
                for u in range(2):
                    k = 2 * j + u
                    r = rot[:, u, :]
                    if k + 1 < 2 * FFN_J:
                        bounded(k + 1)
                    dve.wait_ge(gate_exp, k + 1)
                    dve.tensor_scalar(r, r, 1.0, None, ALU.add).then_inc(g_step, 1)
                    dve.wait_ge(g_step, 2 * k + 1)
                    dve.reciprocal(r, r).then_inc(g_step, 1)
                    dve.wait_ge(g_step, 2 * k + 2)
                    dve.scalar_tensor_tensor(r, ring[(FFN_RING + 2 * k) % 4][:], bcol[:, j:j + 1], r, ALU.add, ALU.mult).then_inc(ring_freed, 1)
                    dve.wait_ge(ring_freed, FFN_RING + 2 * k + 1)
                    dve.wait_ge(ring_filled, FFN_RING + 2 * k + 2)
                    if k >= 2:
                        dve.wait_ge(g_lo, k - 1)
                    dve.scalar_tensor_tensor(prod[:, u, :], ring[(FFN_RING + 2 * k + 1) % 4][:], bcol[:, FFN_J + j:FFN_J + j + 1], r,
                                             ALU.add, ALU.mult).then_inc(ring_freed, 1)
                    dve.wait_ge(g_hi, k + 1)
                    cols = slice(u * HALF, (u + 1) * HALF)
                    dve.tensor_tensor(GT[1][:, j, cols], prod[:, u, :], GT[0][:, j, cols].bitcast(F32), ALU.subtract).then_inc(g_lo, 1)
            dve.wait_ge(x_plus, B)
            for b in range(B):
                dve.wait_ge(ring_filled, Y_RING + b + 1)
                dve.tensor_tensor(xs[:, b, :], ring[(Y_RING + b) % 4][:], xs[:, b, :], ALU.add).then_inc(ring_freed, 1)
            dve.wait_ge(mask_in, 32)
            dve.tensor_scalar(neg[:], raw[2][:, 0:B * S // 4].bitcast(mybir.dt.uint8).rearrange("p (b k) -> p b k", b=B),
                              0.0, MASKED, ALU.is_equal, ALU.mult).then_inc(neg_ready, 1)
            dve.wait_ge(ring_freed, Y_RING + B)
            attention(L1)

            names = []

            def mark(name):
                names.append(name)
                assert name not in TD or TD[name] == len(names), (name, len(names))
                return len(names)

            dve.wait_ge(ring_freed, TAIL_RING)
            dve.wait_ge(tail_pe, 1)
            dve.tensor_copy(vd, score[0][0:VB, 0:SLOTS]).then_inc(tail_dve, 1)
            mark("vd")
            dve.wait_ge(tail_pe, 2)
            dve.tensor_copy(gmat, score[1][:]).then_inc(tail_dve, 1)
            mark("gmat")
            dve.wait_ge(tail_pe, 3)
            dve.tensor_copy(rk[:], ring[0][0:RDIM, 0:SLOTS]).then_inc(tail_dve, 1)
            mark("rk")
            normed(3)
            dve.tensor_scalar(col[:, 0, :], msq[:], 1.0, None, ALU.add).then_inc(tail_dve, 1)
            mark("var1")
            for u in range(2):
                dve.wait_ge(tail_pe, 4 + u)
                v, w = raw[0][:, u * HALF:(u + 1) * HALF], rot[:, u, :]
                dve.tensor_scalar(v, ring[1 + u][:], tcols[:, 0:1], None, ALU.add).then_inc(tail_dve, 1)
                dve.wait_ge(tail_dve, mark(f"v{u}"))
                dve.tensor_tensor(w, v, v, ALU.mult).then_inc(tail_dve, 1)
                dve.wait_ge(tail_dve, mark(f"sq{u}"))
                dve.tensor_scalar(w, w, 0.044715, 1.0, ALU.mult, ALU.add).then_inc(tail_dve, 1)
                dve.wait_ge(tail_dve, mark(f"poly{u}"))
                dve.tensor_tensor(w, w, v, ALU.mult).then_inc(tail_dve, 1)
                dve.wait_ge(tail_dve, mark(f"cubic{u}"))
                dve.tensor_scalar(w, w, -0.5 * EXP_MAX, None, ALU.max).then_inc(tail_dve, 1)
                mark(f"inner{u}")
            for u in range(2):
                dve.wait_ge(tail_pe, 6 + u)
                dve.tensor_copy(query[0:BOT, u * HALF:(u + 1) * HALF], ring[(3, 0)[u]][0:BOT, :]).then_inc(tail_dve, 1)
                mark(f"query{u}")
            for u in range(2):
                v, w = raw[0][:, u * HALF:(u + 1) * HALF], rot[:, u, :]
                dve.wait_ge(tail_act, 2 + u)
                dve.tensor_scalar(w, w, 1.0, None, ALU.add).then_inc(tail_dve, 1)
                dve.wait_ge(tail_dve, mark(f"e1{u}"))
                dve.reciprocal(w, w).then_inc(tail_dve, 1)
                dve.wait_ge(tail_dve, mark(f"sig{u}"))
                dve.tensor_tensor(w, w, v, ALU.mult).then_inc(tail_dve, 1)
                mark(f"gelu{u}")
            for u in range(2):
                dve.wait_ge(tail_pe, 8 + u)
                dve.tensor_copy(rq[0:RDIM, u * HALF:(u + 1) * HALF], turned[u][0:RDIM, :]).then_inc(tail_dve, 1)
                mark(f"rq{u}")
            lr = logrel[:, :].rearrange("p (a n) -> p a n", a=1).to_broadcast([128, 4, SLOTS])
            R3 = raw[0][:].rearrange("p (b n) -> p b n", b=B)
            A3 = raw[1][:].rearrange("p (b n) -> p b n", b=B)
            X3 = raw[2][:].rearrange("p (b n) -> p b n", b=B)
            dve.wait_ge(tail_dve, len(names))
            for u in range(2):
                dve.wait_ge(tail_pe, 10 + u)
                dve.scalar_tensor_tensor(R3[:, 4 * u:4 * u + 4, :], score[u][:].rearrange("p (b n) -> p b n", b=4),
                                         float(RDIM) ** -0.5, lr, ALU.mult, ALU.add).then_inc(tail_dve, 1)
                mark(f"router{u}")
            for u in range(2):
                dve.wait_ge(tail_pe, 12 + u)
                dve.scalar_tensor_tensor(A3[:, 4 * u:4 * u + 4, :], ring[(3, 0)[u]][:].rearrange("p (b n) -> p b n", b=4),
                                         float(BOT) ** -0.5, lr, ALU.mult, ALU.add).then_inc(tail_dve, 1)
                mark(f"attn{u}")
            dve.wait_ge(tail_act, 1)
            dve.tensor_reduce(col[:, 2, 0:1], col[:, 1, :], AX.X, ALU.add).then_inc(tail_dve, 1)
            dve.wait_ge(tail_dve, mark("logsum"))
            for b in range(B):
                dve.max(top[:, b, :], R3[:, b, :]).then_inc(tail_dve, 1)
                mark(f"max{b}")
            dve.wait_ge(tail_dve, len(names))
            for b in range(B):
                dve.match_replace(X3[:, b, :], top[:, b, :], R3[:, b, :], -3e38).then_inc(tail_dve, 1)
                mark(f"replace{b}")
            dve.wait_ge(tail_dve, len(names))
            dve.tensor_tensor(R3, X3, R3, ALU.is_equal).then_inc(tail_dve, 1)
            dve.wait_ge(tail_dve, mark("unselected"))
            dve.scalar_tensor_tensor(raw[1][:], raw[0][:], MASKED, raw[1][:], ALU.mult, ALU.add).then_inc(tail_dve, 1)
            dve.wait_ge(tail_dve, mark("selected"))
            dve.tensor_reduce(col[:, 10, :], A3, AX.X, ALU.max, negate=True).then_inc(tail_dve, 1)
            mark("amax")
            dve.wait_ge(tail_pe, 15)
            dve.tensor_scalar(col[:, 3, :], turned[1][:, 0:B], tsc[:, 2:3], -EXP_MAX, ALU.add, ALU.max).then_inc(tail_dve, 1)
            mark("learned")
            dve.tensor_scalar(col[:, 2, 1:2], turned[0][:, 0:1], 1.0 / T, 1e-6, ALU.mult, ALU.add).then_inc(tail_dve, 1)
            dve.wait_ge(tail_dve, mark("mean"))
            dve.reciprocal(col[:, 2, 2:3], col[:, 2, 1:2]).then_inc(tail_dve, 1)
            dve.wait_ge(tail_dve, mark("imean"))
            dve.tensor_scalar(col[:, 5, :], col[:, 1, :], col[:, 2, 2:3], 0.5, ALU.mult, ALU.mult).then_inc(tail_dve, 1)
            mark("half_norm")
            dve.wait_ge(tail_act, 4)
            dve.tensor_scalar(col[:, 4, :], col[:, 4, :], 1.0, None, ALU.add).then_inc(tail_dve, 1)
            dve.wait_ge(tail_dve, mark("l1"))
            dve.reciprocal(col[:, 4, :], col[:, 4, :]).then_inc(tail_dve, 1)
            dve.wait_ge(tail_dve, mark("l2"))
            dve.scalar_tensor_tensor(col[:, 6, :], col[:, 4, :], 2.5, col[:, 5, :], ALU.mult, ALU.add).then_inc(tail_dve, 1)
            dve.wait_ge(tail_dve, mark("l3"))
            dve.tensor_scalar(col[:, 6, :], col[:, 6, :], 0.0, 5.0, ALU.max, ALU.min).then_inc(tail_dve, 1)
            dve.wait_ge(tail_dve, mark("l4"))
            dve.tensor_scalar(col[:, 6, :], col[:, 6, :], 0.5, 1.0 / 1.5, ALU.subtract, ALU.mult).then_inc(tail_dve, 1)
            dve.wait_ge(tail_dve, mark("l5"))
            dve.tensor_scalar(col[:, 6, :], col[:, 6, :], 0.0, 1.0, ALU.max, ALU.min).then_inc(tail_dve, 1)
            dve.wait_ge(tail_dve, mark("l6"))
            dve.tensor_scalar(col[:, 7, :], col[:, 6, :], tsc[:, 0:1], tsc[:, 1:2], ALU.mult, ALU.add).then_inc(tail_dve, 1)
            dve.wait_ge(tail_dve, mark("l7"))
            dve.tensor_scalar(col[:, 7, :], col[:, 7, :], -EXP_MAX, None, ALU.max).then_inc(tail_dve, 1)
            mark("gate_in")
            dve.wait_ge(tail_act, 5)
            dve.tensor_scalar(col[:, 8, :], col[:, 8, :], 1.0, None, ALU.add).then_inc(tail_dve, 1)
            dve.wait_ge(tail_dve, mark("g1"))
            dve.reciprocal(col[:, 8, :], col[:, 8, :]).then_inc(tail_dve, 1)
            dve.wait_ge(tail_dve, mark("g2"))
            dve.scalar_tensor_tensor(col[:, 9, :], col[:, 8, :], 0.05, col[:, 8, :], ALU.is_ge, ALU.mult).then_inc(tail_dve, 1)
            dve.wait_ge(tail_act, 5 + B)
            dve.reciprocal(col[:, 0, :], col[:, 11, :]).then_inc(tail_dve, 1)
            mark("gate")
            dve.wait_ge(tail_dve, mark("isum"))
            dve.tensor_tensor(col[:, 0, :], col[:, 0, :], col[:, 9, :], ALU.mult).then_inc(tail_dve, 1)
            dve.wait_ge(tail_dve, mark("scale"))
            for u in range(2):
                dve.tensor_tensor(A3[:, 4 * u:4 * u + 4, :], A3[:, 4 * u:4 * u + 4, :],
                                  col[:, 0, 4 * u:4 * u + 4].rearrange("p (b a) -> p b a", a=1).to_broadcast([128, 4, SLOTS]),
                                  ALU.mult).then_inc(tail_dve, 1)
                mark(("weights0", "weights")[u])
            for u in range(2):
                dve.wait_ge(tail_pe, 16 + u)
                dve.tensor_copy(rot[:, u, :], score[u][:]).then_inc(tail_dve, 1)
                mark(("wT0", "wT")[u])
            assert len(names) == OUT_READY, len(names)
            for b in range(B):
                dve.wait_ge(tail_pe, 18 + b)
                if b == 0:
                    dve.wait_ge(x_plus, 3 * B)
                dve.tensor_tensor(xs[:, b, :], ring[b % 4][:], xs[:, b, :], ALU.add).then_inc(tail_dve, 1)

        @block.gpsimd
        def _(pool):
            def low(dest_hi, dest_lo, n, slot):
                pool.wait_ge(w_hi, n)
                pool.tensor_tensor(dest_lo, raw[slot][:], dest_hi.bitcast(F32), ALU.subtract).then_inc(w_ready, 1)

            def rope_sin_of(layer, i, unit):
                pool.wait_ge(hi_done, hi_count(layer, i, unit))
                r = rot[:, unit[2], :].rearrange("p (b t) -> p b t", b=4)
                pool.tensor_tensor(r, r, table[:, 1:2, :].to_broadcast([128, 4, HD]), ALU.mult).then_inc(rope_sin, 1)

            def rope_low(layer, i, unit):
                hi, lo = destination(layer, unit)
                pool.wait_ge(rope_hi, rope_count(layer, i, unit))
                pool.tensor_tensor(lo, prod[:, unit[2], :], hi.bitcast(F32), ALU.subtract).then_inc(rope_ready, 1)

            def normalise(layer, i, j, u):
                p = probs[:, u, :].rearrange("p (b k) -> p b k", b=4)
                pool.wait_ge(rsum_ready, layer.soft(i, j, u))
                pool.tensor_tensor(p, p, rsum[:, u, :].rearrange("p (b a) -> p b a", a=1).to_broadcast([128, 4, S]),
                                   ALU.mult).then_inc(p_ready, 1)

            def combine(i, j, u, count):
                h = table[:, j:j + 1, :].to_broadcast([128, 4, S])
                if u == 0:
                    pool.wait_ge(bias_in[j], i * 16 + 16)
                if count is not None:
                    pool.wait_ge(masked_ready, count)
                pool.tensor_tensor(comb[:, u, :].rearrange("p (b k) -> p b k", b=4), neg[:, 4 * u:4 * u + 4, :], h,
                                   ALU.add).then_inc(comb_ready, 1)

            def attention(layer):
                for k, name in enumerate(layer.early):
                    n = layer.item_base + k
                    low(W[name][0][:], W[name][1][:], n + 1, SLOT[n])
                if layer is L0:
                    units = layer.first
                    for pair in (units[:2], units[2:]):
                        for k in range(3):
                            if k < 2:
                                rope_sin_of(layer, None, pair[k])
                            if k >= 1:
                                rope_low(layer, None, pair[k - 1])
                else:
                    for b in range(B):
                        pool.wait_ge(y_ready, 2 * B + b + 1)
                        pool.tensor_tensor(xs[:, b, :], xs[:, b, :], prod[:, b % 2, :], ALU.add).then_inc(x_plus, 1)
                    pool.wait_ge(neg_ready, 3)
                    combine(0, 0, 0, None)
                    combine(0, 0, 1, None)

                def item(i, last, name):
                    if last and name[0] != "O":
                        return
                    n, slot, _ = item_plan(layer, i, last, name)
                    d = W[DEST[name]]
                    low(d[0][:], d[1][:], n, slot)

                def rope(i, units):
                    for k in range(len(units) + 1):
                        if k < len(units):
                            rope_sin_of(layer, i, units[k])
                        if k >= 1:
                            rope_low(layer, i, units[k - 1])

                def body(i, last):
                    for j in range(layer.heads):
                        steps = layer.steps(j, last)
                        for k, unit in enumerate(steps):
                            if unit[0] == "N":
                                normalise(layer, i, *unit[1:])
                            elif is_rope(layer, unit) and not is_rope(layer, steps[k - 1]):
                                run = [unit]
                                while is_rope(layer, steps[k + len(run)]):
                                    run.append(steps[k + len(run)])
                                rope(i, run)
                        if layer is L1 and j == 0:
                            combine(i, 1, 0, layer.soft(i, 0, 0))
                            combine(i, 1, 1, layer.soft(i, 0, 1))
                        elif layer is L1 and not last:
                            combine(i + 1, 0, 0, layer.soft(i, 1, 0))
                            combine(i + 1, 0, 1, layer.soft(i, 1, 1))
                        for name in layer.splits[j]:
                            item(i, last, name)

                loop(pool, layer, body)

            pool.wait_ge(small_in, 48)
            for c in range(CTX_ITEMS):
                low(cT[0][:, c, :], cT[1][:, c, :], c + 1, SLOT[c])
            attention(L0)
            dest = {"F0": "QA", "F1": "QB", "W3a": "KV", "W3b": "O", "F2": "QA", "F3": "QB"}
            for k, name in enumerate(FFN_ITEMS[:4]):
                low(W[dest[name]][0][:], W[dest[name]][1][:], FFN_ITEM + k + 1, SLOT[FFN_ITEM + k])
            pool.wait_ge(row_in, 16)
            for b in range(B):
                pool.wait_ge(y_ready, B + b + 1)
                pool.tensor_tensor(xs[:, b, :], xs[:, b, :], lnw[:], ALU.add).then_inc(x_plus, 1)
            for k, name in enumerate(FFN_ITEMS[4:]):
                low(W[dest[name]][0][:], W[dest[name]][1][:], FFN_ITEM + k + 5, SLOT[FFN_ITEM + k + 4])
            attention(L1)
            low(W["QA"][0][:], W["QA"][1][:], ITEMS, SLOT[TAIL_ITEM])
            for b in range(B):
                pool.wait_ge(y_ready, 3 * B + b + 1)
                pool.tensor_tensor(xs[:, b, :], xs[:, b, :], probs[:, b % 2, :], ALU.add).then_inc(x_plus, 1)


def kernel(**inputs):
    import numpy as np
    import concourse.bacc as bacc
    from concourse.bass_utils import run_bass_kernel_spmd

    a = {k: np.asarray(v) for k, v in inputs.items()}

    def by_head(w):
        n = w.shape[1] // HD
        return w.reshape(C, 128, n, HD).transpose(2, 1, 0, 3).reshape(n, 128, C * HD)

    def pairs(w, v):
        return np.concatenate([w, v], axis=-1)

    def wo_items(w):
        return w.reshape(-1, 2, HD, D).transpose(0, 2, 1, 3).reshape(-1, 128, 2 * D)

    def ordered(layer, tables):
        items = [tables[n][0] for n in layer.early]
        for i in range(layer.iters):
            for n in layer.items:
                if n[0] == "O":
                    items.append(tables[n][i])
                elif i + 1 < layer.iters:
                    items.append(tables[n][i + 1])
        return items

    items = list(a["ctx_4096"].reshape(T, D).T.reshape(C, 128, T))
    q, o = by_head(a["L0_xattn_wq"]), wo_items(a["L0_xattn_wo"])
    items += ordered(L0, {"KV": pairs(by_head(a["L0_xattn_wk"]), by_head(a["L0_xattn_wv"])), "QA": pairs(q[0::4], q[1::4]),
                          "QB": pairs(q[2::4], q[3::4]), "O0": o[0::2], "O1": o[1::2]})
    w12 = by_head(a["L0_ffn_w12"].T)
    ffn = {f"F{j}": pairs(w12[j], w12[FFN_J + j]) for j in range(FFN_J)}
    ffn["W3a"], ffn["W3b"] = wo_items(a["L0_ffn_w3"].T)
    items += [ffn[n] for n in FFN_ITEMS]
    qk = pairs(by_head(a["L1_xattn_w_q"].T), by_head(a["L1_xattn_w_k"].T))
    v = a["L1_xattn_w_v"].T.reshape(C, 128, L1.iters, L1.v_cols).transpose(2, 1, 0, 3).reshape(L1.iters, 128, C * L1.v_cols)
    items += ordered(L1, {"KV": v, "QA": qk[0::2], "QB": qk[1::2], "O0": wo_items(a["L1_xattn_w_out"].T)})

    def chunked(w):
        return w.reshape(C, 128, -1).transpose(1, 0, 2).reshape(128, -1)

    tail = np.concatenate([chunked(a["L1_ffn_Wq"].T), chunked(a["L1_ffn_Wu1"].T)], axis=1)
    items.append(np.concatenate([tail, np.zeros((128, ITEM - tail.shape[1]), np.float32)], axis=1))
    assert len(items) == ITEMS

    freq = (1.0 / 10000.0 ** (np.arange(0, HD, 2, dtype=np.float32) / HD)).astype(np.float32)
    angle = (np.arange(S, dtype=np.float32)[:, None] * freq[None, :]).T
    root = float(HD) ** -0.25
    cos, sin = np.cos(angle) * root, np.sin(angle) * root
    cos_sin = np.stack([np.concatenate([cos, cos]), np.concatenate([-sin, sin])], axis=1).astype(np.float32)

    arrays = {
        "x": a["x"],
        "stream": np.concatenate(items, axis=0),
        "mask0": a["mask_BxSxS2_ff1"],
        "mask1": a["mask_BxSxS2_bk0"],
        "cos_sin": cos_sin,
        "ident_in": np.eye(128, dtype=np.float32),
        "position_bias": a["L1_xattn_position_bias"].reshape(-1, S),
        "ln_weight": a["L1_xattn_ln_weight"],
        "b12": a["L0_ffn_b12"].reshape(2 * FFN_J, 128).T,
        "b3": a["L0_ffn_b3"],
        "tail_wvd": chunked(a["L1_ffn_Wvd"].T).reshape(128, C, VB),
        "tail_auxv": chunked(a["L1_ffn_aux_values"].T).reshape(128, C, SLOTS),
        "tail_wvu": a["L1_ffn_Wvu"].T,
        "tail_keys": a["L1_ffn_aux_keys"].T,
        "tail_wr": a["L1_ffn_Wr"].T,
        "tail_logrel": a["L1_ffn_log_rel"],
        "tail_cols": np.stack([a["L1_ffn_bu1"], a["L1_ffn_Wu2"].reshape(128)], axis=1),
        "tail_scalars": np.concatenate([a[f"L1_ffn_{n}"].reshape(1) for n in ("gate_w1", "gate_bias", "bu2")]),
    }
    arrays = {k: np.ascontiguousarray(v) for k, v in arrays.items()}
    nc = bacc.Bacc("TRN2", target_bir_lowering=False, num_devices=1)
    args = {k: nc.dram_tensor(f"in_{k}", v.shape, mybir.dt.from_np(v.dtype), kind="ExternalInput").ap() for k, v in arrays.items()}
    out = nc.dram_tensor("out_0", (B, S, D), F32, kind="ExternalOutput").ap()
    xattn_ffn_kernel(nc, out=out, **args)
    got = run_bass_kernel_spmd(nc, [{f"in_{k}": v for k, v in arrays.items()}], core_ids=[0])
    return got.results[0]["out_0"]
```

```python
import concourse.bass as bass
from concourse import mybir
from contextlib import ExitStack

F32 = mybir.dt.float32
F32R = mybir.dt.float32r
ALU = mybir.AluOpType
ACT = mybir.ActivationFunctionType
AX = mybir.AxisListType

B = 8
S = 128
D = 512
C = D // 128
T = B * S
HALF = 512
HD = 128
EPS = 1e-5
EXP_MAX = 80.0
MASKED = -1e30
SLOTS = 128
BOT = 64
RDIM = 48
VB = 32
ITEM = 1024


class Layer:

    def __init__(self, name, iters, heads, shared_kv, ring_base, soft_base, item_base, slots):
        self.name, self.iters, self.heads, self.shared_kv = name, iters, heads, shared_kv
        self.rope = shared_kv
        self.v_cols = HD if shared_kv else heads * HD
        self.v_units = B * self.v_cols // HALF
        self.first = [("K", 0, 0), ("K", 0, 1), ("Q", 0, 0), ("Q", 0, 1)]
        self.ring_base = ring_base
        self.items = ["O0", "QA", "KV", "QB", "O1"] if shared_kv else ["QA", "O0", "KV", "QB"]
        self.early = ["KV", "QA", "QB"] if shared_kv else ["QA", "QB", "KV"]
        self.units = [e for j in range(heads) for e in self.steps(j, False) if e[0] in ("K", "Q", "V", "O", "PV")]
        self.high = [e for e in self.units if e[0] != "O" and not (shared_kv and e[0] == "V")]
        self.loop_ring = ring_base + len(self.first)
        self.ring_end = self.loop_ring + len(self.units) * iters - len(self.first)
        self.soft_base = soft_base
        self.soft_end = soft_base + 2 * heads * iters
        self.slots = slots
        self.item_base = item_base
        self.loop_item = item_base + len(self.early)
        self.item_end = self.loop_item + len(self.items) * iters - len(self.early)

    def steps(self, j, last):
        k, q = [("K", j + 1, u) for u in range(2)], [("Q", j + 1, u) for u in range(2)]
        k_next, q_next = ([], []) if last else (self.first[:2], self.first[2:])
        v = [("V", 0, n) for n in range(self.v_units)]
        w = [("W", 0, n) for n in range(2)]
        s = [("S", j, 0), ("S", j, 1), ("N", j, 0), ("N", j, 1)]
        t = [("T", j, u) for u in range(2)]
        pv = [[("PV", h, u) for u in range(2)] for h in range(self.heads)]
        o = [[("O", p, b) for b in range(B)] for p in range(self.heads // 2)]
        item = {n: [] if last and n[0] != "O" else [("I", n, 0)] for n in self.items}
        if self.shared_kv:
            a = [("A", n, 0) for n in (k_next + q_next if j == 3 else q)]
            if j == 0:
                return item["O0"] + s + v[:1] + q[:1] + w[:1] + q[1:] + a + v[1:] + t
            if j == 1:
                return item["QA"] + s + q[:1] + w[1:] + q[1:] + a + pv[0] + t
            if j == 2:
                return item["KV"] + s + q + a + pv[1] + t
            return (item["QB"] + s + o[0] + item["O1"] + pv[2] + t + k_next + a[:1] + q_next[:1] + a[1:2] + pv[3]
                    + a[2:3] + q_next[1:] + o[1][:2] + a[3:] + o[1][2:])
        c = [] if last and j == 1 else [("C", 1 - j, u) for u in range(2)]
        if j == 0:
            return s + c + v[:2] + t + item["QA"] + v[2:] + k + item["O0"] + q + pv[0]
        return s + c + k_next + t + item["KV"] + q_next[:1] + pv[1] + q_next[1:] + item["QB"] + o[0]

    def ring(self, i, unit, back=0):
        k = self.units.index(unit)
        if isinstance(i, int) and i == self.iters - 1:
            k -= len([n for n in self.units[:k] if n in self.first])
        return (i - back) * len(self.units) + (self.loop_ring + k + 1)

    def bank(self, unit, i=0):
        k = self.units.index(unit)
        return (self.loop_ring + k) % 4

    def soft(self, i, j, u):
        return i * (2 * self.heads) + (self.soft_base + 2 * j + u + 1)

    def item(self, i, name, back=0):
        at = self.items.index(name)
        if isinstance(i, int) and i == self.iters - 1:
            at = [n for n in self.items if n[0] == "O"].index(name)
        return (i - back) * len(self.items) + (self.loop_item + at + 1)


L0 = Layer("L0", 8, 4, True, 0, 0, 0, [2, 0, 1, 2, 0])
FFN_ITEMS = ["F0", "F1", "W3a", "W3b", "F2", "F3"]
FFN_ITEM = L0.item_end
FFN_RING = L0.ring_end
FFN_J = 4
X_UNITS = [(f"X{n}", j, u) for j in range(FFN_J) for u in range(2) for n in (1, 2)]
Y_RING = FFN_RING + len(X_UNITS)
L1 = Layer("L1", 16, 2, False, Y_RING + B, L0.soft_end, FFN_ITEM + len(FFN_ITEMS), [1, 0, 1, 0])
TAIL_ITEM = L1.item_end
TAIL_RING = L1.ring_end
ITEMS = TAIL_ITEM + 1
assert FFN_RING % 4 == 0 and L1.ring_base % 4 == 0 and len(L0.units) % 4 == 0 and len(L1.units) % 4 == 0


def slot_plan():
    slot = [0, 1, 0] + L0.slots * (L0.iters - 1) + [2, 1]
    slot += [0, 1] * (len(FFN_ITEMS) // 2)
    slot += [0, 1, 0] + L1.slots * (L1.iters - 1) + [1]
    return slot + [0]


SLOT = slot_plan()


def loads(n):
    return sum(1 for s in SLOT[:n + 1] if s == SLOT[n])


assert len(SLOT) == ITEMS and all(SLOT[n] != SLOT[n - 1] for n in range(1, ITEMS))
ROPE_ITER = len([n for n in L0.units if n[0] in "KQ"])
ROPE_ALL = len([n for n in L0.units if n[0] in "KQ"]) * L0.iters
LN_VE = [2 * B + 1, 2 * (2 * B + 2) - 1, 3 * (2 * B + 2) - 1, 4 * (2 * B + 2) - 1 + 4 + B]
LN_MS = LN_VE[2] + 4
TAIL_STEPS = (["vd", "gmat", "rk", "var1", "query0", "query1", "rq0", "rq1", "v0", "sq0", "poly0", "cubic0", "inner0",
               "router0", "router1", "v1", "sq1", "poly1", "cubic1", "inner1", "logsum"]
              + [f"max{b}" for b in range(B)] + ["e10", "sig0", "gelu0"] + [f"replace{b}" for b in range(B)]
              + ["e11", "sig1", "gelu1", "unselected", "attn0", "attn1", "selected", "amax", "learned", "mean", "imean",
                 "half_norm", "l1", "l2", "l3", "l4", "l5", "l6", "l7",
                 "gate_in", "g1", "g2", "gate", "isum", "scale", "weights0", "weights", "wT0", "wT"])
TD = {name: n + 1 for n, name in enumerate(TAIL_STEPS)}
OUT_READY = len(TAIL_STEPS)


def xattn_ffn_kernel(nc, x, ctx_t, stream, mask0, mask1, cos_sin, ident_in, position_bias, ln_weight, b12, b3,
                     tail_wvd, tail_auxv, tail_wvu, tail_keys, tail_wr, tail_logrel, tail_cols, tail_scalars, out):
    es = ExitStack()
    with es:
        def sb(name, shape, dt=F32):
            return es.enter_context(nc.sbuf_tensor(name, shape, dt))

        def sem(name):
            return es.enter_context(nc.semaphore(name))

        cT = [sb(f"cT_{p}", [128, C, T], F32R) for p in ("hi", "lo")]
        xT = [sb(f"xT_{p}", [128, C, T], F32R) for p in ("hi", "lo")]
        VO = [sb(f"VO_{p}", [128, 4 * T], F32R) for p in ("hi", "lo")]
        OT = [v[:, 2 * T:4 * T].rearrange("p (h t) -> p h t", h=2) for v in VO]
        GT = [v[:, :].rearrange("p (j t) -> p j t", j=4) for v in VO]
        W = {n: [sb(f"w{n}_{p}", [128, ITEM], F32R) for p in ("hi", "lo")] for n in ("QA", "QB", "KV", "O")}
        QT = [sb(f"QT_{p}", [128, T], F32R) for p in ("hi", "lo")]
        KT = [sb(f"KT_{p}", [128, T], F32R) for p in ("hi", "lo")]
        PT = [sb(f"PT_{p}", [128, 2, HALF], F32R) for p in ("hi", "lo")]
        raw = [sb(f"raw{n}", [128, ITEM]) for n in range(3)]
        xs = sb("xs", [128, B, D])
        neg = sb("neg", [128, B, S])
        probs = sb("probs", [128, 2, HALF])
        rot = sb("rot", [128, 2, HALF])
        prod = sb("prod", [128, 2, HALF])
        table = sb("table", [128, 2, HD])
        comb = rot
        vtmp = sb("vtmp", [128, HALF])
        ctx_raw = [t[:].rearrange("p a n -> p (a n)") for t in (rot, prod, probs)] + [raw[2][:]]
        lnw = sb("lnw", [128, D])
        ident = sb("ident", [128, 128])
        nmax = sb("nmax", [128, 2, 4])
        ssum = sb("ssum", [128, 2, 4])
        sinv = sb("sinv", [128, 2, 4])
        rsum = sb("rsum", [128, 2, 4])
        stats = sb("stats", [128, B, 6])
        mv = sb("mv", [128, B, 2])
        ve = sb("ve", [128, B])
        sd = sb("sd", [128, B])
        rstd = sb("rstd", [128, B])
        msq = sb("msq", [128, B])
        rrms = sb("rrms", [128, B])
        bcol = sb("bcol", [128, 2 * FFN_J])
        logrel = sb("logrel", [128, SLOTS])
        tcols = sb("tcols", [128, 2])
        tsc = sb("tsc", [128, 3])
        keys = sb("keys", [BOT, SLOTS])
        wr = sb("wr", [BOT, RDIM])
        rk = sb("rk", [RDIM, SLOTS])
        top = sb("top", [128, B, 8])
        col = sb("col", [128, 12, B])
        auxv = raw[2][:, 0:HALF].rearrange("p (c n) -> p c n", c=C)
        wvd = sb("wvd", [128, C, VB])
        wvu = raw[2][0:VB, HALF:2 * HALF]
        vd = sb("vd", [VB, SLOTS])[:]
        gmat = lnw[:]
        query = neg[:].rearrange("p b s -> p (b s)")
        rq = prod[:].rearrange("p a s -> p (a s)")
        allones = sb("allones", [128, 128])

        ring = [es.enter_context(nc.psum_tensor(f"ring{n}", [128, HALF], F32)) for n in range(4)]
        score = [es.enter_context(nc.psum_tensor(f"score{n}", [128, HALF], F32)) for n in range(2)]
        turned = [es.enter_context(nc.psum_tensor(f"turned{n}", [128, HALF], F32)) for n in range(2)]

        x_in = sem("x_in")
        small_in = sem("small_in")
        raw_in = [sem(f"raw_in{n}") for n in range(3)]
        w_hi = sem("w_hi")
        w_ready = sem("w_ready")
        ring_filled = sem("ring_filled")
        hi_done = sem("hi_done")
        ring_freed = sem("ring_freed")
        rope_sin = sem("rope_sin")
        rope_sum = sem("rope_sum")
        rope_hi = sem("rope_hi")
        rope_ready = sem("rope_ready")
        s_filled = sem("s_filled")
        masked_ready = sem("masked_ready")
        max_ready = sem("max_ready")
        exp_done = sem("exp_done")
        inv_ready = sem("inv_ready")
        rsum_ready = sem("rsum_ready")
        p_ready = sem("p_ready")
        t_filled = sem("t_filled")
        pt_hi = sem("pt_hi")
        pt_ready = sem("pt_ready")
        v_turned = sem("v_turned")
        v_hi = sem("v_hi")
        v_ready = sem("v_ready")
        ctx_in = [sem(f"ctx_in{c}") for c in range(C)]
        ctx_hi = sem("ctx_hi")
        ctx_ready = sem("ctx_ready")
        bias_in = [sem("bias_in_a"), sem("bias_in_b")]
        comb_ready = sem("comb_ready")
        neg_ready = sem("neg_ready")
        mask_in = sem("mask_in")
        ln_step = sem("ln_step")
        ln_sqrt = sem("ln_sqrt")
        y_ready = sem("y_ready")
        y_turned = sem("y_turned")
        y_hi = sem("y_hi")
        y_lo = sem("y_lo")
        x_plus = sem("x_plus")
        row_in = sem("row_in")
        g_step = sem("g_step")
        g_pre = sem("g_pre")
        gate_exp = sem("gate_exp")
        g_hi = sem("g_hi")
        g_lo = sem("g_lo")
        tail_in = sem("tail_in")
        tail_pe = sem("tail_pe")
        tail_act = sem("tail_act")
        tail_dve = sem("tail_dve")
        out_done = sem("out_done")

        def both(pair, fn):
            return [fn(t) for t in pair]

        PARTS = ((0, 0), (0, 1), (1, 0))

        def weights_of(layer, kind, j):
            if layer.shared_kv:
                name, half = ("KV", "KV".index(kind)) if kind in "KV" else (("QA", "QB")[j // 2], j % 2)
            else:
                name, half = ("QA", "QB")[j], 0 if kind == "Q" else 1
            return [w[:, half * HALF:(half + 1) * HALF].rearrange("p (c d) -> p c d", c=C) for w in W[name]]

        def item_of(layer, kind, j):
            if layer.shared_kv:
                return "KV" if kind in "KV" else ("QA", "QB")[j // 2]
            return ("QA", "QB")[j]

        def values(layer, part):
            return VO[part][:, 0:B * layer.v_cols].rearrange("p (b n) -> p b n", b=B)

        def destination(layer, unit):
            kind, j, u = unit
            if kind == "Q":
                return both(QT, lambda t: t[:, u * HALF:(u + 1) * HALF])
            if kind == "K":
                return both(KT, lambda t: t[:, u * HALF:(u + 1) * HALF])
            if kind == "V":
                return both(VO, lambda t: t[:, u * HALF:(u + 1) * HALF])
            return both(OT, lambda t: t[:, j % 2, u * HALF:(u + 1) * HALF])

        def rope_count(layer, i, unit):
            order = [n for n in layer.units if n[0] in "KQ"]
            if i is None:
                return layer.first.index(unit) + 1
            return i * len(order) + (len(layer.first) + order.index(unit) + 1)

        def hi_count(layer, i, unit):
            order = layer.high
            base = 0 if layer is L0 else HI_L1
            if i is None:
                return base + layer.first.index(unit) + 1
            k = order.index(unit)
            if isinstance(i, int) and i == layer.iters - 1:
                k -= len([n for n in order[:k] if n in layer.first])
            return i * len(order) + (base + len(layer.first) + k + 1)

        HI_L1 = len(L0.high) * L0.iters

        def ring_count(layer, i, unit):
            return layer.ring_base + layer.first.index(unit) + 1 if i is None else layer.ring(i, unit)

        def ring_bank(layer, i, unit):
            if i is None:
                return (layer.ring_base + layer.first.index(unit)) % 4
            if isinstance(i, int):
                return (layer.ring(i, unit) - 1) % 4
            return layer.bank(unit)

        def is_rope(layer, unit):
            return layer.rope and unit[0] in "KQ"

        DEST = {"KV": "KV", "QA": "QA", "QB": "QB", "O0": "O", "O1": "O"}

        def freed_by(layer, i, name):
            if name == "KV":
                return layer.ring(i, ("V", 0, layer.v_units - 1))
            if layer.shared_kv:
                if name == "QA":
                    return layer.ring(i, ("Q", 1, 1))
                if name == "QB":
                    return layer.ring(i, ("Q", 3, 1))
                if name == "O1":
                    return layer.ring(i, ("O", 0, B - 1))
                return layer.ring(i, ("O", 1, B - 1), back=1) if not isinstance(i, int) else layer.ring(i - 1, ("O", 1, B - 1))
            if name == "QA":
                return i * len(layer.units) + layer.loop_ring
            if name == "QB":
                return layer.ring(i, ("Q", 1, 1))
            return layer.ring(i, ("O", 0, B - 1), back=1) if not isinstance(i, int) else layer.ring(i - 1, ("O", 0, B - 1))

        def item_plan(layer, i, last, name):
            n = layer.item(i, name)
            if isinstance(n, int):
                return n, SLOT[n - 1], 16 * loads(n - 1)
            k = layer.items.index(name)
            slot = layer.slots[k]
            each = layer.slots.count(slot)
            return n, slot, i * (16 * each) + 16 * loads(layer.loop_item + k)

        def loop(eng, layer, body):
            with eng.Fori(0, layer.iters - 1) as i:
                body(i, False)
            body(layer.iters - 1, True)

        block = es.enter_context(nc.Block())

        @block.sync
        def _(sp):
            def load(n):
                if n >= 2:
                    sp.wait_ge(w_ready, n - 1)
                sp.dma_start(raw[SLOT[n]][:], stream[n * 128:(n + 1) * 128, :]).then_inc(raw_in[SLOT[n]], 16)

            def layer_loads(layer):
                for n in range(layer.item_base + 2 * (layer is L0), layer.loop_item):
                    load(n)

                def body(i, last):
                    for name in layer.items:
                        if last and name[0] != "O":
                            continue
                        if not layer.shared_kv and name == "QA":
                            sp.wait_ge(comb_ready, i * 4 + 2)
                            sp.dma_start(table[:, 0, :], position_bias[bass.ds(i * (2 * S) + 2 * S, S), :]).then_inc(bias_in[0], 16)
                        if not layer.shared_kv and name == "KV":
                            sp.wait_ge(comb_ready, i * 4 + 4)
                            sp.dma_start(table[:, 1, :], position_bias[bass.ds(i * (2 * S) + 3 * S, S), :]).then_inc(bias_in[1], 16)
                        n, slot, _ = item_plan(layer, i, last, name)
                        sp.wait_ge(w_ready, n - 2)
                        sp.dma_start(raw[slot][:], stream[bass.ds(n * 128 - 128, 128), :]).then_inc(raw_in[slot], 16)

                if layer is L0:
                    sp.wait_ge(ctx_ready, C)
                loop(sp, layer, body)

            sp.dma_start(ctx_raw[0], ctx_t[0:128, :]).then_inc(ctx_in[0], 16)
            load(0)
            for c in range(1, C):
                sp.dma_start(ctx_raw[c], ctx_t[c * 128:(c + 1) * 128, :]).then_inc(ctx_in[c], 16)
            sp.dma_start(xs[:], x.rearrange("b t d -> t b d")).then_inc(x_in, 16)
            load(1)
            sp.dma_start(neg[:], mask0.rearrange("b q k -> q b k")).then_inc(mask_in, 16)
            layer_loads(L0)
            for n in range(FFN_ITEM, FFN_ITEM + len(FFN_ITEMS)):
                load(n)
            layer_loads(L1)
            load(TAIL_ITEM)
            for b in range(B):
                sp.wait_ge(tail_dve, OUT_READY + b + 1)
                sp.dma_start(out[b], xs[:, b, :]).then_inc(out_done, 16)
            sp.wait_ge(out_done, 16 * B)

        @block.scalar
        def _(act):
            act.dma_start(ident[:], ident_in).then_inc(small_in, 16)
            act.dma_start(table[:], cos_sin).then_inc(small_in, 16)
            act.dma_start(bcol[:], b12).then_inc(small_in, 16)
            act.dma_start(lnw[:], b3.partition_broadcast(128)).then_inc(row_in, 16)
            act.dma_start(logrel[:], tail_logrel.partition_broadcast(128)).then_inc(tail_in, 16)
            act.dma_start(tcols[:], tail_cols).then_inc(tail_in, 16)
            act.dma_start(tsc[:], tail_scalars.partition_broadcast(128)).then_inc(tail_in, 16)
            act.dma_start(keys[:], tail_keys).then_inc(tail_in, 16)
            act.dma_start(wr[:], tail_wr).then_inc(tail_in, 16)
            act.dma_start(wvd[:], tail_wvd).then_inc(tail_in, 16)

            def high(dest, n, slot, count):
                act.wait_ge(raw_in[slot], count)
                act.activation(dest, raw[slot][:], ACT.Copy).then_inc(w_hi, 1)

            def normed(stage):
                act.wait_ge(ln_step, LN_VE[stage])
                act.activation(sd[:], ve[:], ACT.Sqrt).then_inc(ln_sqrt, 1)
                if stage == 2:
                    act.wait_ge(ln_step, LN_MS)
                    act.activation(msq[:], msq[:], ACT.Sqrt).then_inc(ln_sqrt, 1)
                for b in range(B):
                    act.wait_ge(y_turned, stage * B + b + 1)
                    act.activation(xT[0][:, :, b * S:(b + 1) * S],
                                   turned[b % 2][:].rearrange("p (c t) -> p c t", c=C), ACT.Copy).then_inc(y_hi, 1)

            def evacuate(layer, i, unit):
                act.wait_ge(ring_filled, ring_count(layer, i, unit))
                bank = ring[ring_bank(layer, i, unit)]
                if is_rope(layer, unit):
                    n = rope_count(layer, i, unit)
                    if not isinstance(n, int) or n > 2:
                        act.wait_ge(rope_sum, n - 2)
                    buf = rot[:, unit[2], :]
                    act.activation(buf[0:64, :], bank[64:128, :], ACT.Copy)
                    act.activation(buf[64:128, :], bank[0:64, :], ACT.Copy).then_inc(hi_done, 1)
                else:
                    act.activation(destination(layer, unit)[0], bank[:], ACT.Copy).then_inc(hi_done, 1)

            def exponentials(layer, i, j, u):
                act.wait_ge(max_ready, layer.soft(i, j, u))
                for t in range(4):
                    p = probs[:, u, t * S:(t + 1) * S]
                    ins = act.activation(p, p, ACT.Exp, bias=nmax[:, u, t:t + 1], accum_out=ssum[:, u, t:t + 1])
                ins.then_inc(exp_done, 1)

            def values_high(layer, i, n):
                act.wait_ge(v_turned, i * 2 + n + 1)
                act.activation(VO[0][:, n * HALF:(n + 1) * HALF], turned[n][:], ACT.Copy).then_inc(v_hi, 1)

            def turned_high(layer, i, j, u):
                act.wait_ge(t_filled, layer.soft(i, j, u))
                act.activation(PT[0][:, u, :], turned[u][:], ACT.Copy).then_inc(pt_hi, 1)

            def attention(layer):
                free = {"KV": Y_RING + B, "QA": FFN_RING + 12, "QB": FFN_RING + 16}
                for k, name in enumerate(layer.early):
                    n = layer.item_base + k
                    if layer is L1:
                        act.wait_ge(ring_filled, free[name])
                    high(W[name][0][:], n + 1, SLOT[n], 16 * loads(n))
                    if layer is L0 and name == "KV":
                        for c in range(1, C):
                            context_high(c)
                for unit in layer.first[:2]:
                    evacuate(layer, None, unit)
                normed(0 if layer is L0 else 2)
                for unit in layer.first[2:]:
                    evacuate(layer, None, unit)

                def item(i, last, name):
                    n, slot, count = item_plan(layer, i, last, name)
                    act.wait_ge(ring_filled, freed_by(layer, i, name))
                    high(W[DEST[name]][0][:], n, slot, count)

                def body(i, last):
                    for j in range(layer.heads):
                        for unit in layer.steps(j, last):
                            if unit[0] == "S":
                                exponentials(layer, i, *unit[1:])
                            elif unit[0] == "T":
                                turned_high(layer, i, *unit[1:])
                            elif unit[0] == "W":
                                values_high(layer, i, unit[2])
                            elif unit[0] == "I":
                                item(i, last, unit[1])
                            elif unit in layer.high:
                                evacuate(layer, i, unit)

                loop(act, layer, body)

            def context_high(c):
                act.wait_ge(ctx_in[c], 16)
                act.activation(cT[0][:, c, :], ctx_raw[c], ACT.Copy).then_inc(ctx_hi, 1)

            context_high(0)
            attention(L0)

            free = {"F0": L0.ring(7, ("Q", 1, 1)), "F1": L0.ring(7, ("Q", 3, 1)), "W3a": L0.ring(7, ("V", 0, 1)),
                    "W3b": L0.ring(7, ("O", 1, B - 1)), "F2": FFN_RING + 4, "F3": FFN_RING + 8}
            dest = {"F0": "QA", "F1": "QB", "W3a": "KV", "W3b": "O", "F2": "QA", "F3": "QB"}

            def ffn_item(name):
                n = FFN_ITEM + FFN_ITEMS.index(name)
                act.wait_ge(ring_filled, free[name])
                high(W[dest[name]][0][:], n + 1, SLOT[n], 16 * loads(n))

            for name in FFN_ITEMS[:4]:
                ffn_item(name)
            normed(1)
            for j in range(FFN_J):
                for u in range(2):
                    k = 2 * j + u
                    act.wait_ge(g_pre, k + 1)
                    act.activation(rot[:, u, :], rot[:, u, :], ACT.Exp, scale=-1.0).then_inc(gate_exp, 1)
                    act.wait_ge(ring_freed, FFN_RING + 2 * k + 2)
                    act.activation(GT[0][:, j, u * HALF:(u + 1) * HALF], prod[:, u, :], ACT.Copy).then_inc(g_hi, 1)
                    if u == 0 and j in (1, 2):
                        ffn_item(("F2", "F3")[j - 1])

            act.wait_ge(x_plus, B)
            act.dma_start(lnw[:], ln_weight.partition_broadcast(128)).then_inc(row_in, 16)
            act.dma_start(raw[2][:, 0:B * S // 4].bitcast(mybir.dt.uint8).rearrange("p (b k) -> p b k", b=B),
                          mask1.rearrange("b q k -> q b k")).then_inc(mask_in, 16)
            act.wait_ge(rope_ready, ROPE_ALL)
            act.dma_start(table[:, 0, :], position_bias[0:S, :]).then_inc(bias_in[0], 16)
            act.dma_start(table[:, 1, :], position_bias[S:2 * S, :]).then_inc(bias_in[1], 16)
            act.wait_ge(neg_ready, 3)
            act.dma_start(auxv, tail_auxv).then_inc(tail_in, 16)
            act.dma_start(wvu, tail_wvu).then_inc(tail_in, 16)
            attention(L1)

            act.wait_ge(ring_filled, TAIL_RING)
            high(W["QA"][0][:], ITEMS, SLOT[TAIL_ITEM], 16 * loads(TAIL_ITEM))
            normed(3)
            act.wait_ge(tail_dve, TD["var1"])
            act.activation(col[:, 1, :], col[:, 0, :], ACT.Ln).then_inc(tail_act, 1)
            for u in range(2):
                act.wait_ge(tail_dve, TD[f"inner{u}"])
                act.activation(rot[:, u, :], rot[:, u, :], ACT.Exp, scale=-2.0 * (2.0 / 3.141592653589793) ** 0.5).then_inc(tail_act, 1)
            act.wait_ge(tail_dve, TD["amax"])
            for b in range(B):
                p = raw[1][:, b * S:(b + 1) * S]
                act.activation(p, p, ACT.Exp, bias=col[:, 10, b:b + 1], accum_out=col[:, 11, b:b + 1]).then_inc(tail_act, 1)
            act.wait_ge(tail_dve, TD["learned"])
            act.activation(col[:, 4, :], col[:, 3, :], ACT.Exp, scale=-1.0).then_inc(tail_act, 1)
            act.wait_ge(tail_dve, TD["gate_in"])
            act.activation(col[:, 8, :], col[:, 7, :], ACT.Exp, scale=-1.0).then_inc(tail_act, 1)

        @block.tensor
        def _(pe):
            def ring_wait(n):
                if isinstance(n, int) and n <= 4:
                    return
                pe.wait_ge(ring_freed, n - 4)

            def project(layer, i, unit):
                kind, j, u = unit
                ring_wait(ring_count(layer, i, unit))
                bank = ring[ring_bank(layer, i, unit)]
                w = weights_of(layer, kind, j)
                src = xT if kind == "Q" else cT
                for c in range(C):
                    if layer is L0 and i is None and unit == layer.first[0]:
                        pe.wait_ge(ctx_ready, c + 1)
                    for k, (a, b) in enumerate(PARTS):
                        mm = pe.matmul(bank[:], w[a][:, c, :], src[b][:, c, u * HALF:(u + 1) * HALF],
                                       start=(c == 0 and k == 0), stop=(c == C - 1 and k == 2))
                mm.then_inc(ring_filled, 1)

            def project_values(layer, i, unit):
                ring_wait(ring_count(layer, i, unit))
                bank = ring[ring_bank(layer, i, unit)]
                n = layer.v_cols
                per = HALF // n
                w = both(W["KV"], lambda t: t[:].rearrange("p (c d) -> p c d", c=C))
                for r in range(per):
                    b = unit[2] * per + r
                    for c in range(C):
                        for k, (a, e) in enumerate(PARTS):
                            mm = pe.matmul(bank[:, r * n:(r + 1) * n], cT[a][:, c, b * S:(b + 1) * S], w[e][:, c, :],
                                           start=(c == 0 and k == 0), stop=(c == C - 1 and k == 2))
                mm.then_inc(ring_filled, 1)

            def output(layer, i, unit):
                _, pair, b = unit
                n = ring_count(layer, i, unit)
                ring_wait(n)
                bank = ring[ring_bank(layer, i, unit)]
                for h in range(2):
                    for k, (a, e) in enumerate(PARTS):
                        mm = pe.matmul(bank[:], OT[a][:, h, b * S:(b + 1) * S], W["O"][e][:, h * D:(h + 1) * D],
                                       start=(h == 0 and k == 0), stop=(h == 1 and k == 2))
                mm.then_inc(ring_filled, 1)

            def scores(layer, i, j, u):
                unit = ("Q", j, u)
                if layer.rope and j > 0:
                    pe.wait_ge(rope_ready, rope_count(layer, i, unit))
                elif layer.rope:
                    pe.wait_ge(rope_ready, i * ROPE_ITER + (len(layer.first) - 1 + u))
                elif j > 0:
                    pe.wait_ge(ring_freed, ring_count(layer, i, unit))
                else:
                    pe.wait_ge(ring_freed, i * len(layer.units) + (layer.loop_ring + layer.units.index(unit) + 1 - len(layer.units)))
                for t in range(4):
                    at = (4 * u + t) * S
                    for k, (a, b) in enumerate(PARTS):
                        mm = pe.matmul(score[u][:, t * S:(t + 1) * S], QT[a][:, at:at + S], KT[b][:, at:at + S],
                                       start=(k == 0), stop=(k == 2))
                mm.then_inc(s_filled, 1)

            def turn_values(layer, i, n):
                pe.wait_ge(ring_freed, layer.ring(i, ("V", 0, n)))
                if n == 1:
                    pe.wait_ge(pt_ready, layer.soft(i, 0, n))
                for t in range(4):
                    mm = pe.transpose(turned[n][:, t * S:(t + 1) * S], vtmp[:, t * S:(t + 1) * S], ident[:])
                mm.then_inc(v_turned, 1)

            def turn_probs(layer, i, j, u):
                pe.wait_ge(p_ready, layer.soft(i, j, u))
                if layer is L0 and j == 0 and u == 0:
                    pe.wait_ge(v_ready, i * 2 + 1)
                for t in range(4):
                    mm = pe.transpose(turned[u][:, t * S:(t + 1) * S], probs[:, u, t * S:(t + 1) * S], ident[:])
                mm.then_inc(t_filled, 1)

            def attend(layer, i, j, u):
                head = 0 if layer.shared_kv else j
                v = [values(layer, p) for p in range(2)]
                unit = ("PV", j, u)
                ring_wait(ring_count(layer, i, unit))
                pe.wait_ge(pt_ready, layer.soft(i, j, u))
                if j == 0 and layer.shared_kv:
                    pe.wait_ge(v_ready, i * 2 + u + 1)
                elif j == 0:
                    pe.wait_ge(ring_freed, layer.ring(i, ("V", 0, (u + 1) * layer.v_units // 2 - 1)))
                bank = ring[ring_bank(layer, i, unit)]
                for t in range(4):
                    b = 4 * u + t
                    for k, (a, e) in enumerate(PARTS):
                        mm = pe.matmul(bank[:, t * S:(t + 1) * S], v[a][:, b, head * HD:(head + 1) * HD],
                                       PT[e][:, u, t * S:(t + 1) * S], start=(k == 0), stop=(k == 2))
                mm.then_inc(ring_filled, 1)

            def outputs(layer, i, pair, b):
                if b == 0:
                    pe.wait_ge(w_ready, layer.item(i, f"O{pair}"))
                if b % 4 == 0:
                    pe.wait_ge(ring_freed, ring_count(layer, i, ("PV", 2 * pair + 1, b // 4)))
                output(layer, i, ("O", pair, b))

            def turn_rows(stage):
                for b in range(B):
                    pe.wait_ge(y_ready, stage * B + b + 1)
                    if stage * B + b >= 2:
                        pe.wait_ge(y_lo, stage * B + b - 1)
                    src = probs[:, b % 2, :]
                    for c in range(C):
                        mm = pe.transpose(turned[b % 2][:, c * 128:(c + 1) * 128], src[:, c * 128:(c + 1) * 128], ident[:])
                    mm.then_inc(y_turned, 1)

            def attention(layer):
                stage = 0 if layer is L0 else 2
                pe.wait_ge(w_ready, layer.item_base + layer.early.index(item_of(layer, "K", 0)) + 1)
                for unit in layer.first[:2]:
                    project(layer, None, unit)
                turn_rows(stage)
                pe.wait_ge(w_ready, layer.item_base + layer.early.index("QA") + 1)
                for unit in layer.first[2:]:
                    pe.wait_ge(y_lo, stage * B + 4 * (unit[2] + 1))
                    project(layer, None, unit)
                pe.wait_ge(w_ready, layer.loop_item)
                if layer is L1:
                    pe.wait_ge(ring_freed, layer.loop_ring)

                def weights_wait(i, unit):
                    kind, j, _ = unit
                    if kind != "V" and j == 0:
                        pe.wait_ge(w_ready, layer.item(i, item_of(layer, kind, 0)))
                    else:
                        name = "KV" if kind == "V" else item_of(layer, kind, j)
                        pe.wait_ge(w_ready, i * len(layer.items) + (layer.loop_item - len(layer.items) + layer.items.index(name) + 1))

                def body(i, last):
                    for j in range(layer.heads):
                        for unit in layer.steps(j, last):
                            if unit in layer.units and unit[0] in "KQV" and unit[2] == 0:
                                weights_wait(i, unit)
                            if unit[0] == "S":
                                scores(layer, i, *unit[1:])
                            elif unit[0] == "T":
                                turn_probs(layer, i, *unit[1:])
                            elif unit[0] == "PV":
                                attend(layer, i, *unit[1:])
                            elif unit[0] == "O":
                                outputs(layer, i, *unit[1:])
                            elif unit[0] == "W":
                                turn_values(layer, i, unit[2])
                            elif unit[0] == "V" and not layer.shared_kv:
                                project_values(layer, i, unit)
                            elif unit in layer.units:
                                project(layer, i, unit)

                loop(pe, layer, body)

            pe.wait_ge(small_in, 48)
            attention(L0)

            turn_rows(1)
            for j in range(FFN_J):
                pe.wait_ge(w_ready, FFN_ITEM + FFN_ITEMS.index(f"F{j}") + 1)
                for u in range(2):
                    if j == 0:
                        pe.wait_ge(y_lo, B + 4 * (u + 1))
                    for half in range(2):
                        k = 4 * j + 2 * u + half
                        ring_wait(FFN_RING + k + 1)
                        w = both(W[("QA", "QB")[j % 2]], lambda t: t[:, half * HALF:(half + 1) * HALF].rearrange("p (c d) -> p c d", c=C))
                        for c in range(C):
                            for p, (a, b) in enumerate(PARTS):
                                mm = pe.matmul(ring[(FFN_RING + k) % 4][:], w[a][:, c, :], xT[b][:, c, u * HALF:(u + 1) * HALF],
                                               start=(c == 0 and p == 0), stop=(c == C - 1 and p == 2))
                        mm.then_inc(ring_filled, 1)
            for b in range(B):
                ring_wait(Y_RING + b + 1)
                pe.wait_ge(g_lo, 2 * FFN_J - 1 + b // 4)
                for j in range(FFN_J):
                    w = W[("KV", "O")[j // 2]]
                    for p, (a, e) in enumerate(PARTS):
                        mm = pe.matmul(ring[(Y_RING + b) % 4][:], GT[a][:, j, b * S:(b + 1) * S],
                                       w[e][:, (j % 2) * D:(j % 2 + 1) * D], start=(j == 0 and p == 0), stop=(j == FFN_J - 1 and p == 2))
                mm.then_inc(ring_filled, 1)

            attention(L1)

            pe.wait_ge(tail_in, 16 * 8)
            for c in range(C):
                mm = pe.matmul(score[0][0:VB, 0:SLOTS], wvd[:, c, :], auxv[:, c, :], start=(c == 0), stop=(c == C - 1))
            mm.then_inc(tail_pe, 1)
            pe.wait_ge(tail_dve, TD["vd"])
            pe.matmul(score[1][:], vd, wvu, start=True, stop=True).then_inc(tail_pe, 1)
            pe.matmul(ring[0][0:RDIM, 0:SLOTS], wr[:], keys[:], start=True, stop=True).then_inc(tail_pe, 1)
            turn_rows(3)
            pe.wait_ge(w_ready, ITEMS)
            wq = both(W["QA"], lambda t: t[:, 0:C * BOT].rearrange("p (c d) -> p c d", c=C))
            wu = both(W["QA"], lambda t: t[:, C * BOT:C * (BOT + 128)].rearrange("p (c d) -> p c d", c=C))
            for w, m, banks in ((wq, BOT, (3, 0)), (wu, 128, (1, 2))):
                for u in range(2):
                    if banks[u] == 0:
                        pe.wait_ge(tail_dve, TD["rk"])
                    pe.wait_ge(y_lo, 3 * B + 4 * (u + 1))
                    for c in range(C):
                        for p, (a, b) in enumerate(PARTS):
                            mm = pe.matmul(ring[banks[u]][0:m, :], w[a][:, c, :], xT[b][:, c, u * HALF:(u + 1) * HALF],
                                           start=(c == 0 and p == 0), stop=(c == C - 1 and p == 2))
                    mm.then_inc(tail_pe, 1)
            for u in range(2):
                pe.wait_ge(tail_dve, TD[f"query{u}"])
                pe.matmul(turned[u][0:RDIM, :], wr[:], query[0:BOT, u * HALF:(u + 1) * HALF], start=True, stop=True).then_inc(tail_pe, 1)
            for u in range(2):
                pe.wait_ge(tail_dve, TD[f"rq{u}"])
                for t in range(4):
                    at = (4 * u + t) * S
                    mm = pe.matmul(score[u][:, t * S:(t + 1) * S], rq[0:RDIM, at:at + S], rk[:], start=True, stop=True)
                mm.then_inc(tail_pe, 1)
            for u in range(2):
                for t in range(4):
                    at = (4 * u + t) * S
                    mm = pe.matmul(ring[(3, 0)[u]][:, t * S:(t + 1) * S], query[0:BOT, at:at + S], keys[:], start=True, stop=True)
                mm.then_inc(tail_pe, 1)
            pe.wait_ge(tail_dve, TD["logsum"])
            pe.matmul(turned[0][:, 0:1], allones[:], col[:, 2, 0:1], start=True, stop=True).then_inc(tail_pe, 1)
            for u in range(2):
                pe.wait_ge(tail_dve, TD[f"gelu{u}"])
                for t in range(4):
                    mm = pe.matmul(turned[1][:, 4 * u + t:4 * u + t + 1], rot[:, u, t * S:(t + 1) * S], tcols[:, 1:2], start=True, stop=True)
            mm.then_inc(tail_pe, 1)
            for u in range(2):
                pe.wait_ge(tail_dve, TD["weights"] - 1 + u)
                for t in range(4):
                    at = (4 * u + t) * S
                    mm = pe.transpose(score[u][:, t * S:(t + 1) * S], raw[1][:, at:at + S], ident[:])
                mm.then_inc(tail_pe, 1)
            for b in range(B):
                pe.wait_ge(tail_dve, TD["wT"] - 1 + b // 4)
                if b >= 4:
                    pe.wait_ge(tail_dve, OUT_READY + b - 3)
                pe.matmul(ring[b % 4][:], rot[:, b // 4, (b % 4) * S:(b % 4 + 1) * S], gmat, start=True, stop=True).then_inc(tail_pe, 1)

        @block.vector
        def _(dve):
            dve.memset(allones[:], 1.0).then_inc(neg_ready, 1)

            class Steps:
                n = 0

            def step():
                Steps.n += 1
                return Steps.n

            def stats_of(b, added=None):
                if added is not None:
                    dve.wait_ge(ring_freed, added)
                dve.bn_stats(stats[:, b, :], xs[:, b, :]).then_inc(ln_step, 1)
                step()

            def means():
                for b in range(B):
                    if b == 0:
                        dve.wait_ge(ln_step, Steps.n)
                    dve.bn_aggr(mv[:, b, :], stats[:, b, :]).then_inc(ln_step, 1)
                    step()

            def lower(stage, b):
                dve.wait_ge(y_hi, stage * B + b + 1)
                dst = slice(b * S, (b + 1) * S)
                dve.tensor_tensor(xT[1][:, :, dst], turned[b % 2][:].rearrange("p (c t) -> p c t", c=C),
                                  xT[0][:, :, dst].bitcast(F32), ALU.subtract).then_inc(y_lo, 1)

            def normed(stage):
                means()
                dve.wait_ge(ln_step, Steps.n)
                dve.tensor_scalar(ve[:], mv[:, :, 1], EPS, None, ALU.add).then_inc(ln_step, 1)
                assert step() == LN_VE[stage], (stage, Steps.n)
                dve.wait_ge(ln_sqrt, stage + 1 + (stage == 3))
                dve.reciprocal(rstd[:], sd[:]).then_inc(ln_step, 1)
                dve.wait_ge(ln_step, step())
                if stage >= 2:
                    dve.tensor_tensor(msq[:], mv[:, :, 1], rstd[:], ALU.mult).then_inc(ln_step, 1)
                    dve.wait_ge(ln_step, step())
                    dve.tensor_tensor(msq[:], msq[:], rstd[:], ALU.mult).then_inc(ln_step, 1)
                    dve.wait_ge(ln_step, step())
                if stage == 2:
                    dve.tensor_scalar(msq[:], msq[:], EPS, None, ALU.add).then_inc(ln_step, 1)
                    assert step() == LN_MS, Steps.n
                    dve.wait_ge(ln_sqrt, stage + 2)
                    dve.reciprocal(rrms[:], msq[:]).then_inc(ln_step, 1)
                    dve.wait_ge(ln_step, step())
                    dve.wait_ge(row_in, 32)
                for b in range(B):
                    if b >= 2:
                        dve.wait_ge(y_turned, stage * B + b - 1)
                    y = probs[:, b % 2, :]
                    if stage == 3 and b >= 2:
                        dve.wait_ge(x_plus, 2 * B + b - 1)
                    if stage != 2:
                        dve.tensor_scalar(y, xs[:, b, :], mv[:, b, 0:1], rstd[:, b:b + 1], ALU.subtract, ALU.mult).then_inc(y_ready, 1)
                    else:
                        if b >= 2:
                            dve.wait_ge(x_plus, B + b - 1)
                        y2 = prod[:, b % 2, :]
                        dve.tensor_scalar(y2, xs[:, b, :], mv[:, b, 0:1], rstd[:, b:b + 1], ALU.subtract, ALU.mult).then_inc(ln_step, 1)
                        dve.wait_ge(ln_step, step())
                        dve.scalar_tensor_tensor(y, y2, rrms[:, b:b + 1], lnw[:], ALU.mult, ALU.mult).then_inc(y_ready, 1)
                    if b >= 1:
                        lower(stage, b - 1)
                lower(stage, B - 1)

            def lows(layer, i, unit):
                hi, lo = destination(layer, unit)
                dve.wait_ge(hi_done, hi_count(layer, i, unit))
                dve.tensor_tensor(lo, ring[ring_bank(layer, i, unit)][:], hi.bitcast(F32), ALU.subtract).then_inc(ring_freed, 1)

            def rope_cos(layer, i, unit):
                n = rope_count(layer, i, unit)
                dve.wait_ge(hi_done, hi_count(layer, i, unit))
                if not isinstance(n, int) or n > 2:
                    dve.wait_ge(rope_ready, n - 2)
                dve.tensor_tensor(prod[:, unit[2], :].rearrange("p (b t) -> p b t", b=4),
                                  ring[ring_bank(layer, i, unit)][:].rearrange("p (b t) -> p b t", b=4),
                                  table[:, 0:1, :].to_broadcast([128, 4, HD]), ALU.mult).then_inc(ring_freed, 1)

            def rope_add(layer, i, unit):
                n = rope_count(layer, i, unit)
                dve.wait_ge(rope_sin, n)
                dve.wait_ge(ring_freed, ring_count(layer, i, unit))
                p = prod[:, unit[2], :]
                dve.tensor_tensor(p, p, rot[:, unit[2], :], ALU.add).then_inc(rope_sum, 1)
                dve.wait_ge(rope_sum, n)
                dve.tensor_copy(destination(layer, unit)[0], p).then_inc(rope_hi, 1)

            def evacuate(layer, i, units):
                for k, unit in enumerate(units):
                    if not is_rope(layer, unit):
                        lows(layer, i, unit)
                        continue
                    rope_cos(layer, i, unit)
                    if k >= 1:
                        rope_add(layer, i, units[k - 1])
                if is_rope(layer, units[-1]):
                    rope_add(layer, i, units[-1])

            def mask_and_max(layer, i, j, u):
                dve.wait_ge(s_filled, layer.soft(i, j, u))
                if layer is L1:
                    dve.wait_ge(comb_ready, i * 4 + 2 * j + u + 1)
                p4 = probs[:, u, :].rearrange("p (b k) -> p b k", b=4)
                s4 = score[u][:].rearrange("p (b k) -> p b k", b=4)
                add = neg[:, 4 * u:4 * u + 4, :] if layer is L0 else comb[:, u, :].rearrange("p (b k) -> p b k", b=4)
                dve.tensor_tensor(p4, s4, add, ALU.add).then_inc(masked_ready, 1)
                dve.wait_ge(masked_ready, layer.soft(i, j, u))
                dve.tensor_reduce(nmax[:, u, :], p4, AX.X, ALU.max, negate=True).then_inc(max_ready, 1)

            def inverse_sum(layer, i, j, u):
                dve.wait_ge(exp_done, layer.soft(i, j, u))
                if layer is L0:
                    dve.reciprocal(rsum[:, u, :], ssum[:, u, :]).then_inc(rsum_ready, 1)
                else:
                    dve.reciprocal(sinv[:, u, :], ssum[:, u, :]).then_inc(inv_ready, 1)
                    dve.wait_ge(inv_ready, i * 4 + 2 * j + u + 1)
                    dve.scalar_tensor_tensor(rsum[:, u, :], nmax[:, u, :], -0.5 * MASKED, sinv[:, u, :],
                                             ALU.is_lt, ALU.mult).then_inc(rsum_ready, 1)

            def add_output(layer, i, unit):
                b = unit[2]
                dve.wait_ge(ring_filled, ring_count(layer, i, unit))
                dve.tensor_tensor(xs[:, b, :], ring[ring_bank(layer, i, unit)][:], xs[:, b, :], ALU.add).then_inc(ring_freed, 1)

            def values_low(layer, i, n):
                cols = slice(n * HALF, (n + 1) * HALF)
                dve.wait_ge(v_hi, i * 2 + n + 1)
                dve.tensor_tensor(VO[1][:, cols], turned[n][:], VO[0][:, cols].bitcast(F32), ALU.subtract).then_inc(v_ready, 1)

            def turned_low(layer, i, j, u):
                dve.wait_ge(pt_hi, layer.soft(i, j, u))
                dve.tensor_tensor(PT[1][:, u, :], turned[u][:], PT[0][:, u, :].bitcast(F32), ALU.subtract).then_inc(pt_ready, 1)

            def attention(layer):
                evacuate(layer, None, layer.first[:2])
                if layer is L0:
                    dve.wait_ge(x_in, 16)
                    for b in range(B):
                        stats_of(b)
                    normed(0)
                    dve.wait_ge(mask_in, 16)
                    dve.tensor_scalar(neg[:], neg[:], 0.0, MASKED, ALU.is_equal, ALU.mult).then_inc(neg_ready, 1)
                    dve.wait_ge(neg_ready, 2)
                else:
                    normed(2)
                evacuate(layer, None, layer.first[2:])
                if layer is L1:
                    dve.wait_ge(x_plus, 2 * B)

                def body(i, last):
                    for j in range(layer.heads):
                        for unit in layer.steps(j, last):
                            if unit[0] == "S":
                                mask_and_max(layer, i, *unit[1:])
                            elif unit[0] == "N":
                                inverse_sum(layer, i, *unit[1:])
                            elif unit[0] == "T":
                                turned_low(layer, i, *unit[1:])
                            elif unit[0] == "O":
                                add_output(layer, i, unit)
                                if last and unit[1] == layer.heads // 2 - 1 and unit[2] >= 1:
                                    stats_of(unit[2] - 1, ring_count(layer, i, unit) - 1)
                            elif unit[0] == "W":
                                values_low(layer, i, unit[2])
                            elif unit[0] == "A":
                                rope_add(layer, i, unit[1])
                            elif unit not in layer.units:
                                pass
                            elif unit[0] == "V" and layer.shared_kv:
                                dve.wait_ge(ring_filled, ring_count(layer, i, unit))
                                dve.tensor_copy(vtmp[:], ring[ring_bank(layer, i, unit)][:]).then_inc(ring_freed, 1)
                            elif is_rope(layer, unit):
                                rope_cos(layer, i, unit)
                            else:
                                lows(layer, i, unit)

                loop(dve, layer, body)

            for c in range(C):
                dve.wait_ge(ctx_hi, c + 1)
                dve.tensor_tensor(cT[1][:, c, :], ctx_raw[c], cT[0][:, c, :].bitcast(F32), ALU.subtract).then_inc(ctx_ready, 1)
            dve.wait_ge(small_in, 48)
            dve.wait_ge(ctx_ready, C)
            attention(L0)

            stats_of(B - 1, L0.ring_end)
            normed(1)

            def bounded(k):
                dve.wait_ge(ring_filled, FFN_RING + 2 * k + 1)
                dve.tensor_scalar(rot[:, k % 2, :], ring[(FFN_RING + 2 * k) % 4][:], bcol[:, k // 2:k // 2 + 1], -EXP_MAX,
                                  ALU.add, ALU.max).then_inc(g_pre, 1)

            bounded(0)
            for j in range(FFN_J):
                for u in range(2):
                    k = 2 * j + u
                    r = rot[:, u, :]
                    if k + 1 < 2 * FFN_J:
                        bounded(k + 1)
                    dve.wait_ge(gate_exp, k + 1)
                    dve.tensor_scalar(r, r, 1.0, None, ALU.add).then_inc(g_step, 1)
                    dve.wait_ge(g_step, 2 * k + 1)
                    dve.reciprocal(r, r).then_inc(g_step, 1)
                    dve.wait_ge(g_step, 2 * k + 2)
                    dve.scalar_tensor_tensor(r, ring[(FFN_RING + 2 * k) % 4][:], bcol[:, j:j + 1], r, ALU.add, ALU.mult).then_inc(ring_freed, 1)
                    dve.wait_ge(ring_freed, FFN_RING + 2 * k + 1)
                    dve.wait_ge(ring_filled, FFN_RING + 2 * k + 2)
                    if k >= 2:
                        dve.wait_ge(g_lo, k - 1)
                    dve.scalar_tensor_tensor(prod[:, u, :], ring[(FFN_RING + 2 * k + 1) % 4][:], bcol[:, FFN_J + j:FFN_J + j + 1], r,
                                             ALU.add, ALU.mult).then_inc(ring_freed, 1)
                    dve.wait_ge(g_hi, k + 1)
                    cols = slice(u * HALF, (u + 1) * HALF)
                    dve.tensor_tensor(GT[1][:, j, cols], prod[:, u, :], GT[0][:, j, cols].bitcast(F32), ALU.subtract).then_inc(g_lo, 1)
            dve.wait_ge(x_plus, B)
            for b in range(B):
                dve.wait_ge(ring_filled, Y_RING + b + 1)
                dve.tensor_tensor(xs[:, b, :], ring[(Y_RING + b) % 4][:], xs[:, b, :], ALU.add).then_inc(ring_freed, 1)
                if b >= 1:
                    stats_of(b - 1, Y_RING + b)
            stats_of(B - 1, Y_RING + B)
            dve.wait_ge(mask_in, 32)
            dve.tensor_scalar(neg[:], raw[2][:, 0:B * S // 4].bitcast(mybir.dt.uint8).rearrange("p (b k) -> p b k", b=B),
                              0.0, MASKED, ALU.is_equal, ALU.mult).then_inc(neg_ready, 1)
            attention(L1)

            names = []

            def mark(name):
                names.append(name)
                assert name not in TD or TD[name] == len(names), (name, len(names))
                return len(names)

            stats_of(B - 1, TAIL_RING)
            dve.wait_ge(tail_pe, 1)
            dve.tensor_copy(vd, score[0][0:VB, 0:SLOTS]).then_inc(tail_dve, 1)
            mark("vd")
            dve.wait_ge(tail_pe, 2)
            dve.tensor_copy(gmat, score[1][:]).then_inc(tail_dve, 1)
            mark("gmat")
            dve.wait_ge(tail_pe, 3)
            dve.tensor_copy(rk[:], ring[0][0:RDIM, 0:SLOTS]).then_inc(tail_dve, 1)
            mark("rk")
            normed(3)
            dve.tensor_scalar(col[:, 0, :], msq[:], 1.0, None, ALU.add).then_inc(tail_dve, 1)
            mark("var1")
            def gelu_inner(u):
                dve.wait_ge(tail_pe, 6 + u)
                v, w = probs[:, u, :], rot[:, u, :]
                dve.tensor_scalar(v, ring[1 + u][:], tcols[:, 0:1], None, ALU.add).then_inc(tail_dve, 1)
                dve.wait_ge(tail_dve, mark(f"v{u}"))
                dve.tensor_tensor(w, v, v, ALU.mult).then_inc(tail_dve, 1)
                dve.wait_ge(tail_dve, mark(f"sq{u}"))
                dve.tensor_scalar(w, w, 0.044715, 1.0, ALU.mult, ALU.add).then_inc(tail_dve, 1)
                dve.wait_ge(tail_dve, mark(f"poly{u}"))
                dve.tensor_tensor(w, w, v, ALU.mult).then_inc(tail_dve, 1)
                dve.wait_ge(tail_dve, mark(f"cubic{u}"))
                dve.tensor_scalar(w, w, -0.5 * EXP_MAX, None, ALU.max).then_inc(tail_dve, 1)
                mark(f"inner{u}")

            def gelu(u):
                v, w = probs[:, u, :], rot[:, u, :]
                dve.wait_ge(tail_act, 2 + u)
                dve.tensor_scalar(w, w, 1.0, None, ALU.add).then_inc(tail_dve, 1)
                dve.wait_ge(tail_dve, mark(f"e1{u}"))
                dve.reciprocal(w, w).then_inc(tail_dve, 1)
                dve.wait_ge(tail_dve, mark(f"sig{u}"))
                dve.tensor_tensor(w, w, v, ALU.mult).then_inc(tail_dve, 1)
                mark(f"gelu{u}")

            lr = logrel[:, :].rearrange("p (a n) -> p a n", a=1).to_broadcast([128, 4, SLOTS])
            R3 = raw[0][:].rearrange("p (b n) -> p b n", b=B)
            A3 = raw[1][:].rearrange("p (b n) -> p b n", b=B)
            X3 = raw[2][:].rearrange("p (b n) -> p b n", b=B)
            for u in range(2):
                dve.wait_ge(tail_pe, 4 + u)
                dve.tensor_copy(query[0:BOT, u * HALF:(u + 1) * HALF], ring[(3, 0)[u]][0:BOT, :]).then_inc(tail_dve, 1)
                mark(f"query{u}")
            dve.wait_ge(x_plus, 4 * B - B)
            for u in range(2):
                dve.wait_ge(tail_pe, 8 + u)
                dve.tensor_copy(rq[0:RDIM, u * HALF:(u + 1) * HALF], turned[u][0:RDIM, :]).then_inc(tail_dve, 1)
                mark(f"rq{u}")
            gelu_inner(0)
            for u in range(2):
                dve.wait_ge(tail_pe, 10 + u)
                dve.scalar_tensor_tensor(R3[:, 4 * u:4 * u + 4, :], score[u][:].rearrange("p (b n) -> p b n", b=4),
                                         float(RDIM) ** -0.5, lr, ALU.mult, ALU.add).then_inc(tail_dve, 1)
                mark(f"router{u}")
            gelu_inner(1)
            dve.wait_ge(tail_act, 1)
            dve.tensor_reduce(col[:, 2, 0:1], col[:, 1, :], AX.X, ALU.add).then_inc(tail_dve, 1)
            dve.wait_ge(tail_dve, mark("logsum"))
            for b in range(B):
                dve.max(top[:, b, :], R3[:, b, :]).then_inc(tail_dve, 1)
                mark(f"max{b}")
            dve.wait_ge(tail_dve, len(names))
            gelu(0)
            for b in range(B):
                dve.match_replace(X3[:, b, :], top[:, b, :], R3[:, b, :], -3e38).then_inc(tail_dve, 1)
                mark(f"replace{b}")
            gelu(1)
            dve.tensor_tensor(R3, X3, R3, ALU.is_equal).then_inc(tail_dve, 1)
            mark("unselected")
            for u in range(2):
                dve.wait_ge(tail_pe, 12 + u)
                dve.scalar_tensor_tensor(A3[:, 4 * u:4 * u + 4, :], ring[(3, 0)[u]][:].rearrange("p (b n) -> p b n", b=4),
                                         float(BOT) ** -0.5, lr, ALU.mult, ALU.add).then_inc(tail_dve, 1)
                mark(f"attn{u}")
            dve.wait_ge(tail_dve, len(names))
            dve.scalar_tensor_tensor(raw[1][:], raw[0][:], MASKED, raw[1][:], ALU.mult, ALU.add).then_inc(tail_dve, 1)
            dve.wait_ge(tail_dve, mark("selected"))
            dve.tensor_reduce(col[:, 10, :], A3, AX.X, ALU.max, negate=True).then_inc(tail_dve, 1)
            mark("amax")
            dve.wait_ge(tail_pe, 15)
            dve.tensor_scalar(col[:, 3, :], turned[1][:, 0:B], tsc[:, 2:3], -EXP_MAX, ALU.add, ALU.max).then_inc(tail_dve, 1)
            mark("learned")
            dve.tensor_scalar(col[:, 2, 1:2], turned[0][:, 0:1], 1.0 / T, 1e-6, ALU.mult, ALU.add).then_inc(tail_dve, 1)
            dve.wait_ge(tail_dve, mark("mean"))
            dve.reciprocal(col[:, 2, 2:3], col[:, 2, 1:2]).then_inc(tail_dve, 1)
            dve.wait_ge(tail_dve, mark("imean"))
            dve.tensor_scalar(col[:, 5, :], col[:, 1, :], col[:, 2, 2:3], 0.5, ALU.mult, ALU.mult).then_inc(tail_dve, 1)
            mark("half_norm")
            dve.wait_ge(tail_act, 4 + B)
            dve.tensor_scalar(col[:, 4, :], col[:, 4, :], 1.0, None, ALU.add).then_inc(tail_dve, 1)
            dve.wait_ge(tail_dve, mark("l1"))
            dve.reciprocal(col[:, 4, :], col[:, 4, :]).then_inc(tail_dve, 1)
            dve.wait_ge(tail_dve, mark("l2"))
            dve.scalar_tensor_tensor(col[:, 6, :], col[:, 4, :], 2.5, col[:, 5, :], ALU.mult, ALU.add).then_inc(tail_dve, 1)
            dve.wait_ge(tail_dve, mark("l3"))
            dve.tensor_scalar(col[:, 6, :], col[:, 6, :], 0.0, 5.0, ALU.max, ALU.min).then_inc(tail_dve, 1)
            dve.wait_ge(tail_dve, mark("l4"))
            dve.tensor_scalar(col[:, 6, :], col[:, 6, :], 0.5, 1.0 / 1.5, ALU.subtract, ALU.mult).then_inc(tail_dve, 1)
            dve.wait_ge(tail_dve, mark("l5"))
            dve.tensor_scalar(col[:, 6, :], col[:, 6, :], 0.0, 1.0, ALU.max, ALU.min).then_inc(tail_dve, 1)
            dve.wait_ge(tail_dve, mark("l6"))
            dve.tensor_scalar(col[:, 7, :], col[:, 6, :], tsc[:, 0:1], tsc[:, 1:2], ALU.mult, ALU.add).then_inc(tail_dve, 1)
            dve.wait_ge(tail_dve, mark("l7"))
            dve.tensor_scalar(col[:, 7, :], col[:, 7, :], -EXP_MAX, None, ALU.max).then_inc(tail_dve, 1)
            mark("gate_in")
            dve.wait_ge(tail_act, 5 + B)
            dve.tensor_scalar(col[:, 8, :], col[:, 8, :], 1.0, None, ALU.add).then_inc(tail_dve, 1)
            dve.wait_ge(tail_dve, mark("g1"))
            dve.reciprocal(col[:, 8, :], col[:, 8, :]).then_inc(tail_dve, 1)
            dve.wait_ge(tail_dve, mark("g2"))
            dve.scalar_tensor_tensor(col[:, 9, :], col[:, 8, :], 0.05, col[:, 8, :], ALU.is_ge, ALU.mult).then_inc(tail_dve, 1)
            dve.wait_ge(tail_act, 5 + B)
            dve.reciprocal(col[:, 0, :], col[:, 11, :]).then_inc(tail_dve, 1)
            mark("gate")
            dve.wait_ge(tail_dve, mark("isum"))
            dve.tensor_tensor(col[:, 0, :], col[:, 0, :], col[:, 9, :], ALU.mult).then_inc(tail_dve, 1)
            dve.wait_ge(tail_dve, mark("scale"))
            for u in range(2):
                dve.tensor_tensor(A3[:, 4 * u:4 * u + 4, :], A3[:, 4 * u:4 * u + 4, :],
                                  col[:, 0, 4 * u:4 * u + 4].rearrange("p (b a) -> p b a", a=1).to_broadcast([128, 4, SLOTS]),
                                  ALU.mult).then_inc(tail_dve, 1)
                mark(("weights0", "weights")[u])
            for u in range(2):
                dve.wait_ge(tail_pe, 16 + u)
                dve.tensor_copy(rot[:, u, :], score[u][:]).then_inc(tail_dve, 1)
                mark(("wT0", "wT")[u])
            assert len(names) == OUT_READY, len(names)
            for b in range(B):
                dve.wait_ge(tail_pe, 18 + b)
                if b == 0:
                    dve.wait_ge(x_plus, 3 * B)
                dve.tensor_tensor(xs[:, b, :], ring[b % 4][:], xs[:, b, :], ALU.add).then_inc(tail_dve, 1)

        @block.gpsimd
        def _(pool):
            def low(dest_hi, dest_lo, n, slot):
                pool.wait_ge(w_hi, n)
                pool.tensor_tensor(dest_lo, raw[slot][:], dest_hi.bitcast(F32), ALU.subtract).then_inc(w_ready, 1)

            def rope_sin_of(layer, i, unit):
                pool.wait_ge(hi_done, hi_count(layer, i, unit))
                r = rot[:, unit[2], :].rearrange("p (b t) -> p b t", b=4)
                pool.tensor_tensor(r, r, table[:, 1:2, :].to_broadcast([128, 4, HD]), ALU.mult).then_inc(rope_sin, 1)

            def rope_low(layer, i, unit):
                hi, lo = destination(layer, unit)
                pool.wait_ge(rope_hi, rope_count(layer, i, unit))
                pool.tensor_tensor(lo, prod[:, unit[2], :], hi.bitcast(F32), ALU.subtract).then_inc(rope_ready, 1)

            def normalise(layer, i, j, u):
                p = probs[:, u, :].rearrange("p (b k) -> p b k", b=4)
                pool.wait_ge(rsum_ready, layer.soft(i, j, u))
                pool.tensor_tensor(p, p, rsum[:, u, :].rearrange("p (b a) -> p b a", a=1).to_broadcast([128, 4, S]),
                                   ALU.mult).then_inc(p_ready, 1)

            def combine(i, j, u, count):
                h = table[:, j:j + 1, :].to_broadcast([128, 4, S])
                if u == 0:
                    pool.wait_ge(bias_in[j], i * 16 + 16)
                if count is not None:
                    pool.wait_ge(masked_ready, count)
                pool.tensor_tensor(comb[:, u, :].rearrange("p (b k) -> p b k", b=4), neg[:, 4 * u:4 * u + 4, :], h,
                                   ALU.add).then_inc(comb_ready, 1)

            def attention(layer):
                for k, name in enumerate(layer.early):
                    n = layer.item_base + k
                    low(W[name][0][:], W[name][1][:], n + 1, SLOT[n])
                if layer is L0:
                    units = layer.first
                    for pair in (units[:2], units[2:]):
                        for k in range(3):
                            if k < 2:
                                rope_sin_of(layer, None, pair[k])
                            if k >= 1:
                                rope_low(layer, None, pair[k - 1])
                else:
                    for b in range(B):
                        pool.wait_ge(y_ready, 2 * B + b + 1)
                        pool.tensor_tensor(xs[:, b, :], xs[:, b, :], prod[:, b % 2, :], ALU.add).then_inc(x_plus, 1)
                    pool.wait_ge(neg_ready, 3)
                    combine(0, 0, 0, None)
                    combine(0, 0, 1, None)

                def item(i, last, name):
                    n, slot, _ = item_plan(layer, i, last, name)
                    d = W[DEST[name]]
                    low(d[0][:], d[1][:], n, slot)

                def body(i, last):
                    for j in range(layer.heads):
                        for unit in layer.steps(j, last):
                            if unit[0] == "N":
                                normalise(layer, i, *unit[1:])
                            elif is_rope(layer, unit):
                                rope_sin_of(layer, i, unit)
                            elif unit[0] == "A":
                                rope_low(layer, i, unit[1])
                            elif unit[0] == "C":
                                _, head, u = unit
                                combine(i + j, head, u, layer.soft(i, j, u))
                            elif unit[0] == "I":
                                item(i, last, unit[1])

                loop(pool, layer, body)

            pool.wait_ge(small_in, 48)
            attention(L0)
            dest = {"F0": "QA", "F1": "QB", "W3a": "KV", "W3b": "O", "F2": "QA", "F3": "QB"}
            for k, name in enumerate(FFN_ITEMS[:4]):
                low(W[dest[name]][0][:], W[dest[name]][1][:], FFN_ITEM + k + 1, SLOT[FFN_ITEM + k])
            pool.wait_ge(row_in, 16)
            for b in range(B):
                pool.wait_ge(y_ready, B + b + 1)
                pool.tensor_tensor(xs[:, b, :], xs[:, b, :], lnw[:], ALU.add).then_inc(x_plus, 1)
            for k, name in enumerate(FFN_ITEMS[4:]):
                low(W[dest[name]][0][:], W[dest[name]][1][:], FFN_ITEM + k + 5, SLOT[FFN_ITEM + k + 4])
            attention(L1)
            low(W["QA"][0][:], W["QA"][1][:], ITEMS, SLOT[TAIL_ITEM])
            for b in range(B):
                pool.wait_ge(y_ready, 3 * B + b + 1)
                pool.tensor_tensor(xs[:, b, :], xs[:, b, :], probs[:, b % 2, :], ALU.add).then_inc(x_plus, 1)


def kernel(**inputs):
    import numpy as np
    import concourse.bacc as bacc
    from concourse.bass_utils import run_bass_kernel_spmd

    a = {k: np.asarray(v) for k, v in inputs.items()}

    def by_head(w):
        n = w.shape[1] // HD
        return w.reshape(C, 128, n, HD).transpose(2, 1, 0, 3).reshape(n, 128, C * HD)

    def pairs(w, v):
        return np.concatenate([w, v], axis=-1)

    def wo_items(w):
        return w.reshape(-1, 2, HD, D).transpose(0, 2, 1, 3).reshape(-1, 128, 2 * D)

    def ordered(layer, tables):
        items = [tables[n][0] for n in layer.early]
        for i in range(layer.iters):
            for n in layer.items:
                if n[0] == "O":
                    items.append(tables[n][i])
                elif i + 1 < layer.iters:
                    items.append(tables[n][i + 1])
        return items

    items = []
    q, o = by_head(a["L0_xattn_wq"]), wo_items(a["L0_xattn_wo"])
    items += ordered(L0, {"KV": pairs(by_head(a["L0_xattn_wk"]), by_head(a["L0_xattn_wv"])), "QA": pairs(q[0::4], q[1::4]),
                          "QB": pairs(q[2::4], q[3::4]), "O0": o[0::2], "O1": o[1::2]})
    w12 = by_head(a["L0_ffn_w12"].T)
    ffn = {f"F{j}": pairs(w12[j], w12[FFN_J + j]) for j in range(FFN_J)}
    ffn["W3a"], ffn["W3b"] = wo_items(a["L0_ffn_w3"].T)
    items += [ffn[n] for n in FFN_ITEMS]
    qk = pairs(by_head(a["L1_xattn_w_q"].T), by_head(a["L1_xattn_w_k"].T))
    v = a["L1_xattn_w_v"].T.reshape(C, 128, L1.iters, L1.v_cols).transpose(2, 1, 0, 3).reshape(L1.iters, 128, C * L1.v_cols)
    items += ordered(L1, {"KV": v, "QA": qk[0::2], "QB": qk[1::2], "O0": wo_items(a["L1_xattn_w_out"].T)})

    def chunked(w):
        return w.reshape(C, 128, -1).transpose(1, 0, 2).reshape(128, -1)

    tail = np.concatenate([chunked(a["L1_ffn_Wq"].T), chunked(a["L1_ffn_Wu1"].T)], axis=1)
    items.append(np.concatenate([tail, np.zeros((128, ITEM - tail.shape[1]), np.float32)], axis=1))
    assert len(items) == ITEMS

    freq = (1.0 / 10000.0 ** (np.arange(0, HD, 2, dtype=np.float32) / HD)).astype(np.float32)
    angle = (np.arange(S, dtype=np.float32)[:, None] * freq[None, :]).T
    root = float(HD) ** -0.25
    cos, sin = np.cos(angle) * root, np.sin(angle) * root
    cos_sin = np.stack([np.concatenate([cos, cos]), np.concatenate([-sin, sin])], axis=1).astype(np.float32)

    arrays = {
        "x": a["x"],
        "ctx_t": a["ctx_4096"].reshape(T, D).T,
        "stream": np.concatenate(items, axis=0),
        "mask0": a["mask_BxSxS2_ff1"],
        "mask1": a["mask_BxSxS2_bk0"],
        "cos_sin": cos_sin,
        "ident_in": np.eye(128, dtype=np.float32),
        "position_bias": a["L1_xattn_position_bias"].reshape(-1, S),
        "ln_weight": a["L1_xattn_ln_weight"],
        "b12": a["L0_ffn_b12"].reshape(2 * FFN_J, 128).T,
        "b3": a["L0_ffn_b3"],
        "tail_wvd": chunked(a["L1_ffn_Wvd"].T).reshape(128, C, VB),
        "tail_auxv": chunked(a["L1_ffn_aux_values"].T).reshape(128, C, SLOTS),
        "tail_wvu": a["L1_ffn_Wvu"].T,
        "tail_keys": a["L1_ffn_aux_keys"].T,
        "tail_wr": a["L1_ffn_Wr"].T,
        "tail_logrel": a["L1_ffn_log_rel"],
        "tail_cols": np.stack([a["L1_ffn_bu1"], a["L1_ffn_Wu2"].reshape(128)], axis=1),
        "tail_scalars": np.concatenate([a[f"L1_ffn_{n}"].reshape(1) for n in ("gate_w1", "gate_bias", "bu2")]),
    }
    arrays = {k: np.ascontiguousarray(v) for k, v in arrays.items()}
    nc = bacc.Bacc("TRN2", target_bir_lowering=False, num_devices=1)
    args = {k: nc.dram_tensor(f"in_{k}", v.shape, mybir.dt.from_np(v.dtype), kind="ExternalInput").ap() for k, v in arrays.items()}
    out = nc.dram_tensor("out_0", (B, S, D), F32, kind="ExternalOutput").ap()
    xattn_ffn_kernel(nc, out=out, **args)
    got = run_bass_kernel_spmd(nc, [{f"in_{k}": v for k, v in arrays.items()}], core_ids=[0])
    return got.results[0]["out_0"]
```

```python
import concourse.bass as bass
from concourse import mybir
from contextlib import ExitStack

F32 = mybir.dt.float32
F32R = mybir.dt.float32r
ALU = mybir.AluOpType
ACT = mybir.ActivationFunctionType
AX = mybir.AxisListType

B = 8
S = 128
D = 512
C = D // 128
T = B * S
HALF = 512
HD = 128
EPS = 1e-5
EXP_MAX = 80.0
MASKED = -1e30
SLOTS = 128
BOT = 64
RDIM = 48
VB = 32
ITEM = 1024


class Layer:

    def __init__(self, name, iters, heads, shared_kv, ring_base, soft_base, item_base, slots):
        self.name, self.iters, self.heads, self.shared_kv = name, iters, heads, shared_kv
        self.rope = shared_kv
        self.v_cols = HD if shared_kv else heads * HD
        self.v_units = B * self.v_cols // HALF
        self.first = [("K", 0, 0), ("K", 0, 1), ("Q", 0, 0), ("Q", 0, 1)]
        self.ring_base = ring_base
        self.items = ["O0", "QA", "KV", "QB", "O1"] if shared_kv else ["QA", "O0", "KV", "QB"]
        self.early = ["KV", "QA", "QB"] if shared_kv else ["QA", "QB", "KV"]
        self.units = [e for j in range(heads) for e in self.steps(j, False) if e[0] in ("K", "Q", "V", "O", "PV")]
        self.high = [e for e in self.units if e[0] != "O" and not (shared_kv and e[0] == "V")]
        self.loop_ring = ring_base + len(self.first)
        self.ring_end = self.loop_ring + len(self.units) * iters - len(self.first)
        self.soft_base = soft_base
        self.soft_end = soft_base + 2 * heads * iters
        self.slots = slots
        self.item_base = item_base
        self.loop_item = item_base + len(self.early)
        self.item_end = self.loop_item + len(self.items) * iters - len(self.early)

    def steps(self, j, last):
        k, q = [("K", j + 1, u) for u in range(2)], [("Q", j + 1, u) for u in range(2)]
        k_next, q_next = ([], []) if last else (self.first[:2], self.first[2:])
        v = [("V", 0, n) for n in range(self.v_units)]
        w = [("W", 0, n) for n in range(2)]
        s, m, e, n = ([[(kind, j, u)] for u in range(2)] for kind in "SMEN")
        low = [("L", j - 1, u) for u in range(2) if self.shared_kv and j >= 1]
        t = [("T", j, u) for u in range(2)]
        pv = [[("PV", p, n) for n in range(4)] for p in range(2)]
        o = [[("O", p, b) for b in range(B)] for p in range(self.heads // 2)]
        item = {n: [] if last and n[0] != "O" else [("I", n, 0)] for n in self.items}
        if self.shared_kv:
            d, a, h = ([(kind, n, 0) for n in (k_next + q_next if j == 3 else q)] for kind in "DAH")
            scores = s[0] + m[0] + s[1] + m[1] + low
            if j < 3:
                before = (item["O0"], item["QA"], item["KV"])[j]
                after = (v[:1], v[1:], pv[0])[j]
                return (before + scores + e[0] + n[0] + q[:1] + d[:1] + w[max(j - 1, 0):j] + e[1] + n[1] + a[:1]
                        + q[1:] + d[1:] + h[:1] + a[1:] + h[1:] + after + t)
            return (item["QB"] + scores + o[0][:2] + e[0] + n[0] + o[0][2:3] + e[1] + n[1] + o[0][3:]
                    + item["O1"] + t + k_next[:1] + d[:1] + k_next[1:] + d[1:2] + a[:1] + h[:1]
                    + q_next[:1] + d[2:3] + pv[1][:2] + a[1:2] + h[1:2] + pv[1][2:] + a[2:3] + h[2:3]
                    + q_next[1:] + d[3:] + o[1][:2] + a[3:] + h[3:] + o[1][2:])
        c = [] if last and j == 1 else [("C", 1 - j, u) for u in range(2)]
        first, second = s[0] + m[0] + e[0] + n[0] + m[1], s[1] + e[1] + n[1] + c
        if j == 0:
            return (first + v[:1] + second + v[1:2] + t[:1] + v[2:3] + t[1:] + item["QA"] + v[3:] + k[:1] + item["O0"]
                    + k[1:] + pv[0][:2] + q[:1] + pv[0][2:] + q[1:])
        return (first + k_next[:1] + second + k_next[1:] + t[:1] + q_next[:1] + t[1:] + item["KV"] + pv[1][:2] + q_next[1:]
                + pv[1][2:] + item["QB"] + o[0])

    def ring(self, i, unit, back=0):
        k = self.units.index(unit)
        if isinstance(i, int) and i == self.iters - 1:
            k -= len([n for n in self.units[:k] if n in self.first])
        return (i - back) * len(self.units) + (self.loop_ring + k + 1)

    def bank(self, unit, i=0):
        k = self.units.index(unit)
        return (self.loop_ring + k) % 4

    def soft(self, i, j, u):
        return i * (2 * self.heads) + (self.soft_base + 2 * j + u + 1)

    def item(self, i, name, back=0):
        at = self.items.index(name)
        if isinstance(i, int) and i == self.iters - 1:
            at = [n for n in self.items if n[0] == "O"].index(name)
        return (i - back) * len(self.items) + (self.loop_item + at + 1)


L0 = Layer("L0", 8, 4, True, 0, 0, 0, [2, 0, 1, 2, 0])
FFN_ITEMS = ["F0", "F1", "W3a", "W3b", "F2", "F3"]
FFN_ITEM = L0.item_end
FFN_RING = L0.ring_end
FFN_J = 4
X_UNITS = [(f"X{n}", j, u) for j in range(FFN_J) for u in range(2) for n in (1, 2)]
Y_RING = FFN_RING + len(X_UNITS) + 2
L1 = Layer("L1", 16, 2, False, Y_RING + B - 2, L0.soft_end, FFN_ITEM + len(FFN_ITEMS), [1, 0, 1, 0])
TAIL_ITEM = L1.item_end
TAIL_RING = L1.ring_end
ITEMS = TAIL_ITEM + 1
assert FFN_RING % 4 == 0 and L1.ring_base % 4 == 0 and len(L0.units) % 4 == 0 and len(L1.units) % 4 == 0


def slot_plan():
    slot = [0, 1, 0] + L0.slots * (L0.iters - 1) + [2, 1]
    slot += [0, 1] * (len(FFN_ITEMS) // 2)
    slot += [0, 1, 0] + L1.slots * (L1.iters - 1) + [1]
    return slot + [0]


SLOT = slot_plan()


def loads(n):
    return sum(1 for s in SLOT[:n + 1] if s == SLOT[n])


assert len(SLOT) == ITEMS and all(SLOT[n] != SLOT[n - 1] for n in range(1, ITEMS))
ROPE_ITER = len([n for n in L0.units if n[0] in "KQ"])
ROPE_ALL = len([n for n in L0.units if n[0] in "KQ"]) * L0.iters


def numbered(names):
    return {name: n + 1 for n, name in enumerate(names)}


def of_half(u, *names):
    return [f"{name}{b}" for name in names for b in range(4 * u, 4 * u + 4)]


TP = numbered(["vd", "rk", "gmat", "query0", "up0", "rq0", "up1", "router0", "attn0", "query1", "rq1", "router1", "attn1",
               "logsum", "turned0"] + of_half(0, "out") + ["learned", "turned1"] + of_half(1, "out"))
TA = numbered(["gmat", "query0", "v0", "rq0", "log", "e0", "v1", "query1", "rq1", "e1"]
              + of_half(0, "exp") + ["wT0"] + of_half(1, "exp") + ["learned", "gate"])
TO = numbered(["sq0", "cubic0", "plus0", "sq1", "cubic1", "gelu0", "plus1", "gelu1"])
TAIL_STEPS = (["vd", "rk", "var1", "poly0", "inner0", "router0"] + of_half(0, "max", "replace")
              + ["unselected0", "attn0", "selected0", "amax0", "poly1", "sig0", "logsum", "inner1", "router1"]
              + of_half(1, "max") + ["sig1"] + of_half(1, "replace")
              + ["unselected1", "attn1", "selected1", "amax1", "mean", "imean", "half_norm", "learned",
                 "l1", "l2", "l3", "l4", "l5", "l6", "l7", "gate_in", "isum", "wT1", "g1", "g2", "gate", "scale"])
TD = numbered(TAIL_STEPS)
OUT_READY = len(TAIL_STEPS)


def xattn_ffn_kernel(nc, x, ctx_t, stream, mask0, mask1, cos_sin, ident_in, position_bias, ln_weight, b12, b3,
                     tail_wvd, tail_auxv, tail_wvu, tail_keys, tail_wr, tail_logrel, tail_cols, tail_scalars, out):
    es = ExitStack()
    with es:
        def sb(name, shape, dt=F32):
            return es.enter_context(nc.sbuf_tensor(name, shape, dt))

        def sem(name):
            return es.enter_context(nc.semaphore(name))

        cT = [sb(f"cT_{p}", [128, C, T], F32R) for p in ("hi", "lo")]
        xT = [sb(f"xT_{p}", [128, C, T], F32R) for p in ("hi", "lo")]
        PVO_BOTH = sb("PVO", [128, 2, 5 * T], F32R)
        PVO = [PVO_BOTH[:, p, :] for p in range(2)]
        VO = [t[:, T:5 * T] for t in PVO]
        PT = [[t[:, 2 * T * h:2 * T * h + T].rearrange("p (u n) -> p u n", u=2) for t in PVO] for h in range(2)]
        PT_PAIR = [t[:, 0:4 * T].rearrange("p (h n) -> p h n", h=2) for t in PVO]
        OT = [v[:, 2 * T:4 * T].rearrange("p (h t) -> p h t", h=2) for v in VO]
        GT = [v[:, :].rearrange("p (j t) -> p j t", j=4) for v in VO]
        W = {n: [sb(f"w{n}_{p}", [128, ITEM], F32R) for p in ("hi", "lo")] for n in ("QA", "QB", "KV", "O")}
        QT = [sb(f"QT_{p}", [128, T], F32R) for p in ("hi", "lo")]
        KT_BOTH = sb("KT", [128, 2, T], F32R)
        KT = [KT_BOTH[:, p, :] for p in range(2)]
        raw = [sb(f"raw{n}", [128, ITEM]) for n in range(3)]
        xs = sb("xs", [128, B, D])
        neg = sb("neg", [128, B, S])
        probs = sb("probs", [128, 2, HALF])
        rot = sb("rot", [128, 2, HALF])
        prod = sb("prod", [128, 2, HALF])
        table = sb("table", [128, 2, HD])
        comb = rot
        rows = sb("rows", [128, 2, HALF])
        vtmp = rows[:, 0, :]
        ctx_raw = [t[:].rearrange("p a n -> p (a n)") for t in (rot, prod, neg)] + [raw[2][:]]
        lnw = sb("lnw", [128, D])
        ident = sb("ident", [128, 128])
        nmax = sb("nmax", [128, 2, 4])
        ssum = sb("ssum", [128, 2, 4])
        sinv = sb("sinv", [128, 2, 4])
        rsum = sb("rsum", [128, 2, 4])
        stats = sb("stats", [128, B, 6])
        mv = sb("mv", [128, B, 2])
        ve = sb("ve", [128, B])
        sd = sb("sd", [128, B])
        rstd = sb("rstd", [128, B])
        msq = sb("msq", [128, B])
        rrms = sb("rrms", [128, B])
        bcol = sb("bcol", [128, 2 * FFN_J])
        logrel = sb("logrel", [128, SLOTS])
        tcols = sb("tcols", [128, 2])
        tsc = sb("tsc", [128, 3])
        keys = sb("keys", [BOT, SLOTS])
        wr = sb("wr", [BOT, RDIM])
        rk = sb("rk", [RDIM, SLOTS])
        top = sb("top", [128, B, 8])
        col = sb("col", [128, 12, B])
        auxv = raw[2][:, 0:HALF].rearrange("p (c n) -> p c n", c=C)
        wvd = sb("wvd", [128, C, VB])
        wvu = raw[2][0:VB, HALF:2 * HALF]
        vd = wvd[0:VB].rearrange("p c n -> p (c n)")
        gmat = lnw[:]
        query = neg[:].rearrange("p b s -> p (b s)")
        rq = raw[0][:]
        expT = neg[:].rearrange("p b s -> p (b s)")
        hidden = prod
        allones = sb("allones", [128, 128])

        ring = [es.enter_context(nc.psum_tensor(f"ring{n}", [128, HALF], F32)) for n in range(4)]
        score_both = es.enter_context(nc.psum_tensor("scores", [128, 2 * HALF], F32))
        score = [score_both[:, n * HALF:(n + 1) * HALF] for n in range(2)]
        turned = [es.enter_context(nc.psum_tensor(f"turned{n}", [128, HALF], F32)) for n in range(2)]

        x_in = [sem(f"x_in{h}") for h in range(2)]
        small_in = sem("small_in")
        raw_in = [sem(f"raw_in{n}") for n in range(3)]
        w_hi = sem("w_hi")
        w_ready = sem("w_ready")
        ring_filled = sem("ring_filled")
        hi_done = sem("hi_done")
        ring_freed = sem("ring_freed")
        rope_sin = sem("rope_sin")
        rope_sum = sem("rope_sum")
        rope_hi = sem("rope_hi")
        rope_ready = sem("rope_ready")
        s_filled = sem("s_filled")
        half_masked = sem("half_masked")
        masked_ready = sem("masked_ready")
        max_ready = sem("max_ready")
        exp_done = sem("exp_done")
        inv_ready = sem("inv_ready")
        rsum_ready = sem("rsum_ready")
        p_ready = sem("p_ready")
        t_filled = sem("t_filled")
        pt_hi = sem("pt_hi")
        pt_ready = sem("pt_ready")
        share_in = sem("share_in")
        pv_ready = sem("pv_ready")
        v_turned = sem("v_turned")
        v_hi = sem("v_hi")
        v_ready = sem("v_ready")
        ctx_in = [sem(f"ctx_in{c}") for c in range(C)]
        ctx_hi = sem("ctx_hi")
        ctx_ready = sem("ctx_ready")
        bias_in = [sem("bias_in_a"), sem("bias_in_b")]
        comb_ready = sem("comb_ready")
        neg_ready = sem("neg_ready")
        mask_in = sem("mask_in")
        ln_step = sem("ln_step")
        ln_var = sem("ln_var")
        ln_sqrt = sem("ln_sqrt")
        ln_ms = sem("ln_ms")
        ln_rms = sem("ln_rms")
        y_ready = sem("y_ready")
        y_turned = sem("y_turned")
        y_hi = sem("y_hi")
        y_lo = sem("y_lo")
        x_plus = sem("x_plus")
        row_in = sem("row_in")
        gate_plus = sem("gate_plus")
        gate_inv = sem("gate_inv")
        x2_in = sem("x2_in")
        g_prod = sem("g_prod")
        g_pre = sem("g_pre")
        gate_exp = sem("gate_exp")
        g_hi = sem("g_hi")
        g_lo = sem("g_lo")
        tail_in = sem("tail_in")
        tail_pe = sem("tail_pe")
        tail_act = sem("tail_act")
        tail_dve = sem("tail_dve")
        tail_pool = sem("tail_pool")
        out_done = sem("out_done")

        def both(pair, fn):
            return [fn(t) for t in pair]

        PARTS = ((0, 0), (0, 1), (1, 0))

        def weights_of(layer, kind, j):
            if layer.shared_kv:
                name, half = ("KV", "KV".index(kind)) if kind in "KV" else (("QA", "QB")[j // 2], j % 2)
            else:
                name, half = ("QA", "QB")[j], 0 if kind == "Q" else 1
            return [w[:, half * HALF:(half + 1) * HALF].rearrange("p (c d) -> p c d", c=C) for w in W[name]]

        def item_of(layer, kind, j):
            if layer.shared_kv:
                return "KV" if kind in "KV" else ("QA", "QB")[j // 2]
            return ("QA", "QB")[j]

        def values(layer, part):
            return VO[part][:, 0:B * layer.v_cols].rearrange("p (b n) -> p b n", b=B)

        def destination(layer, unit):
            kind, j, u = unit
            if kind == "Q":
                return both(QT, lambda t: t[:, u * HALF:(u + 1) * HALF])
            if kind == "K":
                return both(KT, lambda t: t[:, u * HALF:(u + 1) * HALF])
            if kind == "V":
                return both(VO, lambda t: t[:, u * HALF:(u + 1) * HALF])
            if layer.shared_kv:
                return both(OT, lambda t: t[:, :, u * 2 * S:(u + 1) * 2 * S].rearrange("p h (b q) -> p b h q", b=2))
            return both(OT, lambda t: t[:, j, u * 2 * S:(u + 1) * 2 * S])

        def as_destination(layer, unit, bank):
            if layer.shared_kv and unit[0] == "PV":
                return bank[:].rearrange("p (b h q) -> p b h q", b=2, h=2)
            return bank[:]

        def turned_to(layer, j):
            return PT[j % 2 if layer.shared_kv else 0]

        def rope_count(layer, i, unit):
            order = [n for n in layer.units if n[0] in "KQ"]
            if i is None:
                return layer.first.index(unit) + 1
            return i * len(order) + (len(layer.first) + order.index(unit) + 1)

        def hi_count(layer, i, unit):
            order = layer.high
            base = 0 if layer is L0 else HI_L1
            if i is None:
                return base + layer.first.index(unit) + 1
            k = order.index(unit)
            if isinstance(i, int) and i == layer.iters - 1:
                k -= len([n for n in order[:k] if n in layer.first])
            return i * len(order) + (base + len(layer.first) + k + 1)

        HI_L1 = len(L0.high) * L0.iters

        def ring_count(layer, i, unit):
            if i is None:
                return layer.ring_base + layer.first.index(unit) + 1 - (B if layer is L1 and unit[0] == "K" else 0)
            return layer.ring(i, unit)

        def ring_bank(layer, i, unit):
            if i is None:
                return (ring_count(layer, i, unit) - 1) % 4
            if isinstance(i, int):
                return (layer.ring(i, unit) - 1) % 4
            return layer.bank(unit)

        def is_rope(layer, unit):
            return layer.rope and unit[0] in "KQ"

        DEST = {"KV": "KV", "QA": "QA", "QB": "QB", "O0": "O", "O1": "O"}

        def freed_by(layer, i, name):
            if name == "KV":
                return layer.ring(i, ("V", 0, layer.v_units - 1))
            if layer.shared_kv:
                if name == "QA":
                    return layer.ring(i, ("Q", 1, 1))
                if name == "QB":
                    return layer.ring(i, ("Q", 3, 1))
                if name == "O1":
                    return layer.ring(i, ("O", 0, B - 1))
                return layer.ring(i, ("O", 1, B - 1), back=1) if not isinstance(i, int) else layer.ring(i - 1, ("O", 1, B - 1))
            if name == "QA":
                return i * len(layer.units) + layer.loop_ring
            if name == "QB":
                return layer.ring(i, ("Q", 1, 1))
            return layer.ring(i, ("O", 0, B - 1), back=1) if not isinstance(i, int) else layer.ring(i - 1, ("O", 0, B - 1))

        def item_plan(layer, i, last, name):
            n = layer.item(i, name)
            if isinstance(n, int):
                return n, SLOT[n - 1], 16 * loads(n - 1)
            k = layer.items.index(name)
            slot = layer.slots[k]
            each = layer.slots.count(slot)
            return n, slot, i * (16 * each) + 16 * loads(layer.loop_item + k)

        def loop(eng, layer, body):
            with eng.Fori(0, layer.iters - 1) as i:
                body(i, False)
            body(layer.iters - 1, True)

        def x_bank(n):
            return (ring + score + turned)[n % 8]

        def row_of(b):
            buf = probs if b % 4 < 2 else rows
            return buf[:, b % 2, :], (turned + score)[b % 4]

        OUT_BANKS = [ring[2], ring[3], turned[0], score[0], ring[0], ring[1], turned[1], score[1]]
        EARLY_BANKS = [(Y_RING + B + n) % 4 for n in (2, 3)]

        def pv_count(i, unit):
            return i * 8 + (4 * unit[1] + unit[2] + 1)

        def share_sum(unit):
            return rows[:, unit[2] // 2, unit[2] % 2 * 2 * S:(unit[2] % 2 + 1) * 2 * S].rearrange("p (b q) -> p b q", b=2)

        def shares(i, unit):
            return ring[ring_bank(L1, i, unit)][:].rearrange("p (b e q) -> p b e q", b=2, e=2)

        def gate_of(k):
            return (rot, probs)[k // 2 % 2][:, k % 2, :]

        block = es.enter_context(nc.Block())

        @block.sync
        def _(sp):
            def load(n):
                if n >= 2:
                    sp.wait_ge(w_ready, n - 1)
                sp.dma_start(raw[SLOT[n]][:], stream[n * 128:(n + 1) * 128, :]).then_inc(raw_in[SLOT[n]], 16)

            def layer_loads(layer):
                def body(i, last):
                    for name in layer.items:
                        if last and name[0] != "O":
                            continue
                        if not layer.shared_kv and name == "QA":
                            sp.wait_ge(comb_ready, i * 4 + 2)
                            sp.dma_start(table[:, 0, :], position_bias[bass.ds(i * (2 * S) + 2 * S, S), :]).then_inc(bias_in[0], 16)
                        if not layer.shared_kv and name == "KV":
                            sp.wait_ge(comb_ready, i * 4 + 4)
                            sp.dma_start(table[:, 1, :], position_bias[bass.ds(i * (2 * S) + 3 * S, S), :]).then_inc(bias_in[1], 16)
                        n, slot, _ = item_plan(layer, i, last, name)
                        sp.wait_ge(w_ready, n - 2)
                        sp.dma_start(raw[slot][:], stream[bass.ds(n * 128 - 128, 128), :]).then_inc(raw_in[slot], 16)

                if layer is L0:
                    sp.wait_ge(ctx_ready, C)
                loop(sp, layer, body)

            for h in range(2):
                sp.dma_start(xs[:, 4 * h:4 * h + 4, :], x[4 * h:4 * h + 4].rearrange("b t d -> t b d")).then_inc(x_in[h], 16)
                if h == 0:
                    load(0)
                    for c in range(C):
                        sp.dma_start(ctx_raw[c], ctx_t[c * 128:(c + 1) * 128, :]).then_inc(ctx_in[c], 16)
                    load(1)
            load(2)
            sp.wait_ge(ctx_ready, C)
            sp.dma_start(neg[:], mask0.rearrange("b q k -> q b k")).then_inc(mask_in, 16)
            sp.dma_start(bcol[:], b12).then_inc(small_in, 16)
            sp.dma_start(lnw[:], b3.partition_broadcast(128)).then_inc(row_in, 16)
            sp.dma_start(logrel[:], tail_logrel.partition_broadcast(128)).then_inc(tail_in, 16)
            sp.dma_start(tcols[:], tail_cols).then_inc(tail_in, 16)
            sp.dma_start(tsc[:], tail_scalars.partition_broadcast(128)).then_inc(tail_in, 16)
            sp.dma_start(keys[:], tail_keys).then_inc(tail_in, 16)
            sp.dma_start(wr[:], tail_wr).then_inc(tail_in, 16)
            sp.dma_start(wvd[:], tail_wvd).then_inc(tail_in, 16)
            layer_loads(L0)
            for n in range(FFN_ITEM, FFN_ITEM + len(FFN_ITEMS)):
                load(n)
            sp.dma_start(raw[2][:, 0:B * S // 4].bitcast(mybir.dt.uint8).rearrange("p (b k) -> p b k", b=B),
                         mask1.rearrange("b q k -> q b k")).then_inc(mask_in, 16)
            sp.wait_ge(rope_ready, ROPE_ALL)
            for j in range(2):
                sp.dma_start(table[:, j, :], position_bias[j * S:(j + 1) * S, :]).then_inc(bias_in[j], 16)
            load(L1.item_base)
            sp.wait_ge(x_plus, B)
            sp.dma_start(lnw[:], ln_weight.partition_broadcast(128)).then_inc(row_in, 16)
            sp.wait_ge(neg_ready, 3)
            sp.dma_start(auxv, tail_auxv).then_inc(tail_in, 16)
            sp.dma_start(wvu, tail_wvu).then_inc(tail_in, 16)
            load(L1.item_base + 1)
            load(L1.item_base + 2)
            layer_loads(L1)
            load(TAIL_ITEM)
            for b in range(B):
                sp.wait_ge(tail_dve, OUT_READY + b + 1)
                sp.dma_start(out[b], xs[:, b, :]).then_inc(out_done, 16)
            sp.wait_ge(out_done, 16 * B)

        @block.scalar
        def _(act):
            act.dma_start(ident[:], ident_in).then_inc(small_in, 16)
            act.dma_start(table[:], cos_sin).then_inc(small_in, 16)

            def high(dest, n, slot, count):
                act.wait_ge(raw_in[slot], count)
                act.activation(dest, raw[slot][:], ACT.Copy).then_inc(w_hi, 1)

            def roots(stage, h):
                hs = slice(4 * h, 4 * h + 4)
                act.wait_ge(ln_var, 2 * stage + h + 1)
                act.activation(sd[:, hs], ve[:, hs], ACT.Sqrt).then_inc(ln_sqrt, 1)
                if stage == 2:
                    act.wait_ge(ln_ms, h + 1)
                    act.activation(msq[:, hs], msq[:, hs], ACT.Sqrt).then_inc(ln_rms, 1)

            def rows_high(stage, batches):
                for b in batches:
                    act.wait_ge(y_turned, stage * B + b + 1)
                    act.activation(xT[0][:, :, b * S:(b + 1) * S],
                                   row_of(b)[1][:].rearrange("p (c t) -> p c t", c=C), ACT.Copy).then_inc(y_hi, 1)

            def evacuate(layer, i, unit):
                act.wait_ge(ring_filled, ring_count(layer, i, unit))
                bank = ring[ring_bank(layer, i, unit)]
                if is_rope(layer, unit):
                    n = rope_count(layer, i, unit)
                    if not isinstance(n, int) or n > 2:
                        act.wait_ge(rope_sum, n - 2)
                    buf = rot[:, unit[2], :]
                    act.activation(buf[0:64, :], bank[64:128, :], ACT.Copy)
                    act.activation(buf[64:128, :], bank[0:64, :], ACT.Copy).then_inc(hi_done, 1)
                else:
                    act.activation(destination(layer, unit)[0], as_destination(layer, unit, bank), ACT.Copy).then_inc(hi_done, 1)

            def share_copy(i, unit):
                act.wait_ge(ring_filled, ring_count(L1, i, unit))
                act.activation(share_sum(unit), shares(i, unit)[:, :, 0, :], ACT.Copy).then_inc(share_in, 1)

            def share_high(i, unit):
                act.wait_ge(ring_freed, ring_count(L1, i, unit))
                hi = destination(L1, unit)[0].rearrange("p (b q) -> p b q", b=2)
                act.activation(hi, share_sum(unit), ACT.Copy).then_inc(hi_done, 1)

            def exponentials(layer, i, j, u):
                act.wait_ge(max_ready, layer.soft(i, j, u))
                for t in range(4):
                    p = probs[:, u, t * S:(t + 1) * S]
                    ins = act.activation(p, p, ACT.Exp, bias=nmax[:, u, t:t + 1], accum_out=ssum[:, u, t:t + 1])
                ins.then_inc(exp_done, 1)

            def values_high(layer, i, n):
                act.wait_ge(v_turned, i * 2 + n + 1)
                act.activation(VO[0][:, n * HALF:(n + 1) * HALF], turned[0][:], ACT.Copy).then_inc(v_hi, 1)

            def turned_high(layer, i, j, u):
                act.wait_ge(t_filled, layer.soft(i, j, u))
                act.activation(turned_to(layer, j)[0][:, u, :], turned[u][:], ACT.Copy).then_inc(pt_hi, 1)

            def attention(layer):
                def item(i, last, name):
                    n, slot, count = item_plan(layer, i, last, name)
                    act.wait_ge(ring_filled, freed_by(layer, i, name))
                    high(W[DEST[name]][0][:], n, slot, count)

                def body(i, last):
                    for j in range(layer.heads):
                        for unit in layer.steps(j, last):
                            if unit[0] == "E":
                                exponentials(layer, i, *unit[1:])
                            elif unit[0] == "T":
                                turned_high(layer, i, *unit[1:])
                            elif unit[0] == "W":
                                values_high(layer, i, unit[2])
                            elif unit[0] == "I":
                                item(i, last, unit[1])
                            elif layer is L1 and unit[0] == "PV":
                                share_copy(i, unit)
                                if unit[2] % 2 == 1:
                                    share_high(i, ("PV", unit[1], unit[2] - 1))
                                    share_high(i, unit)
                            elif unit in layer.high:
                                evacuate(layer, i, unit)

                loop(act, layer, body)

            def context_high(c):
                act.wait_ge(ctx_in[c], 16)
                act.activation(cT[0][:, c, :], ctx_raw[c], ACT.Copy).then_inc(ctx_hi, 1)

            def early(layer, name, read=None):
                n = layer.item_base + layer.early.index(name)
                if read is not None:
                    act.wait_ge(ring_filled, read)
                high(W[name][0][:], n + 1, SLOT[n], 16 * loads(n))

            early(L0, "KV")
            roots(0, 0)
            context_high(0)
            rows_high(0, (0, 1))
            context_high(1)
            rows_high(0, (2, 3))
            context_high(2)
            context_high(3)
            early(L0, "QA")
            roots(0, 1)
            evacuate(L0, None, L0.first[0])
            evacuate(L0, None, L0.first[1])
            rows_high(0, range(4, B))
            evacuate(L0, None, L0.first[2])
            early(L0, "QB")
            evacuate(L0, None, L0.first[3])
            attention(L0)

            free = {"F0": L0.ring(7, ("Q", 1, 1)), "F1": L0.ring(7, ("Q", 3, 1)), "W3a": L0.ring(7, ("V", 0, 1)),
                    "W3b": L0.ring(7, ("O", 1, B - 1)), "F2": FFN_RING + 4, "F3": FFN_RING + 8}
            dest = {"F0": "QA", "F1": "QB", "W3a": "KV", "W3b": "O", "F2": "QA", "F3": "QB"}

            def ffn_item(name):
                n = FFN_ITEM + FFN_ITEMS.index(name)
                act.wait_ge(ring_filled, free[name])
                high(W[dest[name]][0][:], n + 1, SLOT[n], 16 * loads(n))

            def gate(k):
                act.wait_ge(g_pre, k + 1)
                act.activation(gate_of(k), gate_of(k), ACT.Exp, scale=-1.0).then_inc(gate_exp, 1)

            ffn_item("F0")
            ffn_item("F1")
            roots(1, 0)
            ffn_item("W3a")
            rows_high(1, range(4))
            roots(1, 1)
            ffn_item("W3b")
            act.wait_ge(small_in, 48)
            gate(0)
            rows_high(1, range(4, B))
            for k in range(2 * FFN_J):
                j, u = k // 2, k % 2
                act.wait_ge(ring_filled, FFN_RING + 2 * k + 2)
                if k >= 2:
                    act.wait_ge(g_lo, k - 1)
                act.activation(prod[:, u, :], x_bank(2 * k + 1)[:], ACT.Identity,
                               bias=bcol[:, FFN_J + j:FFN_J + j + 1]).then_inc(x2_in, 1)
                if k in (1, 3):
                    ffn_item(("F2", "F3")[k // 2])
                elif k == 5:
                    early(L1, "QA", FFN_RING + 12)
                if k + 1 < 2 * FFN_J:
                    gate(k + 1)
                else:
                    for unit in L1.first[:2]:
                        evacuate(L1, None, unit)
                act.wait_ge(g_prod, k + 1)
                act.activation(GT[0][:, j, u * HALF:(u + 1) * HALF], prod[:, u, :], ACT.Copy).then_inc(g_hi, 1)
            early(L1, "QB", FFN_RING + 16)
            roots(2, 0)
            rows_high(2, range(4))
            roots(2, 1)
            early(L1, "KV", Y_RING + B)
            evacuate(L1, None, L1.first[2])
            rows_high(2, range(4, B))
            evacuate(L1, None, L1.first[3])
            attention(L1)

            act.wait_ge(ring_filled, L1.ring(L1.iters - 1, ("V", 0, 0)))
            high(W["QA"][0][:], ITEMS, SLOT[TAIL_ITEM], 16 * loads(TAIL_ITEM))
            roots(3, 0)

            def out_of(name, dest, src, shift=None):
                act.wait_ge(tail_pe, TP[name])
                if shift is None:
                    act.activation(dest, src, ACT.Copy).then_inc(tail_act, 1)
                else:
                    act.activation(dest, src, ACT.Identity, bias=shift).then_inc(tail_act, 1)

            def halves(u):
                return slice(u * HALF, (u + 1) * HALF)

            def hidden_exp(u):
                act.wait_ge(tail_dve, TD[f"inner{u}"])
                act.activation(rot[:, u, :], rot[:, u, :], ACT.Exp, scale=-2.0 * (2.0 / 3.141592653589793) ** 0.5).then_inc(tail_act, 1)

            rows_high(3, range(4))
            roots(3, 1)
            out_of("gmat", gmat, ring[3][:])
            out_of("query0", query[0:BOT, halves(0)], ring[0][0:BOT, :])
            rows_high(3, range(4, B))
            out_of("up0", hidden[:, 0, :], ring[1][:], tcols[:, 0:1])
            out_of("rq0", rq[0:RDIM, halves(0)], ring[2][0:RDIM, :])
            act.wait_ge(tail_dve, TD["var1"])
            act.activation(col[:, 1, :], col[:, 0, :], ACT.Ln).then_inc(tail_act, 1)
            hidden_exp(0)
            out_of("up1", hidden[:, 1, :], turned[0][:], tcols[:, 0:1])
            out_of("query1", query[0:BOT, halves(1)], ring[0][0:BOT, :])
            out_of("rq1", rq[0:RDIM, halves(1)], ring[2][0:RDIM, :])
            hidden_exp(1)
            for b in range(B):
                if b % 4 == 0:
                    act.wait_ge(tail_dve, TD[f"amax{b // 4}"])
                p = raw[1][:, b * S:(b + 1) * S]
                act.activation(p, p, ACT.Exp, bias=col[:, 10, b:b + 1], accum_out=col[:, 11, b:b + 1]).then_inc(tail_act, 1)
                if b == 3:
                    out_of("turned0", expT[:, halves(0)], score[0][:])
            act.wait_ge(tail_dve, TD["learned"])
            act.activation(col[:, 4, :], col[:, 3, :], ACT.Exp, scale=-1.0).then_inc(tail_act, 1)
            act.wait_ge(tail_dve, TD["gate_in"])
            act.activation(col[:, 8, :], col[:, 7, :], ACT.Exp, scale=-1.0).then_inc(tail_act, 1)

        @block.tensor
        def _(pe):
            def ring_wait(n):
                if isinstance(n, int) and n <= 4:
                    return
                pe.wait_ge(ring_freed, n - 4)

            def project(layer, i, unit):
                kind, j, u = unit
                if layer is L1 and i is None and kind == "K":
                    pe.wait_ge(ring_freed, FFN_RING + 10)
                else:
                    ring_wait(ring_count(layer, i, unit))
                bank = ring[ring_bank(layer, i, unit)]
                w = weights_of(layer, kind, j)
                src = xT if kind == "Q" else cT
                for c in range(C):
                    if layer is L0 and i is None and unit == layer.first[0]:
                        pe.wait_ge(ctx_ready, c + 1)
                    for k, (a, b) in enumerate(PARTS):
                        mm = pe.matmul(bank[:], w[a][:, c, :], src[b][:, c, u * HALF:(u + 1) * HALF],
                                       start=(c == 0 and k == 0), stop=(c == C - 1 and k == 2))
                mm.then_inc(ring_filled, 1)

            def project_values(layer, i, unit):
                ring_wait(ring_count(layer, i, unit))
                bank = ring[ring_bank(layer, i, unit)]
                n = layer.v_cols
                per = HALF // n
                w = both(W["KV"], lambda t: t[:].rearrange("p (c d) -> p c d", c=C))
                for r in range(per):
                    b = unit[2] * per + r
                    for c in range(C):
                        for k, (a, e) in enumerate(PARTS):
                            mm = pe.matmul(bank[:, r * n:(r + 1) * n], cT[a][:, c, b * S:(b + 1) * S], w[e][:, c, :],
                                           start=(c == 0 and k == 0), stop=(c == C - 1 and k == 2))
                mm.then_inc(ring_filled, 1)

            def output(layer, i, unit):
                _, pair, b = unit
                n = ring_count(layer, i, unit)
                ring_wait(n)
                bank = ring[ring_bank(layer, i, unit)]
                for h in range(2):
                    for k, (a, e) in enumerate(PARTS):
                        mm = pe.matmul(bank[:], OT[a][:, h, b * S:(b + 1) * S], W["O"][e][:, h * D:(h + 1) * D],
                                       start=(h == 0 and k == 0), stop=(h == 1 and k == 2))
                mm.then_inc(ring_filled, 1)

            def scores(layer, i, j, u):
                unit = ("Q", j, u)
                if layer.rope and j > 0:
                    pe.wait_ge(rope_ready, rope_count(layer, i, unit))
                elif layer.rope:
                    pe.wait_ge(rope_ready, i * ROPE_ITER + (len(layer.first) - 1 + u))
                elif j > 0:
                    pe.wait_ge(ring_freed, ring_count(layer, i, unit))
                else:
                    pe.wait_ge(ring_freed, i * len(layer.units) + (layer.loop_ring + layer.units.index(unit) + 1 - len(layer.units)))
                if layer is L0:
                    for t in range(4):
                        at = (4 * u + t) * S
                        for k, (a, b) in enumerate(PARTS):
                            mm = pe.matmul(score[u][:, t * S:(t + 1) * S], QT[a][:, at:at + S], KT[b][:, at:at + S],
                                           start=(k == 0), stop=(k == 2))
                    mm.then_inc(s_filled, 1)
                    return
                if u == 1:
                    pe.wait_ge(masked_ready, layer.soft(i, j, 0))
                for t in range(4):
                    at = (4 * u + t) * S
                    pe.matmul(score_both[:, t * 2 * S:(t + 1) * 2 * S].rearrange("p (e k) -> p e k", e=2), QT[0][:, at:at + S],
                              KT_BOTH[:, :, at:at + S], start=True, stop=False)
                    mm = pe.matmul(score_both[:, (2 * t + 1) * S:(2 * t + 2) * S], QT[1][:, at:at + S], KT[0][:, at:at + S],
                                   start=False, stop=True)
                mm.then_inc(s_filled, 1)

            def turn_values(layer, i, n):
                pe.wait_ge(ring_freed, layer.ring(i, ("V", 0, n)))
                pe.wait_ge(pt_ready, layer.soft(i, n, 0))
                for t in range(4):
                    mm = pe.transpose(turned[0][:, t * S:(t + 1) * S], vtmp[:, t * S:(t + 1) * S], ident[:])
                mm.then_inc(v_turned, 1)

            def turn_probs(layer, i, j, u):
                pe.wait_ge(p_ready, layer.soft(i, j, u))
                if layer is L0 and j == 1 and u == 0:
                    pe.wait_ge(v_ready, i * 2 + 1)
                for t in range(4):
                    mm = pe.transpose(turned[u][:, t * S:(t + 1) * S], probs[:, u, t * S:(t + 1) * S], ident[:])
                mm.then_inc(t_filled, 1)

            def attend(layer, i, j, n):
                v = [values(layer, p) for p in range(2)]
                unit = ("PV", j, n)
                ring_wait(ring_count(layer, i, unit))
                if n % 2 == 0:
                    pe.wait_ge(pt_ready, layer.soft(i, j, n // 2))
                    if j == 0:
                        pe.wait_ge(ring_freed, layer.ring(i, ("V", 0, (n // 2 + 1) * layer.v_units // 2 - 1)))
                bank = ring[ring_bank(layer, i, unit)]
                for t in range(2):
                    b = 2 * n + t
                    channels = slice(j * HD, (j + 1) * HD)
                    pe.matmul(bank[:, t * 2 * S:(t + 1) * 2 * S].rearrange("p (e q) -> p e q", e=2), v[0][:, b, channels],
                              PVO_BOTH[:, :, b * S:(b + 1) * S], start=True, stop=False)
                    mm = pe.matmul(bank[:, (t * 2 + 1) * S:(t * 2 + 2) * S], v[1][:, b, channels],
                                   PVO[0][:, b * S:(b + 1) * S], start=False, stop=True)
                mm.then_inc(ring_filled, 1)

            def attend_pair(layer, i, pair, n):
                v = [values(layer, p) for p in range(2)]
                unit = ("PV", pair, n)
                ring_wait(ring_count(layer, i, unit))
                if n % 2 == 0:
                    pe.wait_ge(pt_ready, layer.soft(i, 2 * pair + 1, n // 2))
                if pair == 0 and n == 0:
                    pe.wait_ge(v_ready, i * 2 + 2)
                bank = ring[ring_bank(layer, i, unit)]
                for t in range(2):
                    b = 2 * n + t
                    for k, (a, e) in enumerate(PARTS):
                        mm = pe.matmul(bank[:, t * 2 * S:(t + 1) * 2 * S].rearrange("p (h q) -> p h q", h=2), v[a][:, b, :],
                                       PT_PAIR[e][:, :, b * S:(b + 1) * S], start=(k == 0), stop=(k == 2))
                mm.then_inc(ring_filled, 1)

            def outputs(layer, i, pair, b):
                if b == 0:
                    pe.wait_ge(w_ready, layer.item(i, f"O{pair}"))
                if layer.shared_kv and b % 2 == 0:
                    pe.wait_ge(ring_freed, ring_count(layer, i, ("PV", pair, b // 2)))
                elif not layer.shared_kv and b % 2 == 0:
                    pe.wait_ge(pv_ready, pv_count(i, ("PV", 1, b // 2)))
                output(layer, i, ("O", pair, b))

            def turn_rows(stage, batches):
                for b in batches:
                    pe.wait_ge(y_ready, stage * B + b + 1)
                    if b >= 4:
                        pe.wait_ge(y_lo, stage * B + b - 3)
                    src, bank = row_of(b)
                    for c in range(C):
                        mm = pe.transpose(bank[:, c * 128:(c + 1) * 128], src[:, c * 128:(c + 1) * 128], ident[:])
                    mm.then_inc(y_turned, 1)

            def first_keys(layer):
                pe.wait_ge(w_ready, layer.item_base + layer.early.index(item_of(layer, "K", 0)) + 1)
                for unit in layer.first[:2]:
                    project(layer, None, unit)

            def attention(layer):
                if layer is L0:
                    turn_rows(0, range(4))
                    first_keys(layer)
                else:
                    turn_rows(2, range(4))
                stage = 0 if layer is L0 else 2
                for u in range(2):
                    pe.wait_ge(y_lo, stage * B + 4 * (u + 1))
                    pe.wait_ge(w_ready, layer.item_base + layer.early.index("QA") + 1)
                    project(layer, None, layer.first[2 + u])
                    if u == 0 and layer is L1:
                        pe.wait_ge(tail_in, 16 * 8)
                        pe.wait_ge(ring_freed, Y_RING + B)
                        for c in range(C):
                            mm = pe.matmul(ring[EARLY_BANKS[0]][0:VB, 0:SLOTS], wvd[:, c, :], auxv[:, c, :], start=(c == 0), stop=(c == C - 1))
                        mm.then_inc(tail_pe, 1)
                        pe.matmul(ring[EARLY_BANKS[1]][0:RDIM, 0:SLOTS], wr[:], keys[:], start=True, stop=True).then_inc(tail_pe, 1)
                    if u == 0:
                        turn_rows(stage, range(4, B))
                if layer is L1:
                    pe.wait_ge(tail_dve, TD["rk"])
                pe.wait_ge(w_ready, layer.loop_item)
                if layer is L1:
                    pe.wait_ge(ring_freed, layer.loop_ring)

                def weights_wait(i, unit):
                    kind, j, _ = unit
                    if kind != "V" and j == 0:
                        pe.wait_ge(w_ready, layer.item(i, item_of(layer, kind, 0)))
                    else:
                        name = "KV" if kind == "V" else item_of(layer, kind, j)
                        pe.wait_ge(w_ready, i * len(layer.items) + (layer.loop_item - len(layer.items) + layer.items.index(name) + 1))

                def body(i, last):
                    for j in range(layer.heads):
                        for unit in layer.steps(j, last):
                            if unit in layer.units and unit[0] in "KQV" and unit[2] == 0:
                                weights_wait(i, unit)
                            if unit[0] == "S":
                                scores(layer, i, *unit[1:])
                            elif unit[0] == "T":
                                turn_probs(layer, i, *unit[1:])
                            elif unit[0] == "PV" and layer.shared_kv:
                                attend_pair(layer, i, *unit[1:])
                            elif unit[0] == "PV":
                                attend(layer, i, *unit[1:])
                            elif unit[0] == "O":
                                outputs(layer, i, *unit[1:])
                            elif unit[0] == "W":
                                turn_values(layer, i, unit[2])
                            elif unit[0] == "V" and not layer.shared_kv:
                                project_values(layer, i, unit)
                            elif unit in layer.units:
                                project(layer, i, unit)

                loop(pe, layer, body)

            pe.wait_ge(small_in, 32)
            attention(L0)

            turn_rows(1, range(4))
            for j in range(FFN_J):
                pe.wait_ge(w_ready, FFN_ITEM + FFN_ITEMS.index(f"F{j}") + 1)
                for u in range(2):
                    if j == 0:
                        if u == 1:
                            turn_rows(1, range(4, B))
                        pe.wait_ge(y_lo, B + 4 * (u + 1))
                    for half in range(2):
                        k = 4 * j + 2 * u + half
                        if k < 4:
                            ring_wait(FFN_RING + k + 1)
                        elif k >= 8:
                            pe.wait_ge(ring_freed, FFN_RING + 2 * ((k - 8) // 2) + 2)
                        w = both(W[("QA", "QB")[j % 2]], lambda t: t[:, half * HALF:(half + 1) * HALF].rearrange("p (c d) -> p c d", c=C))
                        for c in range(C):
                            for p, (a, b) in enumerate(PARTS):
                                mm = pe.matmul(x_bank(k)[:], w[a][:, c, :], xT[b][:, c, u * HALF:(u + 1) * HALF],
                                               start=(c == 0 and p == 0), stop=(c == C - 1 and p == 2))
                        mm.then_inc(ring_filled, 1)
            first_keys(L1)
            for b in range(B):
                if b < 2:
                    pe.wait_ge(ring_freed, FFN_RING + 12)
                else:
                    ring_wait(Y_RING + b + 1)
                pe.wait_ge(g_lo, 2 * FFN_J - 1 + b // 4)
                for j in range(FFN_J):
                    w = W[("KV", "O")[j // 2]]
                    for p, (a, e) in enumerate(PARTS):
                        mm = pe.matmul(ring[(Y_RING + b) % 4][:], GT[a][:, j, b * S:(b + 1) * S],
                                       w[e][:, (j % 2) * D:(j % 2 + 1) * D], start=(j == 0 and p == 0), stop=(j == FFN_J - 1 and p == 2))
                mm.then_inc(ring_filled, 1)

            attention(L1)

            turn_rows(3, range(4))
            pe.wait_ge(ring_freed, TAIL_RING)
            pe.matmul(ring[3][:], vd, wvu, start=True, stop=True).then_inc(tail_pe, 1)
            pe.wait_ge(w_ready, ITEMS)
            wq = both(W["QA"], lambda t: t[:, 0:C * BOT].rearrange("p (c d) -> p c d", c=C))
            wu = both(W["QA"], lambda t: t[:, C * BOT:C * (BOT + 128)].rearrange("p (c d) -> p c d", c=C))

            def wide(w, m, u, bank):
                pe.wait_ge(y_lo, 3 * B + 4 * (u + 1))
                for c in range(C):
                    for p, (a, b) in enumerate(PARTS):
                        mm = pe.matmul(bank[0:m, :], w[a][:, c, :], xT[b][:, c, u * HALF:(u + 1) * HALF],
                                       start=(c == 0 and p == 0), stop=(c == C - 1 and p == 2))
                mm.then_inc(tail_pe, 1)

            def router_queries(u, bank):
                pe.wait_ge(tail_act, TA[f"query{u}"])
                pe.matmul(bank[0:RDIM, :], wr[:], query[0:BOT, u * HALF:(u + 1) * HALF], start=True, stop=True).then_inc(tail_pe, 1)

            def slot_scores(u, router_bank, attention_bank):
                pe.wait_ge(tail_act, TA[f"rq{u}"])
                for bank, src, rows_of in ((router_bank, rq[0:RDIM], rk[:]), (attention_bank, query[0:BOT], keys[:])):
                    for t in range(4):
                        at = (4 * u + t) * S
                        mm = pe.matmul(bank[:, t * S:(t + 1) * S], src[:, at:at + S], rows_of, start=True, stop=True)
                    mm.then_inc(tail_pe, 1)

            wide(wq, BOT, 0, ring[0])
            turn_rows(3, range(4, B))
            wide(wu, 128, 0, ring[1])
            router_queries(0, ring[2])
            pe.wait_ge(y_lo, 4 * B)
            wide(wu, 128, 1, turned[0])
            slot_scores(0, score[0], ring[3])
            wide(wq, BOT, 1, ring[0])
            router_queries(1, ring[2])
            slot_scores(1, score[1], turned[1])
            pe.wait_ge(tail_dve, TD["logsum"])
            pe.matmul(ring[0][:, 0:1], allones[:], col[:, 2, 0:1], start=True, stop=True).then_inc(tail_pe, 1)

            def turn_exponentials(u):
                pe.wait_ge(tail_act, TA[f"exp{4 * u + 3}"])
                if u == 1:
                    pe.wait_ge(tail_dve, TD["router1"])
                for t in range(4):
                    at = (4 * u + t) * S
                    mm = pe.transpose(score[u][:, t * S:(t + 1) * S], raw[1][:, at:at + S], ident[:])
                mm.then_inc(tail_pe, 1)

            def weighted_sums(u):
                if u == 0:
                    pe.wait_ge(tail_act, TA["wT0"])
                else:
                    pe.wait_ge(tail_dve, TD["wT1"])
                for b in range(4 * u, 4 * u + 4):
                    pe.matmul(OUT_BANKS[b][:], expT[:, b * S:(b + 1) * S], gmat, start=True, stop=True).then_inc(tail_pe, 1)

            turn_exponentials(0)
            weighted_sums(0)
            for u in range(2):
                pe.wait_ge(tail_pool, TO[f"gelu{u}"])
                for t in range(4):
                    mm = pe.matmul(ring[1][:, 4 * u + t:4 * u + t + 1], rot[:, u, t * S:(t + 1) * S], tcols[:, 1:2], start=True, stop=True)
            mm.then_inc(tail_pe, 1)
            turn_exponentials(1)
            weighted_sums(1)

        @block.vector
        def _(dve):
            dve.memset(allones[:], 1.0).then_inc(neg_ready, 1)

            class Steps:
                n = 0

            def step():
                Steps.n += 1
                return Steps.n

            def stats_of(b, added=None):
                if added is not None:
                    dve.wait_ge(ring_freed, added)
                dve.bn_stats(stats[:, b, :], xs[:, b, :]).then_inc(ln_step, 1)
                step()

            def variance(h):
                hs = slice(4 * h, 4 * h + 4)
                dve.wait_ge(ln_step, Steps.n)
                for b in range(4 * h, 4 * h + 4):
                    dve.bn_aggr(mv[:, b, :], stats[:, b, :]).then_inc(ln_step, 1)
                    step()
                dve.wait_ge(ln_step, Steps.n)
                dve.tensor_scalar(ve[:, hs], mv[:, hs, 1], EPS, None, ALU.add).then_inc(ln_var, 1)

            def lower(stage, b):
                dve.wait_ge(y_hi, stage * B + b + 1)
                dst = slice(b * S, (b + 1) * S)
                dve.tensor_tensor(xT[1][:, :, dst], row_of(b)[1][:].rearrange("p (c t) -> p c t", c=C),
                                  xT[0][:, :, dst].bitcast(F32), ALU.subtract).then_inc(y_lo, 1)

            def roots(stage, h):
                hs = slice(4 * h, 4 * h + 4)
                dve.wait_ge(ln_sqrt, 2 * stage + h + 1)
                dve.reciprocal(rstd[:, hs], sd[:, hs]).then_inc(ln_step, 1)
                dve.wait_ge(ln_step, step())
                if stage >= 2:
                    dve.tensor_tensor(msq[:, hs], mv[:, hs, 1], rstd[:, hs], ALU.mult).then_inc(ln_step, 1)
                    dve.wait_ge(ln_step, step())
                    dve.tensor_tensor(msq[:, hs], msq[:, hs], rstd[:, hs], ALU.mult).then_inc(ln_step, 1)
                    dve.wait_ge(ln_step, step())
                if stage == 2:
                    dve.tensor_scalar(msq[:, hs], msq[:, hs], EPS, None, ALU.add).then_inc(ln_ms, 1)
                    dve.wait_ge(ln_rms, h + 1)
                    dve.reciprocal(rrms[:, hs], msq[:, hs]).then_inc(ln_step, 1)
                    dve.wait_ge(ln_step, step())

            def row(stage, b):
                if b >= 4:
                    dve.wait_ge(y_turned, stage * B + b - 3)
                y = row_of(b)[0]
                if stage == 3 and b >= 4:
                    dve.wait_ge(x_plus, 2 * B + b - 3)
                if stage != 2:
                    dve.tensor_scalar(y, xs[:, b, :], mv[:, b, 0:1], rstd[:, b:b + 1], ALU.subtract, ALU.mult).then_inc(y_ready, 1)
                    return
                if b == 0:
                    dve.wait_ge(row_in, 32)
                    dve.wait_ge(g_lo, 2 * FFN_J)
                if b >= 2:
                    dve.wait_ge(x_plus, B + b - 1)
                y2 = prod[:, b % 2, :]
                dve.tensor_scalar(y2, xs[:, b, :], mv[:, b, 0:1], rstd[:, b:b + 1], ALU.subtract, ALU.mult).then_inc(ln_step, 1)
                dve.wait_ge(ln_step, step())
                dve.scalar_tensor_tensor(y, y2, rrms[:, b:b + 1], lnw[:], ALU.mult, ALU.mult).then_inc(y_ready, 1)

            def added_rows(stage, b, count):
                if b >= 1:
                    stats_of(b - 1, count)
                if b == 4:
                    variance(0)

            def first_rows(stage):
                roots(stage, 0)
                row(stage, 0)
                row(stage, 1)

            def rest_of_rows(stage, between=None):
                row(stage, 2)
                row(stage, 3)
                stats_of(B - 1, (None, L0.ring_end, Y_RING + B, TAIL_RING)[stage])
                for b in range(4):
                    lower(stage, b)
                variance(1)
                roots(stage, 1)
                row(stage, 4)
                row(stage, 5)
                if between is not None:
                    between()
                row(stage, 6)
                row(stage, 7)
                for b in range(4, B):
                    lower(stage, b)

            def lows(layer, i, unit):
                hi, lo = destination(layer, unit)
                dve.wait_ge(hi_done, hi_count(layer, i, unit))
                bank = as_destination(layer, unit, ring[ring_bank(layer, i, unit)])
                dve.tensor_tensor(lo, bank, hi.bitcast(F32), ALU.subtract).then_inc(ring_freed, 1)

            def rope_cos(layer, i, unit):
                n = rope_count(layer, i, unit)
                dve.wait_ge(hi_done, hi_count(layer, i, unit))
                if not isinstance(n, int) or n > 2:
                    dve.wait_ge(rope_ready, n - 2)
                dve.tensor_tensor(prod[:, unit[2], :].rearrange("p (b t) -> p b t", b=4),
                                  ring[ring_bank(layer, i, unit)][:].rearrange("p (b t) -> p b t", b=4),
                                  table[:, 0:1, :].to_broadcast([128, 4, HD]), ALU.mult).then_inc(ring_freed, 1)

            def rope_add(layer, i, unit):
                n = rope_count(layer, i, unit)
                dve.wait_ge(rope_sin, n)
                dve.wait_ge(ring_freed, ring_count(layer, i, unit))
                p = prod[:, unit[2], :]
                dve.tensor_tensor(p, p, rot[:, unit[2], :], ALU.add).then_inc(rope_sum, 1)

            def rope_split(layer, i, unit):
                n = rope_count(layer, i, unit)
                p = prod[:, unit[2], :]
                dve.wait_ge(rope_sum, n)
                hi, lo = destination(layer, unit)
                dve.tensor_copy(hi, p).then_inc(rope_hi, 1)
                dve.wait_ge(rope_hi, n)
                dve.tensor_tensor(lo, p, hi.bitcast(F32), ALU.subtract).then_inc(rope_ready, 1)

            def sum_shares(i, unit):
                dve.wait_ge(share_in, pv_count(i, unit))
                total = share_sum(unit)
                dve.tensor_tensor(total, shares(i, unit)[:, :, 1, :], total, ALU.add).then_inc(ring_freed, 1)

            def share_low(i, unit):
                hi, lo = destination(L1, unit)
                dve.wait_ge(hi_done, hi_count(L1, i, unit))
                lo, hi = (t.rearrange("p (b q) -> p b q", b=2) for t in (lo, hi))
                dve.tensor_tensor(lo, share_sum(unit), hi.bitcast(F32), ALU.subtract).then_inc(pv_ready, 1)

            def mask_and_max(layer, i, j, u):
                dve.wait_ge(s_filled, layer.soft(i, j, u))
                if layer is L1:
                    dve.wait_ge(comb_ready, i * 4 + 2 * j + u + 1)
                p4 = probs[:, u, :].rearrange("p (b k) -> p b k", b=4)
                add = neg[:, 4 * u:4 * u + 4, :] if layer is L0 else comb[:, u, :].rearrange("p (b k) -> p b k", b=4)
                if layer is L0:
                    dve.tensor_tensor(p4, score[u].rearrange("p (b k) -> p b k", b=4), add, ALU.add).then_inc(masked_ready, 1)
                else:
                    s4 = score_both[:].rearrange("p (b e k) -> p b e k", b=4, e=2)
                    dve.tensor_tensor(p4, s4[:, :, 0, :], add, ALU.add).then_inc(half_masked, 1)
                    if u == 1:
                        inverse_sum(layer, i, j, 0)
                    dve.wait_ge(half_masked, i * 4 + 2 * j + u + 1)
                    dve.tensor_tensor(p4, s4[:, :, 1, :], p4, ALU.add).then_inc(masked_ready, 1)
                dve.wait_ge(masked_ready, layer.soft(i, j, u))
                dve.tensor_reduce(nmax[:, u, :], p4, AX.X, ALU.max, negate=True).then_inc(max_ready, 1)

            def inverse_sum(layer, i, j, u):
                dve.wait_ge(exp_done, layer.soft(i, j, u))
                if layer is L0:
                    dve.reciprocal(rsum[:, u, :], ssum[:, u, :]).then_inc(rsum_ready, 1)
                else:
                    dve.reciprocal(sinv[:, u, :], ssum[:, u, :]).then_inc(inv_ready, 1)
                    dve.wait_ge(inv_ready, i * 4 + 2 * j + u + 1)
                    dve.scalar_tensor_tensor(rsum[:, u, :], nmax[:, u, :], -0.5 * MASKED, sinv[:, u, :],
                                             ALU.is_lt, ALU.mult).then_inc(rsum_ready, 1)

            def add_output(layer, i, unit):
                b = unit[2]
                dve.wait_ge(ring_filled, ring_count(layer, i, unit))
                dve.tensor_tensor(xs[:, b, :], ring[ring_bank(layer, i, unit)][:], xs[:, b, :], ALU.add).then_inc(ring_freed, 1)

            def values_low(layer, i, n):
                cols = slice(n * HALF, (n + 1) * HALF)
                dve.wait_ge(v_hi, i * 2 + n + 1)
                dve.tensor_tensor(VO[1][:, cols], turned[0][:], VO[0][:, cols].bitcast(F32), ALU.subtract).then_inc(v_ready, 1)

            def turned_low(layer, i, j, u):
                dve.wait_ge(pt_hi, layer.soft(i, j, u))
                hi, lo = turned_to(layer, j)
                dve.tensor_tensor(lo[:, u, :], turned[u][:], hi[:, u, :].bitcast(F32), ALU.subtract).then_inc(pt_ready, 1)

            def attention(layer):
                def body(i, last):
                    for j in range(layer.heads):
                        for unit in layer.steps(j, last):
                            if unit[0] == "M":
                                mask_and_max(layer, i, *unit[1:])
                            elif unit[0] == "N":
                                if layer is L0 or unit[2] == 1:
                                    inverse_sum(layer, i, *unit[1:])
                            elif unit[0] == "L" or unit[0] == "T" and (j == layer.heads - 1 or not layer.shared_kv):
                                turned_low(layer, i, *unit[1:])
                            elif unit[0] == "O":
                                final = last and unit[1] == layer.heads // 2 - 1
                                stage = 1 if layer is L0 else 3
                                if final and unit[2] == B - 1:
                                    first_rows(stage)
                                add_output(layer, i, unit)
                                if final:
                                    added_rows(stage, unit[2], ring_count(layer, i, unit) - 1)
                            elif unit[0] == "W":
                                values_low(layer, i, unit[2])
                            elif unit[0] == "D":
                                rope_cos(layer, i, unit[1])
                            elif unit[0] == "A":
                                rope_add(layer, i, unit[1])
                            elif unit[0] == "H":
                                rope_split(layer, i, unit[1])
                            elif unit not in layer.units:
                                pass
                            elif unit[0] == "V" and layer.shared_kv:
                                dve.wait_ge(ring_filled, ring_count(layer, i, unit))
                                dve.tensor_copy(vtmp, ring[ring_bank(layer, i, unit)][:]).then_inc(ring_freed, 1)
                            elif is_rope(layer, unit):
                                pass
                            elif layer is L1 and unit[0] == "PV":
                                sum_shares(i, unit)
                                if unit[2] % 2 == 1:
                                    share_low(i, ("PV", unit[1], unit[2] - 1))
                                    share_low(i, unit)
                            else:
                                lows(layer, i, unit)

                loop(dve, layer, body)

            def context_low(c):
                dve.wait_ge(ctx_hi, c + 1)
                dve.tensor_tensor(cT[1][:, c, :], ctx_raw[c], cT[0][:, c, :].bitcast(F32), ALU.subtract).then_inc(ctx_ready, 1)

            dve.wait_ge(x_in[0], 16)
            for b in range(4):
                stats_of(b)
            variance(0)
            roots(0, 0)
            for b in range(4):
                row(0, b)
            context_low(0)
            lower(0, 0)
            lower(0, 1)
            context_low(1)
            lower(0, 2)
            lower(0, 3)
            context_low(2)
            context_low(3)
            dve.wait_ge(x_in[1], 16)
            for b in range(4, B):
                stats_of(b)
            variance(1)
            roots(0, 1)
            for b in range(4, B):
                row(0, b)
            dve.wait_ge(small_in, 32)
            for unit in L0.first[:2]:
                rope_cos(L0, None, unit)
            lower(0, 4)
            rope_add(L0, None, L0.first[0])
            rope_split(L0, None, L0.first[0])
            for b in range(5, B):
                lower(0, b)
            rope_add(L0, None, L0.first[1])
            rope_split(L0, None, L0.first[1])
            for unit in L0.first[2:]:
                rope_cos(L0, None, unit)
                rope_add(L0, None, unit)
                rope_split(L0, None, unit)
            dve.wait_ge(mask_in, 16)
            dve.tensor_scalar(neg[:], neg[:], 0.0, MASKED, ALU.is_equal, ALU.mult).then_inc(neg_ready, 1)
            dve.wait_ge(neg_ready, 2)
            attention(L0)

            def bounded(k):
                if k == 2:
                    dve.wait_ge(y_turned, 2 * B)
                if k >= 4:
                    dve.wait_ge(g_prod, k - 3)
                dve.wait_ge(ring_filled, FFN_RING + 2 * k + 1)
                dve.tensor_scalar(gate_of(k), x_bank(2 * k)[:], bcol[:, k // 2:k // 2 + 1], -EXP_MAX,
                                  ALU.add, ALU.max).then_inc(g_pre, 1)

            def first_bounded():
                dve.wait_ge(small_in, 48)
                bounded(0)

            rest_of_rows(1, first_bounded)
            for k in range(2 * FFN_J):
                r = gate_of(k)
                if k + 1 < 2 * FFN_J:
                    bounded(k + 1)
                dve.wait_ge(gate_plus, k + 1)
                dve.reciprocal(r, r).then_inc(gate_inv, 1)
                dve.wait_ge(gate_inv, k + 1)
                dve.wait_ge(x2_in, k + 1)
                dve.scalar_tensor_tensor(r, x_bank(2 * k)[:], bcol[:, k // 2:k // 2 + 1], r, ALU.add, ALU.mult).then_inc(ring_freed, 2)
            dve.wait_ge(mask_in, 32)
            dve.tensor_scalar(neg[:], raw[2][:, 0:B * S // 4].bitcast(mybir.dt.uint8).rearrange("p (b k) -> p b k", b=B),
                              0.0, MASKED, ALU.is_equal, ALU.mult).then_inc(neg_ready, 1)
            for unit in L1.first[:2]:
                lows(L1, None, unit)
            for b in range(B):
                if b == B - 1:
                    first_rows(2)
                dve.wait_ge(x_plus, b + 1)
                dve.wait_ge(ring_filled, Y_RING + b + 1)
                dve.tensor_tensor(xs[:, b, :], ring[(Y_RING + b) % 4][:], xs[:, b, :], ALU.add).then_inc(ring_freed, 1)
                added_rows(2, b, Y_RING + b)
            def keys_and_values():
                lows(L1, None, L1.first[2])
                dve.wait_ge(tail_pe, TP["vd"])
                dve.tensor_copy(vd, ring[EARLY_BANKS[0]][0:VB, 0:SLOTS]).then_inc(tail_dve, 1)
                dve.wait_ge(tail_pe, TP["rk"])
                dve.tensor_copy(rk[:], ring[EARLY_BANKS[1]][0:RDIM, 0:SLOTS]).then_inc(tail_dve, 1)

            rest_of_rows(2, keys_and_values)
            lows(L1, None, L1.first[3])
            dve.wait_ge(x_plus, 2 * B)
            attention(L1)

            names = []

            def mark(name):
                names.append(name)
                assert name not in TD or TD[name] == len(names), (name, len(names))
                return len(names)

            names.extend(["vd", "rk"])
            lr = logrel[:, :].rearrange("p (a n) -> p a n", a=1).to_broadcast([128, 4, SLOTS])
            R3 = raw[0][:].rearrange("p (b n) -> p b n", b=B)
            A3 = raw[1][:].rearrange("p (b n) -> p b n", b=B)
            X3 = raw[2][:].rearrange("p (b n) -> p b n", b=B)

            def done(name):
                dve.wait_ge(tail_dve, mark(name))

            def poly(u):
                dve.wait_ge(tail_pool, TO[f"sq{u}"])
                w = rot[:, u, :]
                dve.tensor_scalar(w, w, 0.044715, 1.0, ALU.mult, ALU.add).then_inc(tail_dve, 1)
                mark(f"poly{u}")

            def bounded_inner(u):
                dve.wait_ge(tail_pool, TO[f"cubic{u}"])
                w = rot[:, u, :]
                dve.tensor_scalar(w, w, -0.5 * EXP_MAX, None, ALU.max).then_inc(tail_dve, 1)
                mark(f"inner{u}")

            def sigmoid(u):
                dve.wait_ge(tail_pool, TO[f"plus{u}"])
                dve.reciprocal(rot[:, u, :], rot[:, u, :]).then_inc(tail_dve, 1)
                mark(f"sig{u}")

            def router(u):
                dve.wait_ge(tail_pe, TP[f"router{u}"])
                dve.scalar_tensor_tensor(R3[:, 4 * u:4 * u + 4, :], score[u][:].rearrange("p (b n) -> p b n", b=4),
                                         float(RDIM) ** -0.5, lr, ALU.mult, ALU.add).then_inc(tail_dve, 1)
                done(f"router{u}")

            def largest(u):
                for b in range(4 * u, 4 * u + 4):
                    dve.max(top[:, b, :], R3[:, b, :]).then_inc(tail_dve, 1)
                    mark(f"max{b}")

            def selected(u):
                dve.wait_ge(tail_dve, TD[f"max{4 * u + 3}"])
                for b in range(4 * u, 4 * u + 4):
                    dve.match_replace(X3[:, b, :], top[:, b, :], R3[:, b, :], -3e38).then_inc(tail_dve, 1)
                    mark(f"replace{b}")
                half = slice(4 * u, 4 * u + 4)
                dve.wait_ge(tail_dve, len(names))
                dve.tensor_tensor(R3[:, half, :], X3[:, half, :], R3[:, half, :], ALU.is_equal).then_inc(tail_dve, 1)
                mark(f"unselected{u}")
                dve.wait_ge(tail_pe, TP[f"attn{u}"])
                bank = (ring[3], turned[1])[u]
                dve.scalar_tensor_tensor(A3[:, half, :], bank[:].rearrange("p (b n) -> p b n", b=4),
                                         float(BOT) ** -0.5, lr, ALU.mult, ALU.add).then_inc(tail_dve, 1)
                done(f"attn{u}")
                dve.scalar_tensor_tensor(A3[:, half, :], R3[:, half, :], MASKED, A3[:, half, :], ALU.mult, ALU.add).then_inc(tail_dve, 1)
                done(f"selected{u}")
                dve.tensor_reduce(col[:, 10, half], A3[:, half, :], AX.X, ALU.max, negate=True).then_inc(tail_dve, 1)
                mark(f"amax{u}")

            rest_of_rows(3)
            dve.tensor_scalar(col[:, 0, :], msq[:], 1.0, None, ALU.add).then_inc(tail_dve, 1)
            mark("var1")
            poly(0)
            bounded_inner(0)
            router(0)
            largest(0)
            selected(0)
            poly(1)
            sigmoid(0)
            dve.wait_ge(tail_act, TA["log"])
            dve.tensor_reduce(col[:, 2, 0:1], col[:, 1, :], AX.X, ALU.add).then_inc(tail_dve, 1)
            mark("logsum")
            bounded_inner(1)
            router(1)
            largest(1)
            sigmoid(1)
            selected(1)
            dve.wait_ge(tail_pe, TP["logsum"])
            dve.tensor_scalar(col[:, 2, 1:2], ring[0][:, 0:1], 1.0 / T, 1e-6, ALU.mult, ALU.add).then_inc(tail_dve, 1)
            done("mean")
            dve.reciprocal(col[:, 2, 2:3], col[:, 2, 1:2]).then_inc(tail_dve, 1)
            done("imean")
            dve.tensor_scalar(col[:, 5, :], col[:, 1, :], col[:, 2, 2:3], 0.5, ALU.mult, ALU.mult).then_inc(tail_dve, 1)
            mark("half_norm")
            dve.wait_ge(tail_pe, TP["learned"])
            dve.tensor_scalar(col[:, 3, :], ring[1][:, 0:B], tsc[:, 2:3], -EXP_MAX, ALU.add, ALU.max).then_inc(tail_dve, 1)
            mark("learned")
            dve.wait_ge(tail_act, TA["learned"])
            dve.tensor_scalar(col[:, 4, :], col[:, 4, :], 1.0, None, ALU.add).then_inc(tail_dve, 1)
            done("l1")
            dve.reciprocal(col[:, 4, :], col[:, 4, :]).then_inc(tail_dve, 1)
            done("l2")
            dve.scalar_tensor_tensor(col[:, 6, :], col[:, 4, :], 2.5, col[:, 5, :], ALU.mult, ALU.add).then_inc(tail_dve, 1)
            done("l3")
            dve.tensor_scalar(col[:, 6, :], col[:, 6, :], 0.0, 5.0, ALU.max, ALU.min).then_inc(tail_dve, 1)
            done("l4")
            dve.tensor_scalar(col[:, 6, :], col[:, 6, :], 0.5, 1.0 / 1.5, ALU.subtract, ALU.mult).then_inc(tail_dve, 1)
            done("l5")
            dve.tensor_scalar(col[:, 6, :], col[:, 6, :], 0.0, 1.0, ALU.max, ALU.min).then_inc(tail_dve, 1)
            done("l6")
            dve.tensor_scalar(col[:, 7, :], col[:, 6, :], tsc[:, 0:1], tsc[:, 1:2], ALU.mult, ALU.add).then_inc(tail_dve, 1)
            done("l7")
            dve.tensor_scalar(col[:, 7, :], col[:, 7, :], -EXP_MAX, None, ALU.max).then_inc(tail_dve, 1)
            mark("gate_in")
            dve.reciprocal(col[:, 0, :], col[:, 11, :]).then_inc(tail_dve, 1)
            mark("isum")
            dve.wait_ge(tail_pe, TP["turned1"])
            dve.tensor_copy(expT[:, HALF:2 * HALF], score[1][:]).then_inc(tail_dve, 1)
            mark("wT1")
            dve.wait_ge(tail_act, TA["gate"])
            dve.tensor_scalar(col[:, 8, :], col[:, 8, :], 1.0, None, ALU.add).then_inc(tail_dve, 1)
            done("g1")
            dve.reciprocal(col[:, 8, :], col[:, 8, :]).then_inc(tail_dve, 1)
            done("g2")
            dve.scalar_tensor_tensor(col[:, 9, :], col[:, 8, :], 0.05, col[:, 8, :], ALU.is_ge, ALU.mult).then_inc(tail_dve, 1)
            done("gate")
            dve.tensor_tensor(col[:, 0, :], col[:, 0, :], col[:, 9, :], ALU.mult).then_inc(tail_dve, 1)
            done("scale")
            assert len(names) == OUT_READY, len(names)
            for b in range(B):
                dve.wait_ge(tail_pe, TP[f"out{b}"])
                if b == 0:
                    dve.wait_ge(x_plus, 3 * B)
                dve.scalar_tensor_tensor(xs[:, b, :], OUT_BANKS[b][:], col[:, 0, b:b + 1], xs[:, b, :], ALU.mult, ALU.add).then_inc(tail_dve, 1)

        @block.gpsimd
        def _(pool):
            def low(dest_hi, dest_lo, n, slot):
                pool.wait_ge(w_hi, n)
                pool.tensor_tensor(dest_lo, raw[slot][:], dest_hi.bitcast(F32), ALU.subtract).then_inc(w_ready, 1)

            def rope_sin_of(layer, i, unit):
                pool.wait_ge(hi_done, hi_count(layer, i, unit))
                r = rot[:, unit[2], :].rearrange("p (b t) -> p b t", b=4)
                pool.tensor_tensor(r, r, table[:, 1:2, :].to_broadcast([128, 4, HD]), ALU.mult).then_inc(rope_sin, 1)

            def normalise(layer, i, j, u):
                p = probs[:, u, :].rearrange("p (b k) -> p b k", b=4)
                pool.wait_ge(rsum_ready, layer.soft(i, j, u))
                pool.tensor_tensor(p, p, rsum[:, u, :].rearrange("p (b a) -> p b a", a=1).to_broadcast([128, 4, S]),
                                   ALU.mult).then_inc(p_ready, 1)

            def combine(i, j, u, count):
                h = table[:, j:j + 1, :].to_broadcast([128, 4, S])
                if u == 0:
                    pool.wait_ge(bias_in[j], i * 16 + 16)
                if count is not None:
                    pool.wait_ge(masked_ready, count)
                pool.tensor_tensor(comb[:, u, :].rearrange("p (b k) -> p b k", b=4), neg[:, 4 * u:4 * u + 4, :], h,
                                   ALU.add).then_inc(comb_ready, 1)

            def attention(layer):
                def item(i, last, name):
                    n, slot, _ = item_plan(layer, i, last, name)
                    d = W[DEST[name]]
                    low(d[0][:], d[1][:], n, slot)

                def body(i, last):
                    for j in range(layer.heads):
                        for unit in layer.steps(j, last):
                            if unit[0] == "N":
                                normalise(layer, i, *unit[1:])
                            elif is_rope(layer, unit):
                                rope_sin_of(layer, i, unit)
                            elif unit[0] == "C":
                                _, head, u = unit
                                combine(i + j, head, u, layer.soft(i, j, u))
                            elif unit[0] == "I":
                                item(i, last, unit[1])

                loop(pool, layer, body)

            def early(layer, name):
                n = layer.item_base + layer.early.index(name)
                low(W[name][0][:], W[name][1][:], n + 1, SLOT[n])

            early(L0, "KV")
            early(L0, "QA")
            pool.wait_ge(small_in, 32)
            for unit in L0.first[:3]:
                rope_sin_of(L0, None, unit)
            early(L0, "QB")
            rope_sin_of(L0, None, L0.first[3])
            attention(L0)
            dest = {"F0": "QA", "F1": "QB", "W3a": "KV", "W3b": "O", "F2": "QA", "F3": "QB"}

            def ffn_item(name):
                n = FFN_ITEM + FFN_ITEMS.index(name)
                low(W[dest[name]][0][:], W[dest[name]][1][:], n + 1, SLOT[n])

            def add_b3(b):
                pool.wait_ge(y_ready, B + b + 1)
                pool.tensor_tensor(xs[:, b, :], xs[:, b, :], lnw[:], ALU.add).then_inc(x_plus, 1)

            def gate_plus_one(k):
                pool.wait_ge(gate_exp, k + 1)
                r = gate_of(k).rearrange("p (a n) -> p a n", a=4)
                pool.tensor_tensor(r, r, allones[:].rearrange("p (a n) -> p a n", a=1).to_broadcast([128, 4, 128]),
                                   ALU.add).then_inc(gate_plus, 1)

            def add_rows(stage, b, src):
                pool.wait_ge(y_ready, stage * B + b + 1)
                pool.tensor_tensor(xs[:, b, :], xs[:, b, :], src, ALU.add).then_inc(x_plus, 1)

            for name in FFN_ITEMS[:3]:
                ffn_item(name)
            pool.wait_ge(row_in, 16)
            for b in range(4):
                add_b3(b)
            ffn_item("W3b")
            pool.wait_ge(neg_ready, 1)
            gate_plus_one(0)
            for k in range(2 * FFN_J):
                p = prod[:, k % 2, :]
                if k in (1, 3):
                    ffn_item(("F2", "F3")[k // 2])
                if k + 1 < 2 * FFN_J:
                    gate_plus_one(k + 1)
                pool.wait_ge(ring_freed, FFN_RING + 2 * k + 2)
                pool.tensor_tensor(p, p, gate_of(k), ALU.mult).then_inc(g_prod, 1)
                if k == 5:
                    early(L1, "QA")
                pool.wait_ge(g_hi, k + 1)
                cols = slice(k % 2 * HALF, (k % 2 + 1) * HALF)
                pool.tensor_tensor(GT[1][:, k // 2, cols], p, GT[0][:, k // 2, cols].bitcast(F32), ALU.subtract).then_inc(g_lo, 1)
                if k in (0, 2, 4):
                    add_b3(4 + k // 2)
            add_b3(7)
            early(L1, "QB")
            pool.wait_ge(neg_ready, 3)
            combine(0, 0, 0, None)
            combine(0, 0, 1, None)
            for b in range(4):
                add_rows(2, b, prod[:, b % 2, :])
            early(L1, "KV")
            for b in range(4, B):
                add_rows(2, b, prod[:, b % 2, :])
            attention(L1)
            low(W["QA"][0][:], W["QA"][1][:], ITEMS, SLOT[TAIL_ITEM])
            for b in range(4):
                add_rows(3, b, row_of(b)[0])

            def square(u):
                pool.wait_ge(tail_act, TA[f"v{u}"])
                pool.tensor_tensor(rot[:, u, :], hidden[:, u, :], hidden[:, u, :], ALU.mult).then_inc(tail_pool, 1)

            def times_hidden(u, name):
                pool.wait_ge(tail_dve, TD[name])
                pool.tensor_tensor(rot[:, u, :], rot[:, u, :], hidden[:, u, :], ALU.mult).then_inc(tail_pool, 1)

            def exp_plus_one(u):
                pool.wait_ge(tail_act, TA[f"e{u}"])
                r = rot[:, u, :].rearrange("p (a n) -> p a n", a=4)
                pool.tensor_tensor(r, r, allones[:].rearrange("p (a n) -> p a n", a=1).to_broadcast([128, 4, 128]),
                                   ALU.add).then_inc(tail_pool, 1)

            square(0)
            times_hidden(0, "poly0")
            for b in range(4, B):
                add_rows(3, b, row_of(b)[0])
            exp_plus_one(0)
            square(1)
            times_hidden(1, "poly1")
            times_hidden(0, "sig0")
            exp_plus_one(1)
            times_hidden(1, "sig1")


def kernel(**inputs):
    import numpy as np
    import concourse.bacc as bacc
    from concourse.bass_utils import run_bass_kernel_spmd

    a = {k: np.asarray(v) for k, v in inputs.items()}

    def by_head(w):
        n = w.shape[1] // HD
        return w.reshape(C, 128, n, HD).transpose(2, 1, 0, 3).reshape(n, 128, C * HD)

    def pairs(w, v):
        return np.concatenate([w, v], axis=-1)

    def wo_items(w):
        return w.reshape(-1, 2, HD, D).transpose(0, 2, 1, 3).reshape(-1, 128, 2 * D)

    def ordered(layer, tables):
        items = [tables[n][0] for n in layer.early]
        for i in range(layer.iters):
            for n in layer.items:
                if n[0] == "O":
                    items.append(tables[n][i])
                elif i + 1 < layer.iters:
                    items.append(tables[n][i + 1])
        return items

    items = []
    q, o = by_head(a["L0_xattn_wq"]), wo_items(a["L0_xattn_wo"])
    items += ordered(L0, {"KV": pairs(by_head(a["L0_xattn_wk"]), by_head(a["L0_xattn_wv"])), "QA": pairs(q[0::4], q[1::4]),
                          "QB": pairs(q[2::4], q[3::4]), "O0": o[0::2], "O1": o[1::2]})
    w12 = by_head(a["L0_ffn_w12"].T)
    ffn = {f"F{j}": pairs(w12[j], w12[FFN_J + j]) for j in range(FFN_J)}
    ffn["W3a"], ffn["W3b"] = wo_items(a["L0_ffn_w3"].T)
    items += [ffn[n] for n in FFN_ITEMS]
    qk = pairs(by_head(a["L1_xattn_w_q"].T), by_head(a["L1_xattn_w_k"].T))
    v = a["L1_xattn_w_v"].T.reshape(C, 128, L1.iters, L1.v_cols).transpose(2, 1, 0, 3).reshape(L1.iters, 128, C * L1.v_cols)
    items += ordered(L1, {"KV": v, "QA": qk[0::2], "QB": qk[1::2], "O0": wo_items(a["L1_xattn_w_out"].T)})

    def chunked(w):
        return w.reshape(C, 128, -1).transpose(1, 0, 2).reshape(128, -1)

    tail = np.concatenate([chunked(a["L1_ffn_Wq"].T), chunked(a["L1_ffn_Wu1"].T)], axis=1)
    items.append(np.concatenate([tail, np.zeros((128, ITEM - tail.shape[1]), np.float32)], axis=1))
    assert len(items) == ITEMS

    freq = (1.0 / 10000.0 ** (np.arange(0, HD, 2, dtype=np.float32) / HD)).astype(np.float32)
    angle = (np.arange(S, dtype=np.float32)[:, None] * freq[None, :]).T
    root = float(HD) ** -0.25
    cos, sin = np.cos(angle) * root, np.sin(angle) * root
    cos_sin = np.stack([np.concatenate([cos, cos]), np.concatenate([-sin, sin])], axis=1).astype(np.float32)

    arrays = {
        "x": a["x"],
        "ctx_t": a["ctx_4096"].reshape(T, D).T,
        "stream": np.concatenate(items, axis=0),
        "mask0": a["mask_BxSxS2_ff1"],
        "mask1": a["mask_BxSxS2_bk0"],
        "cos_sin": cos_sin,
        "ident_in": np.eye(128, dtype=np.float32),
        "position_bias": a["L1_xattn_position_bias"].reshape(-1, S),
        "ln_weight": a["L1_xattn_ln_weight"],
        "b12": a["L0_ffn_b12"].reshape(2 * FFN_J, 128).T,
        "b3": a["L0_ffn_b3"],
        "tail_wvd": chunked(a["L1_ffn_Wvd"].T).reshape(128, C, VB),
        "tail_auxv": chunked(a["L1_ffn_aux_values"].T).reshape(128, C, SLOTS),
        "tail_wvu": a["L1_ffn_Wvu"].T,
        "tail_keys": a["L1_ffn_aux_keys"].T,
        "tail_wr": a["L1_ffn_Wr"].T,
        "tail_logrel": a["L1_ffn_log_rel"],
        "tail_cols": np.stack([a["L1_ffn_bu1"], a["L1_ffn_Wu2"].reshape(128)], axis=1),
        "tail_scalars": np.concatenate([a[f"L1_ffn_{n}"].reshape(1) for n in ("gate_w1", "gate_bias", "bu2")]),
    }
    arrays = {k: np.ascontiguousarray(v) for k, v in arrays.items()}
    nc = bacc.Bacc("TRN2", target_bir_lowering=False, num_devices=1)
    args = {k: nc.dram_tensor(f"in_{k}", v.shape, mybir.dt.from_np(v.dtype), kind="ExternalInput").ap() for k, v in arrays.items()}
    out = nc.dram_tensor("out_0", (B, S, D), F32, kind="ExternalOutput").ap()
    xattn_ffn_kernel(nc, out=out, **args)
    got = run_bass_kernel_spmd(nc, [{f"in_{k}": v for k, v in arrays.items()}], core_ids=[0])
    return got.results[0]["out_0"]
```
